# Optimizing a Trainium2 kernel written in Bass

```python
import numpy as np
import jax
import jax.numpy as jnp

def _softmax(x, axis=-1):
    return jax.nn.softmax(x, axis=axis)

def _gelu(x):
    return jax.nn.gelu(x, approximate=True)

def _silu(x):
    return jax.nn.silu(x)

def _sigmoid(x):
    return jax.nn.sigmoid(x)

def _layernorm(x, axis=-1, eps=1e-05):
    m = jnp.mean(x, axis=axis, keepdims=True)
    v = jnp.var(x, axis=axis, keepdims=True)
    return (x - m) / jnp.sqrt(v + eps)

def _scatter_add(tgt, idx, src, axis=0):
    return tgt.at[idx].add(src)

def _segment_sum(src, seg, n):
    return jax.ops.segment_sum(src, seg, n)
kernel_name = 'mk_xattn_ffn_d2_seqx_r2_52fbe6'

def setup_inputs(seed: int=0):
    np.random.seed(seed)
    _w = jnp.asarray

    def _rec_inputs():
        import jax
        import jax.numpy as jnp
        _rk = jax.random.key(seed)
        x = -0.0002928 + 1 * jax.random.normal(jax.random.fold_in(_rk, 1), (4, 2048, 512), jnp.float32)
        _lenS = 2048 - jax.random.randint(jax.random.fold_in(_rk, 7), (4,), 0, max(1, 2048 // 4) + 1, jnp.int32)
        _lenS2 = 77 - jax.random.randint(jax.random.fold_in(_rk, 8), (4,), 0, max(1, 77 // 4) + 1, jnp.int32)
        _ctx_1024P = jax.random.normal(jax.random.fold_in(_rk, 11), (4, 16, 512), jnp.float32)
        _ctx_1024c = jax.random.dirichlet(jax.random.fold_in(_rk, 511), 0.3 * jnp.ones((16,), jnp.float32), (4, 77))
        _ctx_1024t = jnp.einsum('bsk,bkd->bsd', _ctx_1024c, _ctx_1024P)
        _ctx_1024t = _ctx_1024t * jax.lax.rsqrt(jnp.mean(jnp.square(_ctx_1024t)) + 1e-12) * 0.953939
        ctx_1024 = -1.39393e-06 + 0.999914 * (_ctx_1024t + 0.3 * jax.random.normal(jax.random.fold_in(_rk, 611), (4, 77, 512), jnp.float32))
        _validS = jnp.arange(2048)[None, :] < _lenS[:, None]
        _validS2 = jnp.arange(77)[None, :] < _lenS2[:, None]
        _causal = jnp.tril(jnp.ones((2048, 2048), dtype=bool))
        mask_Bx1xSxS2_bf1 = jnp.ones((4, 1, 2048, 77), dtype=bool)
        return (x, ctx_1024, mask_Bx1xSxS2_bf1)
    x, ctx_1024, mask_Bx1xSxS2_bf1 = _rec_inputs()

    def _L0_xattn_setup():
        import jax, jax.numpy as jnp
        import numpy as np
        D_MODEL = 512
        N_HEADS = 16
        HEAD_DIM = D_MODEL // N_HEADS
        MAX_LEN = 1024
        MAX_REL = MAX_LEN - 1

        def _relative_bias(rel_emb, tgt_len, src_len):
            rel_pos = jnp.arange(tgt_len)[:, None] - jnp.arange(src_len)[None, :]
            rel_pos = jnp.clip(rel_pos, -MAX_REL, MAX_REL) + MAX_REL
            bias = rel_emb[rel_pos]
            return jnp.transpose(bias, (2, 0, 1))[None]
        key = jax.random.key(seed)
        ks = jax.random.split(key, 12)
        B, T, S = (2, 1024, 1024)
        s = 1.0 / np.sqrt(D_MODEL)
        inp = {'query': jax.random.normal(ks[0], (B, T, D_MODEL), jnp.float32), 'key': jax.random.normal(ks[1], (B, S, D_MODEL), jnp.float32), 'value': jax.random.normal(ks[2], (B, S, D_MODEL), jnp.float32), 'attn_mask': jnp.ones((B, 1, T, S), dtype=bool), 'Wq': jax.random.normal(ks[3], (D_MODEL, D_MODEL), jnp.float32) * s, 'bq': jnp.zeros((D_MODEL,), jnp.float32), 'Wk': jax.random.normal(ks[4], (D_MODEL, D_MODEL), jnp.float32) * s, 'bk': jnp.zeros((D_MODEL,), jnp.float32), 'Wv': jax.random.normal(ks[5], (D_MODEL, D_MODEL), jnp.float32) * s, 'bv': jnp.zeros((D_MODEL,), jnp.float32), 'Wo': jax.random.normal(ks[6], (D_MODEL, D_MODEL), jnp.float32) * s, 'bo': jnp.zeros((D_MODEL,), jnp.float32), 'rel_emb': jax.random.normal(ks[7], (2 * MAX_REL + 1, N_HEADS), jnp.float32) * 0.02}
        return inp
    _L0_xattn_all = _L0_xattn_setup()
    _L0_xattn_in = {k: v for k, v in _L0_xattn_all.items() if k in ('Wq', 'bq', 'Wk', 'bk', 'Wv', 'bv', 'Wo', 'bo', 'rel_emb')}
    del _L0_xattn_all

    def _L0_ffn_setup():
        import jax, jax.numpy as jnp
        import numpy as np
        import math
        BETA = 0.9
        THRESHOLD = 1.0
        NUM_STEPS = 5
        ALPHA = 2.0

        @jax.custom_vjp
        def spike_fn(u):
            return (u > 0).astype(u.dtype)

        def _spike_fwd(u):
            return (spike_fn(u), u)

        def _spike_bwd(u, g):
            s = jnp.pi / 2.0 * ALPHA * u
            return (g * (ALPHA / 2.0) / (1.0 + s * s),)
        spike_fn.defvjp(_spike_fwd, _spike_bwd)
        key = jax.random.key(seed)
        k1, k2, k3 = jax.random.split(key, 3)
        n_embd = 512
        x = jax.random.normal(k1, (4, 1024, n_embd), dtype=jnp.float32)
        W_fc = jax.random.normal(k2, (4 * n_embd, n_embd), dtype=jnp.float32) / math.sqrt(n_embd)
        W_proj = jax.random.normal(k3, (n_embd, 4 * n_embd), dtype=jnp.float32) / math.sqrt(4 * n_embd)
        return {'x': x, 'W_fc': W_fc, 'W_proj': W_proj}
    _L0_ffn_all = _L0_ffn_setup()
    _L0_ffn_in = {k: v for k, v in _L0_ffn_all.items() if k in ('W_fc', 'W_proj')}
    del _L0_ffn_all

    def _L1_xattn_setup():
        import jax, jax.numpy as jnp
        import numpy as np
        from jax import lax
        BIG = jnp.float32(1e+30)

        def _pairwise_euclidean(a, b):
            aa = jnp.sum(a * a, axis=-1)[:, None]
            bb = jnp.sum(b * b, axis=-1)[None, :]
            ab = a @ b.T
            return jnp.sqrt(jnp.maximum(aa + bb - 2.0 * ab, 0.0))

        def _dtw_cost(D):
            row0 = jnp.cumsum(D[0])

            def row_step(prev_row, d_row):
                first = d_row[0] + prev_row[0]

                def col_step(left, inp):
                    d_ij, up, diag = inp
                    r = d_ij + jnp.minimum(jnp.minimum(up, left), diag)
                    return (r, r)
                _, rest = lax.scan(col_step, first, (d_row[1:], prev_row[1:], prev_row[:-1]))
                row = jnp.concatenate([first[None], rest])
                return (row, row)
            _, rows = lax.scan(row_step, row0, D[1:])
            return jnp.concatenate([row0[None], rows], axis=0)

        def _backtrack(R, T1, T2):
            L = T1 + T2 - 1

            def step(carry, _):
                i, j, done = carry
                valid = jnp.logical_not(done)
                cd = jnp.where((i > 0) & (j > 0), R[jnp.maximum(i - 1, 0), jnp.maximum(j - 1, 0)], BIG)
                cu = jnp.where(i > 0, R[jnp.maximum(i - 1, 0), j], BIG)
                cl = jnp.where(j > 0, R[i, jnp.maximum(j - 1, 0)], BIG)
                choice = jnp.argmin(jnp.stack([cd, cu, cl]))
                ni = jnp.where(choice <= 1, i - 1, i)
                nj = jnp.where((choice == 0) | (choice == 2), j - 1, j)
                at_origin = (i == 0) & (j == 0)
                ni = jnp.where(at_origin, 0, ni)
                nj = jnp.where(at_origin, 0, nj)
                return ((ni, nj, done | at_origin), (i, j, valid))
            init = (jnp.int32(T1 - 1), jnp.int32(T2 - 1), jnp.bool_(False))
            _, (i_idx, j_idx, valid) = lax.scan(step, init, None, length=L)
            return (i_idx, j_idx, valid)

        def _align_one(small, large):
            T_small, d = small.shape
            T_large = large.shape[0]
            D = _pairwise_euclidean(small, large)
            R = _dtw_cost(D)
            i_idx, j_idx, valid = _backtrack(R, T_small, T_large)
            contrib = small[i_idx] * valid[:, None].astype(small.dtype)
            expanded = jnp.zeros((T_large, d), dtype=small.dtype).at[j_idx].add(contrib)
            return expanded
        key = jax.random.key(seed)
        k1, k2 = jax.random.split(key)
        teacher = jax.random.normal(k1, (16, 200, 512), dtype=jnp.float32)
        student = jax.random.normal(k2, (16, 300, 512), dtype=jnp.float32)
        return {'teacher_features': teacher, 'student_features': student}
    _L1_xattn_all = _L1_xattn_setup()
    _L1_xattn_in = {k: v for k, v in _L1_xattn_all.items() if k in ()}
    del _L1_xattn_all

    def _L1_ffn_setup():
        import jax, jax.numpy as jnp
        import numpy as np
        DIM = 512

        def _reference_tuple_inner(x, W_r, W_k, W_v, mu_r, mu_k):
            B, T, C = x.shape
            x_prev = jnp.concatenate([jnp.zeros((B, 1, C), x.dtype), x[:, :-1, :]], axis=1)
            xr = mu_r * x + (1.0 - mu_r) * x_prev
            xk = mu_k * x + (1.0 - mu_k) * x_prev
            r = jax.nn.sigmoid(jnp.einsum('btc,dc->btd', xr, W_r))
            k = jnp.einsum('btc,dc->btd', xk, W_k)
            k_act = jnp.square(jax.nn.relu(k))
            out = r * jnp.einsum('btc,dc->btd', k_act, W_v)
            new_state = x[:, -1, :]
            return (out, new_state)
        key = jax.random.key(seed)
        ks = jax.random.split(key, 6)
        B, T, C = (8, 1024, DIM)
        x = jax.random.normal(ks[0], (B, T, C), dtype=jnp.float32)
        s = 1.0 / np.sqrt(C)
        W_r = jax.random.uniform(ks[1], (C, C), jnp.float32, -s, s)
        W_k = jax.random.uniform(ks[2], (C, C), jnp.float32, -s, s)
        W_v = jax.random.uniform(ks[3], (C, C), jnp.float32, -s, s)
        mu_r = jax.random.uniform(ks[4], (C,), jnp.float32)
        mu_k = jax.random.uniform(ks[5], (C,), jnp.float32)
        return {'x': x, 'W_r': W_r, 'W_k': W_k, 'W_v': W_v, 'mu_r': mu_r, 'mu_k': mu_k}
    _L1_ffn_all = _L1_ffn_setup()
    _L1_ffn_in = {k: v for k, v in _L1_ffn_all.items() if k in ('W_r', 'W_k', 'W_v', 'mu_r', 'mu_k')}
    del _L1_ffn_all
    return {'x': x, 'ctx_1024': ctx_1024, 'mask_Bx1xSxS2_bf1': mask_Bx1xSxS2_bf1, 'L0_xattn_Wq': _L0_xattn_in['Wq'], 'L0_xattn_bq': _L0_xattn_in['bq'], 'L0_xattn_Wk': _L0_xattn_in['Wk'], 'L0_xattn_bk': _L0_xattn_in['bk'], 'L0_xattn_Wv': _L0_xattn_in['Wv'], 'L0_xattn_bv': _L0_xattn_in['bv'], 'L0_xattn_Wo': _L0_xattn_in['Wo'], 'L0_xattn_bo': _L0_xattn_in['bo'], 'L0_xattn_rel_emb': _L0_xattn_in['rel_emb'], 'L0_ffn_W_fc': _L0_ffn_in['W_fc'], 'L0_ffn_W_proj': _L0_ffn_in['W_proj'], 'L1_ffn_W_r': _L1_ffn_in['W_r'], 'L1_ffn_W_k': _L1_ffn_in['W_k'], 'L1_ffn_W_v': _L1_ffn_in['W_v'], 'L1_ffn_mu_r': _L1_ffn_in['mu_r'], 'L1_ffn_mu_k': _L1_ffn_in['mu_k']}

def reference(x, ctx_1024, mask_Bx1xSxS2_bf1, L0_xattn_Wq, L0_xattn_bq, L0_xattn_Wk, L0_xattn_bk, L0_xattn_Wv, L0_xattn_bv, L0_xattn_Wo, L0_xattn_bo, L0_xattn_rel_emb, L0_ffn_W_fc, L0_ffn_W_proj, L1_ffn_W_r, L1_ffn_W_k, L1_ffn_W_v, L1_ffn_mu_r, L1_ffn_mu_k):
    import jax
    import jax.numpy as jnp

    def _L0_xattn_ref(query, key, value, attn_mask, Wq, bq, Wk, bk, Wv, bv, Wo, bo, rel_emb):
        import jax, jax.numpy as jnp
        import numpy as np
        D_MODEL = 512
        N_HEADS = 16
        HEAD_DIM = D_MODEL // N_HEADS
        MAX_LEN = 1024
        MAX_REL = MAX_LEN - 1

        def _relative_bias(rel_emb, tgt_len, src_len):
            rel_pos = jnp.arange(tgt_len)[:, None] - jnp.arange(src_len)[None, :]
            rel_pos = jnp.clip(rel_pos, -MAX_REL, MAX_REL) + MAX_REL
            bias = rel_emb[rel_pos]
            return jnp.transpose(bias, (2, 0, 1))[None]
        B, T, _ = query.shape
        S = key.shape[1]
        scale = HEAD_DIM ** (-0.5)
        q = (query @ Wq.T + bq).reshape(B, T, N_HEADS, HEAD_DIM).transpose(0, 2, 1, 3)
        k = (key @ Wk.T + bk).reshape(B, S, N_HEADS, HEAD_DIM).transpose(0, 2, 1, 3)
        v = (value @ Wv.T + bv).reshape(B, S, N_HEADS, HEAD_DIM).transpose(0, 2, 1, 3)
        scores = jnp.einsum('bhtd,bhsd->bhts', q, k) * scale
        scores = scores + _relative_bias(rel_emb, T, S)
        scores = jnp.where(attn_mask, scores, -jnp.inf)
        weights = jax.nn.softmax(scores, axis=-1)
        out = jnp.einsum('bhts,bhsd->bhtd', weights, v)
        out = out.transpose(0, 2, 1, 3).reshape(B, T, D_MODEL)
        return out @ Wo.T + bo

    def _L0_ffn_ref(x, W_fc, W_proj):
        import jax, jax.numpy as jnp
        import numpy as np
        import math
        BETA = 0.9
        THRESHOLD = 1.0
        NUM_STEPS = 5
        ALPHA = 2.0

        @jax.custom_vjp
        def spike_fn(u):
            return (u > 0).astype(u.dtype)

        def _spike_fwd(u):
            return (spike_fn(u), u)

        def _spike_bwd(u, g):
            s = jnp.pi / 2.0 * ALPHA * u
            return (g * (ALPHA / 2.0) / (1.0 + s * s),)
        spike_fn.defvjp(_spike_fwd, _spike_bwd)
        h = jnp.square(jax.nn.relu(jnp.einsum('bsd,fd->bsf', x, W_fc)))
        y = jnp.einsum('bsf,df->bsd', h, W_proj)

        def step(mem, _):
            reset = jax.lax.stop_gradient(spike_fn(mem - THRESHOLD))
            mem_new = BETA * mem + y - reset * THRESHOLD
            spk = spike_fn(mem_new - THRESHOLD)
            return (mem_new, spk)
        mem0 = jnp.zeros_like(y)
        _, spks = jax.lax.scan(step, mem0, None, length=NUM_STEPS)
        return jnp.sum(spks, axis=0) / NUM_STEPS

    def _L1_xattn_ref(teacher_features, student_features):
        import jax, jax.numpy as jnp
        import numpy as np
        from jax import lax
        BIG = jnp.float32(1e+30)

        def _pairwise_euclidean(a, b):
            aa = jnp.sum(a * a, axis=-1)[:, None]
            bb = jnp.sum(b * b, axis=-1)[None, :]
            ab = a @ b.T
            return jnp.sqrt(jnp.maximum(aa + bb - 2.0 * ab, 0.0))

        def _dtw_cost(D):
            row0 = jnp.cumsum(D[0])

            def row_step(prev_row, d_row):
                first = d_row[0] + prev_row[0]

                def col_step(left, inp):
                    d_ij, up, diag = inp
                    r = d_ij + jnp.minimum(jnp.minimum(up, left), diag)
                    return (r, r)
                _, rest = lax.scan(col_step, first, (d_row[1:], prev_row[1:], prev_row[:-1]))
                row = jnp.concatenate([first[None], rest])
                return (row, row)
            _, rows = lax.scan(row_step, row0, D[1:])
            return jnp.concatenate([row0[None], rows], axis=0)

        def _backtrack(R, T1, T2):
            L = T1 + T2 - 1

            def step(carry, _):
                i, j, done = carry
                valid = jnp.logical_not(done)
                cd = jnp.where((i > 0) & (j > 0), R[jnp.maximum(i - 1, 0), jnp.maximum(j - 1, 0)], BIG)
                cu = jnp.where(i > 0, R[jnp.maximum(i - 1, 0), j], BIG)
                cl = jnp.where(j > 0, R[i, jnp.maximum(j - 1, 0)], BIG)
                choice = jnp.argmin(jnp.stack([cd, cu, cl]))
                ni = jnp.where(choice <= 1, i - 1, i)
                nj = jnp.where((choice == 0) | (choice == 2), j - 1, j)
                at_origin = (i == 0) & (j == 0)
                ni = jnp.where(at_origin, 0, ni)
                nj = jnp.where(at_origin, 0, nj)
                return ((ni, nj, done | at_origin), (i, j, valid))
            init = (jnp.int32(T1 - 1), jnp.int32(T2 - 1), jnp.bool_(False))
            _, (i_idx, j_idx, valid) = lax.scan(step, init, None, length=L)
            return (i_idx, j_idx, valid)

        def _align_one(small, large):
            T_small, d = small.shape
            T_large = large.shape[0]
            D = _pairwise_euclidean(small, large)
            R = _dtw_cost(D)
            i_idx, j_idx, valid = _backtrack(R, T_small, T_large)
            contrib = small[i_idx] * valid[:, None].astype(small.dtype)
            expanded = jnp.zeros((T_large, d), dtype=small.dtype).at[j_idx].add(contrib)
            return expanded
        return jax.vmap(_align_one)(teacher_features, student_features)

    def _L1_ffn_ref(x, W_r, W_k, W_v, mu_r, mu_k):
        import jax, jax.numpy as jnp
        import numpy as np
        DIM = 512

        def _reference_tuple_inner(x, W_r, W_k, W_v, mu_r, mu_k):
            B, T, C = x.shape
            x_prev = jnp.concatenate([jnp.zeros((B, 1, C), x.dtype), x[:, :-1, :]], axis=1)
            xr = mu_r * x + (1.0 - mu_r) * x_prev
            xk = mu_k * x + (1.0 - mu_k) * x_prev
            r = jax.nn.sigmoid(jnp.einsum('btc,dc->btd', xr, W_r))
            k = jnp.einsum('btc,dc->btd', xk, W_k)
            k_act = jnp.square(jax.nn.relu(k))
            out = r * jnp.einsum('btc,dc->btd', k_act, W_v)
            new_state = x[:, -1, :]
            return (out, new_state)
        return _reference_tuple_inner(x, W_r, W_k, W_v, mu_r, mu_k)[0]
    x = x + _L0_xattn_ref(_layernorm(x, axis=-1), ctx_1024, ctx_1024, mask_Bx1xSxS2_bf1, L0_xattn_Wq, L0_xattn_bq, L0_xattn_Wk, L0_xattn_bk, L0_xattn_Wv, L0_xattn_bv, L0_xattn_Wo, L0_xattn_bo, L0_xattn_rel_emb)
    x = x + _L0_ffn_ref(_layernorm(x, axis=-1), L0_ffn_W_fc, L0_ffn_W_proj)
    x = x + _L1_xattn_ref(ctx_1024, _layernorm(x, axis=-1))
    x = x + _L1_ffn_ref(_layernorm(x, axis=-1), L1_ffn_W_r, L1_ffn_W_k, L1_ffn_W_v, L1_ffn_mu_r, L1_ffn_mu_k)
    return x

_drawn_inputs = setup_inputs


def setup_inputs(seed=0):
    import zlib

    import numpy as np

    out = dict(_drawn_inputs(seed))
    spreads = {'L0_xattn_bq': (0.0, 0.293),
     'L0_xattn_bk': (0.0, 2.0),
     'L0_xattn_bv': (0.0, 0.1),
     'L0_xattn_bo': (0.0, 0.1)}
    factors = {'L0_xattn_rel_emb': 26.21, 'L1_ffn_W_r': 3.685, 'L1_ffn_mu_r': 8.0}
    for name, (base, spread) in spreads.items():
        noise = np.random.default_rng([zlib.crc32(name.encode()), seed]).standard_normal(out[name].shape)
        drawn = base * np.exp(spread * noise) if base else spread * noise
        out[name] = jnp.asarray(drawn.astype(out[name].dtype))
    for name, factor in factors.items():
        out[name] = (out[name] * factor).astype(out[name].dtype)
    return out
```

```python
import concourse.bass as bass
from concourse import mybir
from contextlib import ExitStack

F32 = mybir.dt.float32
F32R = mybir.dt.float32r
BF16 = mybir.dt.bfloat16
U8 = mybir.dt.uint8
ALU = mybir.AluOpType
ACT = mybir.ActivationFunctionType
AX = mybir.AxisListType.X

P = 128
B, T, DM = 4, 2048, 512
S = 77
H, DH = 16, 32
HP = P // DH
C = DM // P
FF = 2048
NF = FF // P
G = 512
NT = G // P
NG = B * T // G
GB = T // G
MAX_REL = 1023
SCALE = DH ** -0.5
LN_EPS = 1e-5
BETA, THRESHOLD, STEPS = 0.9, 1.0, 5
BIG = 1e30
PAD = T - 1 - MAX_REL
RELW = PAD + 2 * MAX_REL + 1

W = 64
NB = T // W
SLOTS = S + NB - 1
SKEW_ROW, SKEW_BLOCK, SKEW_BATCH = W, (SLOTS + 1) * W, NB * SLOTS * W
GBLK = G // W


def wait(eng, sem, value):
    if not isinstance(value, int) or value > 0:
        eng.wait_ge(sem, value)


def start(eng, offset):
    return offset if isinstance(offset, int) else eng.snap(offset)


def rows(dram, first, tiles=NT, width=DM):
    tile = [[P * width, tiles]] if tiles > 1 else []
    return bass.AP(tensor=dram.tensor, offset=first, ap=[[width, P]] + tile + [[1, width]])


def skew_start(eng, group):
    return start(eng, (group // GB) * SKEW_BATCH + (group % GB) * (GBLK * SKEW_BLOCK))


def skewed(scratch, first):
    return bass.AP(tensor=scratch.tensor, offset=first,
                   ap=[[SKEW_ROW, S], [SKEW_BLOCK, GBLK], [1, W]])


def place(nc, ctx):
    def sb(name, shape, dt=F32):
        return ctx.enter_context(nc.sbuf_tensor(name, shape, dt))

    def ps(name, shape=(P, 512)):
        return ctx.enter_context(nc.psum_tensor(name, list(shape), F32))

    def sem(name):
        return ctx.enter_context(nc.semaphore(name))

    return sb, ps, sem


def identity(nc, eng, ident, s_ident):
    nc.gpsimd.memset(ident[:, :], 0.0).then_inc(s_ident, 1)
    eng.wait_ge(s_ident, 1)
    nc.gpsimd.affine_select(out=ident[:, :], in_=ident[:, :], compare_op=ALU.not_equal, fill=1.0,
                            base=0, pattern=[[-1, P]], channel_multiplier=1).then_inc(s_ident, 1)


def prepare(nc, a, d):
    with ExitStack() as ctx:
        sb, ps, sem = place(nc, ctx)
        ident = sb("p_ident", [P, P])
        wk = sb("p_wk", [P, C, DM])
        wv = sb("p_wv", [P, C, DM])
        bk = sb("p_bk", [P, C])
        bv = sb("p_bv", [S, DM])
        cx = sb("p_cx", [S, B, DM])
        cxT = sb("p_cxT", [P, B, C, S])
        cxR = sb("p_cxR", [P, B, C, S])
        kf = sb("p_kf", [P, B, C, S])
        kh = sb("p_kh", [P, B, C, S], F32R)
        kl = sb("p_kl", [P, B, C, S], F32R)
        vf = sb("p_vf", [S, B, DM])
        vh = sb("p_vh", [S, B, DM], F32R)
        vl = sb("p_vl", [S, B, DM], F32R)
        c2f = sb("p_c2f", [P, B, C, S])
        c2h = sb("p_c2h", [P, B, C, S], F32R)
        c2l = sb("p_c2l", [P, B, C, S], F32R)
        ch = sb("p_ch", [S, B, DM], F32R)
        cl = sb("p_cl", [S, B, DM], F32R)
        sq = sb("p_sq", [S, DM])
        aa = sb("p_aa", [S, B])
        rel = sb("p_rel", [H, 2 * MAX_REL + 1])
        relp = sb("p_relp", [H, PAD])
        zero = sb("p_zero", [P, SLOTS * W])
        pT = [ps(f"p_pT{b}") for b in range(B)]
        pK = [ps(f"p_pK{b}") for b in range(B)]
        s_ident, s_cx, s_w, s_b, s_rel = sem("p_ident_s"), sem("p_cx_s"), sem("p_w_s"), sem("p_b_s"), sem("p_rel_s")
        s_zero, s_relp, s_T, s_cxT, s_K, s_V = (sem("p_zero_s"), sem("p_relp_s"), sem("p_T_s"),
                                               sem("p_cxT_s"), sem("p_K_s"), sem("p_V_s"))
        s_full, s_hi, s_lo, s_aa, s_out = sem("p_full_s"), sem("p_hi_s"), sem("p_lo_s"), sem("p_aa_s"), sem("p_out_s")
        block = ctx.enter_context(nc.Block())

        @block.sync
        def _(sp):
            sp.dma_start(cx[:, :, :], a["ctx"].rearrange("b s d -> s b d")).then_inc(s_cx, 16)
            sp.dma_start(wk[:, :, :], a["WkT"].rearrange("(c p) d -> p c d", p=P)).then_inc(s_w, 16)
            sp.dma_start(wv[:, :, :], a["WvT"].rearrange("(c p) d -> p c d", p=P)).then_inc(s_w, 16)
            sp.dma_start(bk[:, :], a["bk"]).then_inc(s_b, 16)
            sp.dma_start(bv[:, :], a["bv"].partition_broadcast(S)).then_inc(s_b, 16)
            sp.dma_start(rel[:, :], a["rel"]).then_inc(s_rel, 16)
            n = 0
            sp.wait_ge(s_rel, 16)
            sp.dma_start(d["rel"][:, 0:2 * MAX_REL + 1], rel[:, :]).then_inc(s_out, 16)
            sp.wait_ge(s_relp, 1)
            sp.dma_start(d["rel"][:, 2 * MAX_REL + 1:RELW], relp[:, :]).then_inc(s_out, 16)
            n += 2
            sp.wait_ge(s_zero, 1)
            for b in range(B):
                sp.dma_start(bass.AP(tensor=d["dist"].tensor, offset=b * SKEW_BATCH,
                                     ap=[[SLOTS * W, NB], [1, SLOTS * W]]),
                             zero[b * NB:(b + 1) * NB, :]).then_inc(s_out, 16)
                n += 1
            sp.wait_ge(s_hi, 4)
            sp.wait_ge(s_lo, 4)
            sp.wait_ge(s_aa, B)
            for dst, src in (("kh", kh), ("kl", kl), ("c2h", c2h), ("c2l", c2l)):
                sp.dma_start(d[dst].rearrange("b p c s -> p b c s"), src[:, :, :, :].bitcast(F32)).then_inc(s_out, 16)
                n += 1
            for dst, src in (("vh", vh), ("vl", vl), ("ch", ch), ("cl", cl)):
                sp.dma_start(d[dst].rearrange("b s d -> s b d"), src[:, :, :].bitcast(F32)).then_inc(s_out, 16)
                n += 1
            for b in range(B):
                sp.dma_start(d["aa"][b, :, :], aa[:, b:b + 1]).then_inc(s_out, 16)
                n += 1
            sp.wait_ge(s_out, 16 * n)

        @block.gpsimd
        def _(pool):
            identity(nc, pool, ident, s_ident)
            nc.gpsimd.memset(zero[:, :], 0.0).then_inc(s_zero, 1)
            pool.wait_ge(s_rel, 16)
            nc.gpsimd.tensor_copy(relp[:, :], rel[:, 2 * MAX_REL:2 * MAX_REL + 1].broadcast_to([H, PAD])).then_inc(s_relp, 1)

        @block.tensor
        def _(pe):
            pe.wait_ge(s_ident, 2)
            pe.wait_ge(s_cx, 16)
            for b in range(B):
                for c in range(C):
                    last = nc.tensor.transpose(pT[b][:, c * S:(c + 1) * S], cx[:, b, c * P:(c + 1) * P],
                                               ident[0:S, 0:S])
                last.then_inc(s_T, 1)
            pe.wait_ge(s_w, 32)
            for b in range(B):
                pe.wait_ge(s_cxT, 2 * b + 2)
                for m in range(C):
                    for c in range(C):
                        last = nc.tensor.matmul(pK[b][:, m * S:(m + 1) * S], wk[:, c, m * P:(m + 1) * P],
                                                cxR[:, b, c, :], start=c == 0, stop=c == C - 1)
                last.then_inc(s_K, 1)
            for b in range(B):
                for c in range(C):
                    last = nc.tensor.matmul(pT[b][0:S, :], cxR[:, b, c, :], wv[:, c, :],
                                            start=c == 0, stop=c == C - 1)
                last.then_inc(s_V, 1)

        @block.vector
        def _(dve):
            for b in range(B):
                dve.wait_ge(s_T, b + 1)
                nc.vector.tensor_copy(cxT[:, b, :, :], pT[b][:, 0:C * S].rearrange("p (c s) -> p c s", s=S)).then_inc(s_cxT, 1)
                dve.wait_ge(s_cxT, 2 * b + 1)
                nc.vector.tensor_copy(cxR[:, b, :, :], cxT[:, b, :, ::-1]).then_inc(s_cxT, 1)
            dve.wait_ge(s_b, 32)
            for b in range(B):
                dve.wait_ge(s_K, b + 1)
                for m in range(C):
                    nc.vector.tensor_scalar(kf[:, b, m, :], pK[b][:, m * S:(m + 1) * S], bk[:, m:m + 1], SCALE,
                                            ALU.add, ALU.mult).then_inc(s_full, 1)
            for b in range(B):
                dve.wait_ge(s_V, b + 1)
                nc.vector.tensor_tensor(vf[:, b, :], pT[b][0:S, :], bv[:, :], ALU.add).then_inc(s_full, 1)
            dve.wait_ge(s_cxT, 2 * B)
            nc.vector.tensor_scalar(c2f[:, :, :, :], cxT[:, :, :, :], -2.0, None, ALU.mult).then_inc(s_full, 1)
            for n, (full, hi, lo) in enumerate(((kf, kh, kl), (vf, vh, vl), (c2f, c2h, c2l), (cx, ch, cl))):
                dve.wait_ge(s_hi, n + 1)
                flat = "p b d -> p (b d)" if n % 2 else "p b c s -> p (b c s)"
                full, hi, lo = (r[:].rearrange(flat) for r in (full, hi, lo))
                nc.vector.tensor_tensor(lo, full, hi.bitcast(F32), ALU.subtract).then_inc(s_lo, 1)

        @block.scalar
        def _(act):
            act.wait_ge(s_cx, 16)
            for b in range(B):
                if b:
                    act.wait_ge(s_aa, b)
                nc.scalar.activation(sq[:, :], cx[:, b, :], ACT.Square, accum_out=aa[:, b:b + 1]).then_inc(s_aa, 1)
            act.wait_ge(s_full, B * C)
            nc.scalar.activation(kh[:, :, :, :], kf[:, :, :, :], ACT.Copy).then_inc(s_hi, 1)
            act.wait_ge(s_full, B * C + B)
            nc.scalar.activation(vh[:, :, :], vf[:, :, :], ACT.Copy).then_inc(s_hi, 1)
            act.wait_ge(s_full, B * C + B + 1)
            nc.scalar.activation(c2h[:, :, :, :], c2f[:, :, :, :], ACT.Copy).then_inc(s_hi, 1)
            nc.scalar.activation(ch[:, :, :], cx[:, :, :], ACT.Copy).then_inc(s_hi, 1)


def attention(nc, a, d):
    with ExitStack() as ctx:
        sb, ps, sem = place(nc, ctx)
        SPLITS = 2 * C + NT * (C + 1)
        ident = sb("a_ident", [P, P])
        wqh, wql = (sb(f"a_wq{n}", [P, C, DM], F32R) for n in "hl")
        woh, wol = (sb(f"a_wo{n}", [P, C, DM], F32R) for n in "hl")
        bq = sb("a_bq", [P, C])
        bo = sb("a_bo", [P, DM])
        half = sb("a_half", [P, NT])
        x = sb("a_x", [P, NT, DM])
        xn = sb("a_xn", [P, NT, DM])
        xb = sb("a_xb", [P, NT, DM])
        stats = sb("a_stats", [P, NT, 6])
        pause = sb("a_pause", [P, 1])
        mv = sb("a_mv", [P, NT, 2])
        ve = sb("a_ve", [P, NT])
        rstd = sb("a_rstd", [P, NT])
        xTh, xTl = (sb(f"a_xT{n}", [P, C, G], F32R) for n in "hl")
        qTh, qTl = (sb(f"a_qT{n}", [P, C, G], F32R) for n in "hl")
        kbh, kbl = (sb(f"a_kb{n}", [P, C, HP * S], F32R) for n in "hl")
        vh, vl = (sb(f"a_v{n}", [S, DM], F32R) for n in "hl")
        mask = sb("a_mask", [P, NT, S], U8)
        mneg = sb("a_mneg", [P, NT, S])
        huge = sb("a_huge", [P, 2])
        bias = sb("a_bias", [P, NT, H, S])
        bm = sb("a_bm", [P, 2, H, S])
        sc = sb("a_sc", [P, 2, H, S])
        mx = sb("a_mx", [P, 2, H])
        rs = sb("a_rs", [P, H])
        ri = sb("a_ri", [P, H])
        pTh, pTl = (sb(f"a_pT{n}", [S, H, P], F32R) for n in "hl")
        on = sb("a_on", [P, DM])
        oTh, oTl = (sb(f"a_oT{n}", [P, C, P], F32R) for n in "hl")
        x1 = sb("a_x1", [P, 2, DM])
        pW = [ps(f"a_pW{n}") for n in range(2)]
        pS = ctx.enter_context(nc.psum_tensor("a_pS", [P, C, 512], F32))
        pV = ps("a_pV")
        pO = ps("a_pO")
        names = ("cleared ident w wh wl const x stat aggr var rstd xn xb split hi lo kb v mask mneg bm score added maxed "
                 "shifted exped summed recip pv normed wo x1").split()
        s = {n: sem(f"a_{n}_s") for n in names}
        s_bias = [sem(f"a_bias{t}_s") for t in range(NT)]
        s_store = [sem(f"a_store{n}_s") for n in range(2)]
        block = ctx.enter_context(nc.Block())

        stage = [x, xn]

        def pt(t, j):
            n = 2 * C + (C + 1) * t - (1 if t else 0)
            return n + j + (1 if t and j else 0)

        def ot(t):
            return pt(t + 1, 0) + 1 if t < NT - 1 else SPLITS - 1

        def load_group(sp, i):
            first = start(sp, (i // GB) * (P * C * S))
            at = [start(sp, first + j * DH * C * S) for j in range(HP)]
            for hi_lo, (dst, src) in enumerate(((kbh, d["kh"]), (kbl, d["kl"]))):
                for j in range(HP):
                    r = slice(j * DH, (j + 1) * DH)
                    if j == 0 and hi_lo == 0:
                        wait(sp, s["score"], 2 * NT * i)
                    sp.dma_start(dst[r, :, j * S:(j + 1) * S].bitcast(F32),
                                 bass.AP(tensor=src.tensor, offset=at[j], ap=[[C * S, DH], [S, C], [1, S]])).then_inc(s["kb"], 16)

        def load_v(sp, i):
            first = start(sp, (i // GB) * (S * DM))
            wait(sp, s["pv"], NT * i)
            sp.dma_start(vh[:, :].bitcast(F32), bass.AP(tensor=d["vh"].tensor, offset=first, ap=[[DM, S], [1, DM]])).then_inc(s["v"], 16)
            sp.dma_start(vl[:, :].bitcast(F32), bass.AP(tensor=d["vl"].tensor, offset=first, ap=[[DM, S], [1, DM]])).then_inc(s["v"], 16)

        def load_bias(sp, i, t):
            first = start(sp, (i % GB) * G + (MAX_REL - (S - 1) + t * P))
            wait(sp, s["bm"], NT * (i - 1) + t + 1)
            src = bass.AP(tensor=d["rel"].tensor,
                          offset=first,
                          ap=[[1, P], [RELW, H], [1, S]])
            sp.dma_start(bias[:, t, :, :], src).then_inc(s_bias[t], 16)

        def load_mask(sp, i):
            first = start(sp, i * (G * S))
            sp.dma_start(mask[:, :, :], rows(a["mask"], first, width=S)).then_inc(s["mask"], 16)

        def load_x(sp, i):
            first = start(sp, i * (G * DM))
            if isinstance(i, int) and i == 1:
                sp.wait_ge(s["xn"], NT)
            wait(sp, s["xb"], i)
            sp.dma_start(x[:, :, :], rows(a["x"], first)).then_inc(s["x"], 16)

        @block.sync
        def _(sp):
            sp.dma_start(bq[:, :], a["bq"]).then_inc(s["const"], 16)
            sp.dma_start(bo[:, :], a["bo"].partition_broadcast(P)).then_inc(s["const"], 16)
            for n, w in enumerate(("WqT", "WoT")):
                sp.dma_start(stage[n][:, :, :], a[w].rearrange("(c p) d -> p c d", p=P)).then_inc(s["w"], 16)
                sp.wait_ge(s["w"], 16 * n + 16)
            load_mask(sp, 0)
            for t in range(NT):
                load_bias(sp, 0, t)
            sp.wait_ge(s["cleared"], 2)
            load_group(sp, 0)
            load_v(sp, 0)
            sp.wait_ge(s["wl"], 1)
            load_x(sp, 0)

            def store(i, t):
                first = start(sp, i * (G * DM) + t * P * DM)
                sp.wait_ge(s["x1"], NT * i + t + 1)
                sp.dma_start(rows(d["x1"], first, 1), x1[:, t % 2, :]).then_inc(s_store[t % 2], 16)

            def group(i, more):
                if more:
                    load_x(sp, i + 1)
                    load_bias(sp, i + 1, 0)
                    load_mask(sp, i + 1)
                    load_bias(sp, i + 1, 1)
                store(i, 0)
                if more:
                    load_bias(sp, i + 1, 2)
                    load_bias(sp, i + 1, 3)
                store(i, 1)
                if more:
                    load_group(sp, i + 1)
                store(i, 2)
                if more:
                    load_v(sp, i + 1)
                store(i, 3)

            group(0, True)
            with sp.Fori(1, NG - 1) as i:
                group(i, True)
            group(NG - 1, False)
            for n in range(2):
                sp.wait_ge(s_store[n], 16 * NG * NT // 2)

        @block.gpsimd
        def _(pool):
            identity(nc, pool, ident, s["ident"])
            nc.gpsimd.memset(half[:, :], -0.5).then_inc(s["ident"], 1)
            pool.wait_ge(s["const"], 32)

            nc.gpsimd.memset(huge[:, 0:1], -1.0).then_inc(s["ident"], 1)
            nc.gpsimd.memset(huge[:, 1:2], 3e38).then_inc(s["ident"], 1)
            pool.wait_ge(s["ident"], 5)

            def column(n):
                return huge[:, n:n + 1].unsqueeze(2).broadcast_to([P, NT, S])

            def exponent(i):
                pool.wait_ge(s["var"], i + 1)
                nc.gpsimd.tensor_tensor(rstd[:, :], ve[:, :], half[:, :], ALU.pow).then_inc(s["rstd"], 1)

            def add_bo(i):
                pool.wait_ge(s["x"], 16 * i + 16)
                wait(pool, s["x1"], NT * i)
                nc.gpsimd.tensor_tensor(xb[:, :, :], x[:, :, :],
                                        bo[:, :].unsqueeze(1).broadcast_to([P, NT, DM]), ALU.add).then_inc(s["xb"], 1)

            def add_mask(i, t):
                pool.wait_ge(s_bias[t], 16 * i + 16)
                wait(pool, s["added"], 2 * NT * i + 2 * (t - 2) + 2)
                nc.gpsimd.tensor_tensor(bm[:, t % 2, :, :], bias[:, t, :, :],
                                        mneg[:, t, :].unsqueeze(1).broadcast_to([P, H, S]), ALU.add).then_inc(s["bm"], 1)

            def group(i, more):
                pool.wait_ge(s["mask"], 16 * i + 16)
                wait(pool, s["bm"], NT * i)
                for n, (in0, in1, op) in enumerate(((mask[:, :, :], column(0), ALU.add), (mneg[:, :, :], column(1), ALU.mult),
                                                    (mneg[:, :, :], mneg[:, :, :], ALU.add))):
                    nc.gpsimd.tensor_tensor(mneg[:, :, :], in0, in1, op).then_inc(s["mneg"], 1)
                    pool.wait_ge(s["mneg"], 3 * i + n + 1)
                add_mask(i, 0)
                for t in range(NT):
                    if t + 1 < NT:
                        add_mask(i, t + 1)
                    for h in range(2):
                        r = slice(h * H // 2, (h + 1) * H // 2)
                        pool.wait_ge(s["maxed"], 2 * (NT * i + t) + h + 1)
                        nc.gpsimd.tensor_tensor(sc[:, t % 2, r, :], sc[:, t % 2, r, :],
                                                mx[:, t % 2, r].unsqueeze(2).broadcast_to([P, H // 2, S]),
                                                ALU.subtract).then_inc(s["shifted"], 1)
                    if more and t == 2:
                        exponent(i + 1)
                if more:
                    add_bo(i + 1)

            exponent(0)
            add_bo(0)
            group(0, True)
            with pool.Fori(1, NG - 1) as i:
                group(i, True)
            group(NG - 1, False)

        @block.scalar
        def _(act):
            for n, wh in enumerate((wqh, woh)):
                act.wait_ge(s["w"], 16 * n + 16)
                nc.scalar.activation(wh[:, :, :], stage[n][:, :, :], ACT.Copy).then_inc(s["wh"], 1)
            act.wait_ge(s["const"], 32)

            def hi(i, n, out, in_):
                act.wait_ge(s["split"], SPLITS * i + n + 1)
                nc.scalar.activation(out, in_, ACT.Copy).then_inc(s["hi"], 1)

            def exp(i, t):
                for h in range(2):
                    r = slice(h * H // 2, (h + 1) * H // 2)
                    act.wait_ge(s["shifted"], 2 * (NT * i + t) + h + 1)
                    nc.scalar.activation(sc[:, t % 2, r, :], sc[:, t % 2, r, :], ACT.Exp).then_inc(s["exped"], 1)

            def group(i):
                for c in range(C):
                    hi(i, c, xTh[:, c, :], pW[c % 2][:, :])
                for c in range(C):
                    act.wait_ge(s["split"], SPLITS * i + C + c + 1)
                    nc.scalar.activation(qTh[:, c, :], pW[c % 2][:, :], ACT.Identity, bias=bq[:, c:c + 1]).then_inc(s["hi"], 1)
                exp(i, 0)
                for t in range(NT):
                    for j in range(C):
                        n = pt(t, j)
                        hi(i, n, pTh[:, j * HP:(j + 1) * HP, :], pW[n % 2][0:S, :].rearrange("s (h p) -> s h p", p=P))
                        if j == 0 and t:
                            hi(i, ot(t - 1), oTh[:, :, :], pW[ot(t - 1) % 2][:, :].rearrange("p (c q) -> p c q", q=P))
                    if t + 1 < NT:
                        exp(i, t + 1)
                hi(i, ot(NT - 1), oTh[:, :, :], pW[ot(NT - 1) % 2][:, :].rearrange("p (c q) -> p c q", q=P))

            group(0)
            with act.Fori(1, NG) as i:
                group(i)

        @block.vector
        def _(dve):
            nc.vector.memset(kbh[:, :, :].bitcast(F32), 0.0).then_inc(s["cleared"], 1)
            nc.vector.memset(kbl[:, :, :].bitcast(F32), 0.0).then_inc(s["cleared"], 1)
            for n, (wh, wl) in enumerate(((wqh, wql), (woh, wol))):
                dve.wait_ge(s["wh"], n + 1)
                nc.vector.tensor_tensor(wl[:, :, :], stage[n][:, :, :], wh[:, :, :].bitcast(F32), ALU.subtract).then_inc(s["wl"], 1)

            def norm_stats(i):
                dve.wait_ge(s["x"], 16 * i + 16)
                for t in range(NT):
                    nc.vector.bn_stats(stats[:, t, :], x[:, t, :]).then_inc(s["stat"], 1)
                dve.wait_ge(s["stat"], NT * i + NT)
                nc.vector.memset(pause[:, :], 0.0)
                for t in range(NT):
                    nc.vector.bn_aggr(mv[:, t, :], stats[:, t, :]).then_inc(s["aggr"], 1)
                dve.wait_ge(s["aggr"], NT * i + NT)
                nc.vector.tensor_scalar(ve[:, :], mv[:, :, 1], LN_EPS, None, ALU.add).then_inc(s["var"], 1)

            def normalise(i):
                dve.wait_ge(s["rstd"], i + 1)
                for t in range(NT):
                    nc.vector.tensor_scalar(xn[:, t, :], x[:, t, :], mv[:, t, 0:1], rstd[:, t:t + 1],
                                            ALU.subtract, ALU.mult).then_inc(s["xn"], 1)

            def lo(i, n, out, in_, high):
                dve.wait_ge(s["hi"], SPLITS * i + n + 1)
                nc.vector.tensor_tensor(out, in_, high.bitcast(F32), ALU.subtract).then_inc(s["lo"], 1)

            def lo_o(i, t):
                n = ot(t)
                lo(i, n, oTl[:, :, :], pW[n % 2][:, :].rearrange("p (c q) -> p c q", q=P), oTh[:, :, :])

            def add_max(i, t, h):
                r = slice(h * H // 2, (h + 1) * H // 2)
                n = 2 * (NT * i + t) + h + 1
                dve.wait_ge(s["score"], n)
                dve.wait_ge(s["bm"], NT * i + t + 1)
                nc.vector.tensor_tensor(
                    sc[:, t % 2, r, :].rearrange("p (m j) s -> p m (j s)", j=HP), pS[:, 2 * h:2 * h + 2, 0:HP * S],
                    bm[:, t % 2, r, :].rearrange("p (m j) s -> p m (j s)", j=HP), ALU.add).then_inc(s["added"], 1)
                dve.wait_ge(s["added"], n)
                nc.vector.reduce_max(mx[:, t % 2, r], sc[:, t % 2, r, :], AX).then_inc(s["maxed"], 1)

            def add_x(i, t):
                dve.wait_ge(s["wo"], NT * i + t + 1)
                dve.wait_ge(s["xb"], i + 1)
                wait(dve, s_store[t % 2], 16 * (NT // 2 * i + t // 2))
                nc.vector.tensor_tensor(x1[:, t % 2, :], pO[:, :], xb[:, t, :], ALU.add).then_inc(s["x1"], 1)

            def group(i, more):
                for c in range(C):
                    lo(i, c, xTl[:, c, :], pW[c % 2][:, :], xTh[:, c, :])
                for c in range(C):
                    dve.wait_ge(s["hi"], SPLITS * i + C + c + 1)
                    nc.vector.scalar_tensor_tensor(qTl[:, c, :], pW[c % 2][:, :], bq[:, c:c + 1],
                                                   qTh[:, c, :].bitcast(F32), ALU.add, ALU.subtract).then_inc(s["lo"], 1)
                add_max(i, 0, 0)
                add_max(i, 0, 1)
                for t in range(NT):
                    for j in range(C):
                        n = pt(t, j)
                        if j == C - 1 and t + 1 < NT:
                            add_max(i, t + 1, 0)
                        lo(i, n, pTl[:, j * HP:(j + 1) * HP, :], pW[n % 2][0:S, :].rearrange("s (h p) -> s h p", p=P),
                           pTh[:, j * HP:(j + 1) * HP, :])
                        if j == 0 and t:
                            lo_o(i, t - 1)
                    if t + 1 < NT:
                        add_max(i, t + 1, 1)
                    dve.wait_ge(s["exped"], 2 * (NT * i + t) + 2)
                    nc.vector.reduce_sum(rs[:, :], sc[:, t % 2, :, :], AX).then_inc(s["summed"], 1)
                    if t:
                        add_x(i, t - 1)
                    dve.wait_ge(s["summed"], NT * i + t + 1)
                    nc.vector.reciprocal(ri[:, :], rs[:, :]).then_inc(s["recip"], 1)
                    dve.wait_ge(s["recip"], NT * i + t + 1)
                    dve.wait_ge(s["pv"], NT * i + t + 1)
                    nc.vector.tensor_tensor(on[:, :].rearrange("p (h e) -> p h e", e=DH),
                                            pV[:, :].rearrange("p (h e) -> p h e", e=DH),
                                            ri[:, :].unsqueeze(2).broadcast_to([P, H, DH]), ALU.mult).then_inc(s["normed"], 1)
                    if more and t == 1:
                        norm_stats(i + 1)
                    if more and t == 2:
                        normalise(i + 1)
                lo_o(i, NT - 1)
                add_x(i, NT - 1)

            norm_stats(0)
            dve.wait_ge(s["wl"], 2)
            normalise(0)
            group(0, True)
            with dve.Fori(1, NG - 1) as i:
                group(i, True)
            group(NG - 1, False)

        @block.tensor
        def _(pe):
            pe.wait_ge(s["ident"], 2)
            pe.wait_ge(s["wl"], 2)

            def bank_free(i, n):
                wait(pe, s["lo"], SPLITS * i + n - 1)

            def three(out, xh, xl, yh, yl, first=True, last=True):
                nc.tensor.matmul(out, xh, yh, start=first, stop=False)
                nc.tensor.matmul(out, xh, yl, start=False, stop=False)
                return nc.tensor.matmul(out, xl, yh, start=False, stop=last)

            def scores(i, t, m):
                if m % 2 == 0:
                    wait(pe, s["added"], 2 * (NT * i + t) + m // 2 - 1)
                q = slice(t * P, (t + 1) * P)
                last = three(pS[:, m, 0:HP * S], qTh[:, m, q], qTl[:, m, q], kbh[:, m, :], kbl[:, m, :])
                if m % 2:
                    last.then_inc(s["score"], 1)

            def probs(i, t, j):
                n = pt(t, j)
                bank_free(i, n)
                pe.wait_ge(s["exped"], 2 * (NT * i + t) + j // 2 + 1)
                for h in range(HP):
                    last = nc.tensor.transpose(pW[n % 2][0:S, h * P:(h + 1) * P], sc[:, t % 2, j * HP + h, :], ident[:, :])
                last.then_inc(s["split"], 1)

            def out_turn(i, t):
                n = ot(t)
                bank_free(i, n)
                pe.wait_ge(s["normed"], NT * i + t + 1)
                for c in range(C):
                    last = nc.tensor.transpose(pW[n % 2][:, c * P:(c + 1) * P], on[:, c * P:(c + 1) * P], ident[:, :])
                last.then_inc(s["split"], 1)

            def project(i, t, c):
                if c == 0:
                    pe.wait_ge(s["lo"], SPLITS * i + ot(t) + 1)
                    wait(pe, s["x1"], NT * i + t)
                last = three(pO[:, :], oTh[:, c, :], oTl[:, c, :], woh[:, c, :], wol[:, c, :], c == 0, c == C - 1)
                if c == C - 1:
                    last.then_inc(s["wo"], 1)

            def group(i):
                pe.wait_ge(s["xn"], NT * (i + 1))
                for c in range(C):
                    bank_free(i, c)
                    for t in range(NT):
                        last = nc.tensor.transpose(pW[c % 2][:, t * P:(t + 1) * P], xn[:, t, c * P:(c + 1) * P], ident[:, :])
                    last.then_inc(s["split"], 1)
                pe.wait_ge(s["lo"], SPLITS * i + C)
                for m in range(C):
                    bank_free(i, C + m)
                    w = slice(m * P, (m + 1) * P)
                    for c in range(C):
                        last = three(pW[m % 2][:, :], wqh[:, c, w], wql[:, c, w], xTh[:, c, :], xTl[:, c, :], c == 0, c == C - 1)
                    last.then_inc(s["split"], 1)
                pe.wait_ge(s["lo"], SPLITS * i + 2 * C)
                pe.wait_ge(s["kb"], 16 * 2 * HP * (i + 1))
                for m in range(C):
                    scores(i, 0, m)
                for t in range(NT):
                    probs(i, t, 0)
                    if t:
                        out_turn(i, t - 1)
                    probs(i, t, 1)
                    if t + 1 < NT:
                        scores(i, t + 1, 0)
                        scores(i, t + 1, 1)
                    probs(i, t, 2)
                    if t:
                        project(i, t - 1, 0)
                        project(i, t - 1, 1)
                    probs(i, t, 3)
                    if t + 1 < NT:
                        scores(i, t + 1, 2)
                        scores(i, t + 1, 3)
                    if t:
                        project(i, t - 1, 2)
                        project(i, t - 1, 3)
                    pe.wait_ge(s["v"], 32 * (i + 1))
                    pe.wait_ge(s["lo"], SPLITS * i + pt(t, C - 1) + 1)
                    wait(pe, s["normed"], NT * i + t)
                    for h in range(H):
                        e = slice(h * DH, (h + 1) * DH)
                        last = three(pV[:, e], pTh[:, h, :], pTl[:, h, :], vh[:, e], vl[:, e])
                    last.then_inc(s["pv"], 1)
                out_turn(i, NT - 1)
                for c in range(C):
                    project(i, NT - 1, c)

            group(0)
            with pe.Fori(1, NG) as i:
                group(i)


def spiking(nc, a, d):
    with ExitStack() as ctx:
        sb, ps, sem = place(nc, ctx)
        TURNS = C + NF
        BACKS = C + 1
        ident = sb("f_ident", [P, P])
        ones = sb("f_ones", [1, S])
        half = sb("f_half", [P, NT])
        wfh, wfl = (sb(f"f_wf{n}", [P, C, FF], F32R) for n in "hl")
        wph, wpl = (sb(f"f_wp{n}", [P, NF, DM], F32R) for n in "hl")
        x = sb("f_x", [P, NT, DM])
        y = sb("f_y", [P, NT, DM])
        xp = sb("f_xp", [P, NT, DM])
        xTh, xTl = (sb(f"f_xT{n}", [P, C, G], F32R) for n in "hl")
        r = sb("f_r", [P, 2, G])
        hh, hl = (sb(f"f_h{n}", [P, 2, G], F32R) for n in "hl")
        bTh, bTl = (sb(f"f_bT{n}", [P, 2, G], F32R) for n in "hl")
        mem = sb("f_mem", [P, DM])
        lead = sb("f_lead", [P, DM])
        count = sb("f_count", [P, DM])
        dist = sb("f_dist", [S, G])
        stats = sb("f_stats", [P, NT, 6])
        pause = sb("f_pause", [P, 1])
        mv = sb("f_mv", [P, NT, 2])
        ve = sb("f_ve", [P, NT])
        rstd = sb("f_rstd", [P, NT])
        stats2 = sb("f_stats2", [P, NT, 6])
        mv2 = sb("f_mv2", [P, NT, 2])
        ve2 = sb("f_ve2", [P, NT])
        rstd2 = sb("f_rstd2", [P, NT])
        sq = sb("f_sq", [P, NT])
        bb = sb("f_bb", [1, G])
        ch, cl = (sb(f"f_c{n}", [P, C, S], F32R) for n in "hl")
        aa = sb("f_aa", [S, 1])
        pH = [ps(f"f_pH{n}") for n in range(2)]
        pY = ctx.enter_context(nc.psum_tensor("f_pY", [P, NT, 512], F32))
        pB = ps("f_pB")
        pD = ps("f_pD")
        names = ("ident w wh wl x stat aggr var rstd xn turn hi lo relued squared hhi hlo y ycopied xp lif "
                 "x2 stored2 stat2 aggr2 var2 rstd2 xn2 sq back bhi blo bb ctx dist dclip dsqrt dstore").split()
        s = {n: sem(f"f_{n}_s") for n in names}
        block = ctx.enter_context(nc.Block())
        stage = [x, y]
        WCH = 2 * C
        LIF = 4 + 3 * (STEPS - 2)
        F_STATS, F_NEXT, F_BACK = 8, 10, 10

        @block.sync
        def _(sp):
            for n in range(WCH):
                if n >= 2:
                    sp.wait_ge(s["wl"], n - 1)
                if n < C:
                    src = a["WfcT"][n * P:(n + 1) * P, :].rearrange("p (q d) -> p q d", d=DM)
                else:
                    src = a["WprojT"][(n - C) * 4 * P:(n - C + 1) * 4 * P, :].rearrange("(q p) d -> p q d", p=P)
                if n:
                    sp.wait_ge(s["w"], 16 * n)
                sp.dma_start(stage[n % 2][:, :, :], src).then_inc(s["w"], 16)

            def load_x(i):
                first = start(sp, i * (G * DM))
                wait(sp, s["lo"], C * i)
                sp.dma_start(x[:, :, :], rows(d["x1"], first)).then_inc(s["x"], 16)

            def load_back(k):
                batch, at_aa, first = (start(sp, (k // GB) * (P * C * S)), start(sp, (k // GB) * S), start(sp, k * (G * DM)))
                wait(sp, s["dsqrt"], k)
                sp.dma_start(ch[:, :, :].bitcast(F32), bass.AP(tensor=d["c2h"].tensor, offset=batch, ap=[[C * S, P], [S, C], [1, S]])).then_inc(s["ctx"], 16)
                sp.dma_start(cl[:, :, :].bitcast(F32), bass.AP(tensor=d["c2l"].tensor, offset=batch, ap=[[C * S, P], [S, C], [1, S]])).then_inc(s["ctx"], 16)
                sp.dma_start(aa[:, :], bass.AP(tensor=d["aa"].tensor, offset=at_aa, ap=[[1, S], [1, 1]])).then_inc(s["ctx"], 16)
                wait(sp, s["stored2"], 16 * k)
                sp.dma_start(xp[:, :, :], rows(d["x1"], first)).then_inc(s["xp"], 16)

            def store_back(k):
                first, block_ = start(sp, k * (G * DM)), skew_start(sp, k)
                sp.wait_ge(s["x2"], NT * (k + 1))
                sp.dma_start(rows(d["x2"], first), xp[:, :, :]).then_inc(s["stored2"], 16)
                sp.wait_ge(s["dsqrt"], k + 1)
                sp.dma_start(skewed(d["dist"], block_), dist[:, :].rearrange("s (c w) -> s c w", w=W)).then_inc(s["dstore"], 16)

            def group(i, back, more):
                if back:
                    load_back(i - 1)
                if more:
                    load_x(i + 1)
                if back:
                    store_back(i - 1)

            sp.wait_ge(s["wl"], WCH - 1)
            load_x(0)
            group(0, False, True)
            group(1, True, True)
            with sp.Fori(2, NG - 1) as i:
                group(i, True, True)
            group(NG - 1, True, False)
            load_back(NG - 1)
            store_back(NG - 1)
            sp.wait_ge(s["stored2"], 16 * NG)
            sp.wait_ge(s["dstore"], 16 * NG)

        @block.gpsimd
        def _(pool):
            identity(nc, pool, ident, s["ident"])
            nc.gpsimd.memset(half[:, :], -0.5).then_inc(s["ident"], 1)
            nc.gpsimd.memset(ones[:, :], 1.0).then_inc(s["ident"], 1)
            pool.wait_ge(s["ident"], 4)

            def exponent(i):
                pool.wait_ge(s["var"], i + 1)
                nc.gpsimd.tensor_tensor(rstd[:, :], ve[:, :], half[:, :], ALU.pow).then_inc(s["rstd"], 1)

            def exponent2(k):
                pool.wait_ge(s["var2"], k + 1)
                nc.gpsimd.tensor_tensor(rstd2[:, :], ve2[:, :], half[:, :], ALU.pow).then_inc(s["rstd2"], 1)

            def group(i, back, more):
                for f in range(NF):
                    pool.wait_ge(s["hhi"], NF * i + f + 1)
                    nc.gpsimd.tensor_tensor(hl[:, f % 2, :], r[:, f % 2, :], hh[:, f % 2, :].bitcast(F32), ALU.subtract).then_inc(s["hlo"], 1)
                    if back and f == F_STATS:
                        exponent2(i - 1)
                    if more and f == F_NEXT:
                        exponent(i + 1)

            exponent(0)
            group(0, False, True)
            group(1, True, True)
            with pool.Fori(2, NG - 1) as i:
                group(i, True, True)
            group(NG - 1, True, False)
            exponent2(NG - 1)

        @block.scalar
        def _(act):
            for n in range(WCH):
                act.wait_ge(s["w"], 16 * n + 16)
                out = wfh[:, n, :] if n < C else wph[:, 4 * (n - C):4 * (n - C) + 4, :].rearrange("p q d -> p (q d)")
                nc.scalar.activation(out, stage[n % 2][:, :, :].rearrange("p q d -> p (q d)"), ACT.Copy).then_inc(s["wh"], 1)

            def back_squares(k):
                for t in range(NT):
                    act.wait_ge(s["xn2"], NT * k + t + 1)
                    wait(act, s["sq"], NT * k + t)
                    nc.scalar.activation(lead[:, :], y[:, t, :], ACT.Square, accum_out=sq[:, t:t + 1]).then_inc(s["sq"], 1)

            def back_hi(k, c):
                act.wait_ge(s["back"], BACKS * k + c + 1)
                nc.scalar.activation(bTh[:, c % 2, :], pB[:, :], ACT.Copy).then_inc(s["bhi"], 1)

            def back_root(k):
                act.wait_ge(s["dclip"], k + 1)
                nc.scalar.activation(dist[:, :], dist[:, :], ACT.Sqrt).then_inc(s["dsqrt"], 1)

            def turns(i):
                for c in range(C):
                    act.wait_ge(s["turn"], TURNS * i + c + 1)
                    nc.scalar.activation(xTh[:, c, :], pH[c % 2][:, :], ACT.Copy).then_inc(s["hi"], 1)

            def group(i, back, more):
                for f in range(NF):
                    act.wait_ge(s["turn"], TURNS * i + C + f + 1)
                    wait(act, s["hlo"], NF * i + f - 1)
                    nc.scalar.activation(r[:, f % 2, :], pH[f % 2][:, :], ACT.Relu).then_inc(s["relued"], 1)
                    act.wait_ge(s["squared"], NF * i + f + 1)
                    nc.scalar.activation(hh[:, f % 2, :], r[:, f % 2, :], ACT.Copy).then_inc(s["hhi"], 1)
                    if back and f == F_BACK:
                        back_squares(i - 1)
                    if back and F_BACK < f <= F_BACK + C:
                        back_hi(i - 1, f - F_BACK - 1)
                if more:
                    turns(i + 1)
                act.wait_ge(s["y"], i + 1)
                for t in range(NT):
                    nc.scalar.activation(y[:, t, :], pY[:, t, :], ACT.Copy).then_inc(s["ycopied"], 1)
                if back:
                    back_root(i - 1)

            turns(0)
            group(0, False, True)
            group(1, True, True)
            with act.Fori(2, NG - 1) as i:
                group(i, True, True)
            group(NG - 1, True, False)
            back_squares(NG - 1)
            for c in range(C):
                back_hi(NG - 1, c)
            back_root(NG - 1)

        @block.vector
        def _(dve):
            for n in range(WCH):
                dve.wait_ge(s["wh"], n + 1)
                h, l = ((w[:, n, :] if n < C else w[:, 4 * (n - C):4 * (n - C) + 4, :].rearrange("p q d -> p (q d)"))
                        for w in ((wfh, wfl) if n < C else (wph, wpl)))
                nc.vector.tensor_tensor(l, stage[n % 2][:, :, :].rearrange("p q d -> p (q d)"), h.bitcast(F32), ALU.subtract).then_inc(s["wl"], 1)

            def norm_stats(i):
                dve.wait_ge(s["x"], 16 * i + 16)
                for t in range(NT):
                    nc.vector.bn_stats(stats[:, t, :], x[:, t, :]).then_inc(s["stat"], 1)
                dve.wait_ge(s["stat"], NT * i + NT)
                nc.vector.memset(pause[:, :], 0.0)
                for t in range(NT):
                    nc.vector.bn_aggr(mv[:, t, :], stats[:, t, :]).then_inc(s["aggr"], 1)
                dve.wait_ge(s["aggr"], NT * i + NT)
                nc.vector.tensor_scalar(ve[:, :], mv[:, :, 1], LN_EPS, None, ALU.add).then_inc(s["var"], 1)

            def normalise(i):
                dve.wait_ge(s["rstd"], i + 1)
                for t in range(NT):
                    nc.vector.tensor_scalar(x[:, t, :], x[:, t, :], mv[:, t, 0:1], rstd[:, t:t + 1],
                                            ALU.subtract, ALU.mult).then_inc(s["xn"], 1)

            def spikes(k, t, part):
                n = (NT * k + t) * LIF
                if part == 0:
                    dve.wait_ge(s["ycopied"], NT * (k + 1))
                    wait(dve, s["x2"], NT * k + t)
                    nc.vector.tensor_scalar(count[:, :], y[:, t, :], THRESHOLD, None, ALU.is_gt).then_inc(s["lif"], 1)
                for q in {0: (0,), 1: (1, 2), 2: (3,)}[part]:
                    m = n + 1 + 3 * q
                    old = y[:, t, :] if q == 0 else mem[:, :]
                    if q:
                        dve.wait_ge(s["lif"], m - 1)
                    nc.vector.scalar_tensor_tensor(lead[:, :], old, BETA, y[:, t, :], ALU.mult, ALU.add).then_inc(s["lif"], 1)
                    dve.wait_ge(s["lif"], m + 1)
                    nc.vector.scalar_tensor_tensor(mem[:, :], old, THRESHOLD, lead[:, :], ALU.is_gt, ALU.subtract,
                                                   reverse1=True).then_inc(s["lif"], 1)
                    dve.wait_ge(s["lif"], m + 2)
                    nc.vector.scalar_tensor_tensor(count[:, :], mem[:, :], THRESHOLD, count[:, :], ALU.is_gt, ALU.add).then_inc(s["lif"], 1)
                if part == 2:
                    if t == 0:
                        dve.wait_ge(s["xp"], 16 * (k + 1))
                    dve.wait_ge(s["lif"], n + LIF)
                    nc.vector.scalar_tensor_tensor(xp[:, t, :], count[:, :], 1.0 / STEPS, xp[:, t, :], ALU.mult, ALU.add).then_inc(s["x2"], 1)

            def back_stats(k):
                for t in range(NT):
                    dve.wait_ge(s["x2"], NT * k + t + 1)
                    nc.vector.bn_stats(stats2[:, t, :], xp[:, t, :]).then_inc(s["stat2"], 1)
                dve.wait_ge(s["stat2"], NT * k + NT)
                nc.vector.memset(pause[:, :], 0.0)
                for t in range(NT):
                    nc.vector.bn_aggr(mv2[:, t, :], stats2[:, t, :]).then_inc(s["aggr2"], 1)
                dve.wait_ge(s["aggr2"], NT * k + NT)
                nc.vector.tensor_scalar(ve2[:, :], mv2[:, :, 1], LN_EPS, None, ALU.add).then_inc(s["var2"], 1)

            def back_normalise(k):
                dve.wait_ge(s["rstd2"], k + 1)
                for t in range(NT):
                    nc.vector.tensor_scalar(y[:, t, :], xp[:, t, :], mv2[:, t, 0:1], rstd2[:, t:t + 1],
                                            ALU.subtract, ALU.mult).then_inc(s["xn2"], 1)

            def back_lo(k, c):
                dve.wait_ge(s["bhi"], C * k + c + 1)
                nc.vector.tensor_tensor(bTl[:, c % 2, :], pB[:, :], bTh[:, c % 2, :].bitcast(F32), ALU.subtract).then_inc(s["blo"], 1)

            def back_row(k):
                dve.wait_ge(s["back"], BACKS * k + BACKS)
                nc.vector.tensor_copy(bb[:, :], pB[0:1, :]).then_inc(s["bb"], 1)

            def back_distance(k):
                dve.wait_ge(s["dist"], k + 1)
                wait(dve, s["dstore"], 16 * k)
                nc.vector.tensor_scalar(dist[:, :], pD[0:S, :], aa[:, :], 0.0, ALU.add, ALU.max).then_inc(s["dclip"], 1)

            def turn(i, c):
                dve.wait_ge(s["hi"], C * i + c + 1)
                nc.vector.tensor_tensor(xTl[:, c, :], pH[c % 2][:, :], xTh[:, c, :].bitcast(F32), ALU.subtract).then_inc(s["lo"], 1)

            def group(i, back, more):
                for f in range(NF):
                    dve.wait_ge(s["relued"], NF * i + f + 1)
                    nc.vector.scalar_tensor_tensor(r[:, f % 2, :], pH[f % 2][:, :], 0.0, r[:, f % 2, :], ALU.max, ALU.mult).then_inc(s["squared"], 1)
                    if back and f < F_STATS:
                        for n in range(3 * NT * f // F_STATS, 3 * NT * (f + 1) // F_STATS):
                            spikes(i - 1, n // 3, n % 3)
                    if back and f == F_STATS:
                        back_stats(i - 1)
                    if back and f == F_STATS + 1:
                        back_normalise(i - 1)
                    if more and f == F_NEXT:
                        norm_stats(i + 1)
                    if more and f == F_NEXT + 1:
                        normalise(i + 1)
                    if back and F_BACK < f <= F_BACK + C:
                        back_lo(i - 1, f - F_BACK - 1)
                for c in range(C):
                    if back and c == C - 1:
                        back_row(i - 1)
                    if more:
                        turn(i + 1, c)
                if back:
                    back_distance(i - 1)

            norm_stats(0)
            normalise(0)
            for c in range(C):
                turn(0, c)
            group(0, False, True)
            group(1, True, True)
            with dve.Fori(2, NG - 1) as i:
                group(i, True, True)
            group(NG - 1, True, False)
            for t in range(NT):
                for part in range(3):
                    spikes(NG - 1, t, part)
            back_stats(NG - 1)
            back_normalise(NG - 1)
            for c in range(C):
                back_lo(NG - 1, c)
            back_row(NG - 1)
            back_distance(NG - 1)

        @block.tensor
        def _(pe):
            pe.wait_ge(s["ident"], 4)
            pe.wait_ge(s["wl"], WCH)

            def three(out, xh, xl, yh, yl, first, last):
                nc.tensor.matmul(out, xh, yh, start=first, stop=False)
                nc.tensor.matmul(out, xh, yl, start=False, stop=False)
                return nc.tensor.matmul(out, xl, yh, start=False, stop=last)

            def hidden(i, f):
                if f > 1:
                    pe.wait_ge(s["squared"], NF * i + f - 1)
                w = slice(f * P, (f + 1) * P)
                for c in range(C):
                    last = three(pH[f % 2][:, :], wfh[:, c, w], wfl[:, c, w], xTh[:, c, :], xTl[:, c, :], c == 0, c == C - 1)
                last.then_inc(s["turn"], 1)

            def project(i, f, tiles=range(NT)):
                pe.wait_ge(s["hlo"], NF * i + f + 1)
                if f == 0:
                    wait(pe, s["ycopied"], NT * i)
                for t in tiles:
                    q = slice(t * P, (t + 1) * P)
                    last = three(pY[:, t, :], hh[:, f % 2, q], hl[:, f % 2, q], wph[:, f, :], wpl[:, f, :], f == 0, f == NF - 1)
                if f == NF - 1 and t == NT - 1:
                    last.then_inc(s["y"], 1)

            def back_turn(k, c):
                pe.wait_ge(s["xn2"], NT * (k + 1))
                if c:
                    pe.wait_ge(s["blo"], C * k + c)
                else:
                    wait(pe, s["bb"], k)
                for t in range(NT):
                    last = nc.tensor.transpose(pB[:, t * P:(t + 1) * P], y[:, t, c * P:(c + 1) * P], ident[:, :])
                last.then_inc(s["back"], 1)

            def back_dist(k, c):
                pe.wait_ge(s["blo"], C * k + c + 1)
                if c == 0:
                    pe.wait_ge(s["ctx"], 48 * (k + 1))
                    wait(pe, s["dclip"], k)
                three(pD[0:S, :], ch[:, c, :], cl[:, c, :], bTh[:, c % 2, :], bTl[:, c % 2, :], c == 0, False)

            def back_row(k):
                pe.wait_ge(s["sq"], NT * (k + 1))
                pe.wait_ge(s["blo"], C * (k + 1))
                for t in range(NT):
                    last = nc.tensor.matmul(pB[0:1, t * P:(t + 1) * P], sq[:, t:t + 1], ident[:, :], start=True, stop=True)
                last.then_inc(s["back"], 1)

            def back_finish(k):
                pe.wait_ge(s["bb"], k + 1)
                nc.tensor.matmul(pD[0:S, :], ones[:, :], bb[:, :], start=False, stop=True).then_inc(s["dist"], 1)

            def turn(i, c):
                if c == 0:
                    pe.wait_ge(s["xn"], NT * (i + 1))
                if c < 2:
                    wait(pe, s["squared"], NF * i - 1 + c)
                else:
                    pe.wait_ge(s["lo"], C * i + c - 1)
                for t in range(NT):
                    last = nc.tensor.transpose(pH[c % 2][:, t * P:(t + 1) * P], x[:, t, c * P:(c + 1) * P], ident[:, :])
                last.then_inc(s["turn"], 1)

            def group(i, back, more):
                pe.wait_ge(s["lo"], C * i + C)
                hidden(i, 0)
                hidden(i, 1)
                for f in range(NF):
                    if f < NF - 1:
                        project(i, f)
                    if f + 2 < NF:
                        hidden(i, f + 2)
                    if back and F_BACK < f <= F_BACK + C:
                        back_dist(i - 1, f - F_BACK - 1)
                    if back and F_BACK <= f < F_BACK + C:
                        back_turn(i - 1, f - F_BACK)
                    if more and f == NF - 3:
                        turn(i + 1, 0)
                    if more and f == NF - 2:
                        turn(i + 1, 1)
                        turn(i + 1, 2)
                    if back and f == NF - 2:
                        back_row(i - 1)
                project(i, NF - 1, range(0, NT // 2))
                if more:
                    turn(i + 1, C - 1)
                if back:
                    back_finish(i - 1)
                project(i, NF - 1, range(NT // 2, NT))

            for c in range(C):
                turn(0, c)
            group(0, False, True)
            group(1, True, True)
            with pe.Fori(2, NG - 1) as i:
                group(i, True, True)
            group(NG - 1, True, False)
            for c in range(C):
                back_turn(NG - 1, c)
                back_dist(NG - 1, c)
            back_row(NG - 1)
            back_finish(NG - 1)


def align(nc, a, d):
    with ExitStack() as ctx:
        sb, ps, sem = place(nc, ctx)
        D = sb("d_D", [P, SLOTS, W + 1])
        R = sb("d_R", [P, SLOTS + 1, W + 1])
        M = sb("d_M", [P, SLOTS, W + 1])
        le = sb("d_le", [P, SLOTS, W], BF16)
        left = sb("d_left", [P, SLOTS, W + 1], BF16)
        diag = sb("d_diag", [P, SLOTS, W + 1], BF16)
        up = sb("d_up", [P, SLOTS, W], BF16)
        edge = sb("d_edge", [P, 2, SLOTS], BF16)
        on = sb("d_on", [P, SLOTS + 1, W + 1])
        inner = sb("d_inner", [P, 1])
        viaD = sb("d_viaD", [P, W])
        viaU = sb("d_viaU", [P, W])
        enter = sb("d_enter", [P, W])
        names = "D init R best edge flags inner on0 sh pr en on out".split()
        s = {n: sem(f"d_{n}_s") for n in names}
        block = ctx.enter_context(nc.Block())
        from_left = [(p - 1) % 32 for p in range(32)]
        from_right = [(p + 1) % 32 for p in range(32)]

        @block.sync
        def _(sp):
            for b in range(B):
                sp.dma_start(D[b * NB:(b + 1) * NB, :, 1:W + 1],
                             bass.AP(tensor=d["dist"].tensor, offset=b * SKEW_BATCH,
                                     ap=[[SLOTS * W, NB], [W, SLOTS], [1, W]])).then_inc(s["D"], 16)
            sp.wait_ge(s["on"], SLOTS)
            for b in range(B):
                sp.dma_start(bass.AP(tensor=d["on"].tensor, offset=b * SKEW_BATCH,
                                     ap=[[SLOTS * W, NB], [W, SLOTS], [1, W]]),
                             on[b * NB:(b + 1) * NB, 0:SLOTS, 0:W]).then_inc(s["out"], 16)
            sp.wait_ge(s["out"], 16 * B)

        @block.gpsimd
        def _(pool):
            nc.gpsimd.memset(inner[:, :], 1.0).then_inc(s["inner"], 1)
            nc.gpsimd.memset(enter[:, :], 0.0).then_inc(s["inner"], 1)
            for b in range(B):
                pool.wait_ge(s["inner"], 2 * b + 2)
                last = (b + 1) * NB - 1
                nc.gpsimd.affine_select(out=inner[:, :], in_=inner[:, :], compare_op=ALU.not_equal, fill=0.0,
                                        base=-last, pattern=[[0, 1]], channel_multiplier=1).then_inc(s["inner"], 1)
                nc.gpsimd.affine_select(out=enter[:, :], in_=enter[:, :], compare_op=ALU.not_equal, fill=1.0,
                                        base=-(last * W + W - 1), pattern=[[1, W]], channel_multiplier=W).then_inc(s["inner"], 1)

        @block.vector
        def _(dve):
            nc.vector.memset(R[:, 0, :], BIG).then_inc(s["init"], 1)
            nc.vector.memset(D[:, :, 0:1], 0.0).then_inc(s["init"], 1)
            dve.wait_ge(s["init"], 2)
            for b in range(B):
                nc.vector.memset(R[b * NB:b * NB + 1, 0, 0:1], 0.0).then_inc(s["init"], 1)
                nc.vector.memset(D[b * NB:b * NB + 1, :, 0:1], BIG).then_inc(s["init"], 1)
            dve.wait_ge(s["init"], 2 + 2 * B)
            dve.wait_ge(s["D"], 16 * B)
            for t in range(SLOTS):
                if t:
                    dve.wait_ge(s["R"], t)
                nc.vector.stream_shuffle(M[:, t, 0:1], R[:, t, W:W + 1], from_left).then_inc(s["best"], 1)
                nc.vector.tensor_tensor(M[:, t, 1:W + 1], R[:, t, 1:W + 1], R[:, t, 0:W], ALU.min).then_inc(s["best"], 1)
                dve.wait_ge(s["best"], 2 * t + 2)
                nc.vector.tensor_tensor_scan(R[:, t + 1, :], M[:, t, :], D[:, t, :], BIG, ALU.min, ALU.add).then_inc(s["R"], 1)
            dve.wait_ge(s["R"], SLOTS)

            nc.vector.tensor_tensor(le[:, :, :], R[:, 0:SLOTS, 0:W], R[:, 0:SLOTS, 1:W + 1], ALU.is_le).then_inc(s["flags"], 1)
            nc.vector.tensor_tensor(left[:, :, 0:W], R[:, 1:SLOTS + 1, 0:W], M[:, :, 1:W + 1], ALU.is_lt).then_inc(s["flags"], 1)
            dve.wait_ge(s["flags"], 2)
            nc.vector.scalar_tensor_tensor(diag[:, :, 0:W], left[:, :, 0:W], 0.5, le[:, :, :], ALU.is_lt, ALU.mult).then_inc(s["flags"], 1)
            dve.wait_ge(s["flags"], 3)
            nc.vector.tensor_tensor(up[:, :, :], diag[:, :, 0:W], left[:, :, 0:W], ALU.add).then_inc(s["flags"], 1)
            dve.wait_ge(s["flags"], 4)
            nc.vector.tensor_scalar(up[:, :, :], up[:, :, :], 0.5, None, ALU.is_lt).then_inc(s["flags"], 1)
            for n, flag in enumerate((left, diag)):
                nc.vector.stream_shuffle(edge[:, n, :], flag[:, :, 0], from_right).then_inc(s["edge"], 1)
            dve.wait_ge(s["edge"], 2)
            dve.wait_ge(s["inner"], 2 + 2 * B)
            for n, flag in enumerate((left, diag)):
                nc.vector.memset(flag[:, SLOTS - 1, W:W + 1], 0.0).then_inc(s["flags"], 1)
                nc.vector.tensor_scalar(flag[:, 0:SLOTS - 1, W], edge[:, n, 1:SLOTS], inner[:, 0:1], None, ALU.mult).then_inc(s["flags"], 1)
            nc.vector.memset(on[:, SLOTS, :], 0.0).then_inc(s["on0"], 1)
            dve.wait_ge(s["flags"], 9)
            dve.wait_ge(s["on0"], 1)

            for n in range(SLOTS):
                t = SLOTS - 1 - n
                if n:
                    dve.wait_ge(s["on"], n)
                    nc.vector.stream_shuffle(on[:, t, W:W + 1], on[:, t + 1, 0:1], from_right).then_inc(s["sh"], 1)
                    nc.vector.tensor_tensor(viaD[:, :], on[:, t + 1, 1:W + 1], diag[:, t + 1, 1:W + 1], ALU.mult).then_inc(s["pr"], 1)
                    nc.vector.tensor_tensor(viaU[:, :], on[:, t + 1, 0:W], up[:, t + 1, :], ALU.mult).then_inc(s["pr"], 1)
                    dve.wait_ge(s["pr"], 2 * n)
                    nc.vector.tensor_tensor(enter[:, :], viaD[:, :], viaU[:, :], ALU.add).then_inc(s["en"], 1)
                    dve.wait_ge(s["en"], n)
                else:
                    nc.vector.memset(on[:, t, W:W + 1], 0.0).then_inc(s["sh"], 1)
                dve.wait_ge(s["sh"], n + 1)
                nc.vector.tensor_tensor_scan(on[:, t, W - 1::-1], left[:, t, W:0:-1], enter[:, ::-1], on[:, t, W:W + 1],
                                             ALU.mult, ALU.add).then_inc(s["on"], 1)


def mixing(nc, a, d, out):
    with ExitStack() as ctx:
        sb, ps, sem = place(nc, ctx)
        ident = sb("m_ident", [P, P])
        half = sb("m_half", [P, NT])
        w = {k: [sb(f"m_{k}{n}", [P, C, DM], F32R) for n in "hl"] for k in ("r", "k", "v")}
        mu = sb("m_mu", [P, 2, C])
        nu = sb("m_nu", [P, 2, C])
        inside = sb("m_inside", [P, NG])
        x2 = sb("m_x2", [P, NT, DM])
        path = sb("m_path", [S, G], F32R)
        ch, cl = (sb(f"m_c{n}", [S, DM], F32R) for n in "hl")
        x3 = sb("m_x3", [P, NT, DM])
        xn = sb("m_xn", [P, NT, DM])
        stats = sb("m_stats", [P, NT, 6])
        pause = sb("m_pause", [P, 1])
        mv = sb("m_mv", [P, NT, 2])
        ve = sb("m_ve", [P, NT])
        rstd = sb("m_rstd", [P, NT])
        xT = sb("m_xT", [P, C, G + 1])
        part = sb("m_part", [P, 2, G])
        mix = sb("m_mix", [P, 2, G])
        zh, zl = (sb(f"m_z{n}", [P, 2, C, G], F32R) for n in "hl")
        r = sb("m_relu", [P, 2, G])
        hh, hl = (sb(f"m_h{n}", [P, C, G], F32R) for n in "hl")
        gate = sb("m_gate", [P, NT, DM])
        res = sb("m_res", [P, 2, DM])
        pE = [ps(f"m_pE{n}") for n in range(2)]
        pT = [ps(f"m_pT{n}") for n in range(2)]
        pK = [ps(f"m_pK{n}") for n in range(2)]
        pR = [ps(f"m_pR{n}") for n in range(2)]
        names = ("ident w wh wl mu nu x2 path ctx exp x3 stat aggr var rstd xn turn first xT part mix zhi zlo "
                 "R gate K relued squared hhi hlo V gated res moved").split()
        s = {n: sem(f"m_{n}_s") for n in names}
        s_store = [sem(f"m_store{n}_s") for n in range(2)]
        block = ctx.enter_context(nc.Block())
        stage = [x2, xn, gate]

        @block.sync
        def _(sp):
            sp.dma_start(mu[:, 0, :], a["mu_r"]).then_inc(s["mu"], 16)
            sp.dma_start(mu[:, 1, :], a["mu_k"]).then_inc(s["mu"], 16)
            for n, k in enumerate(("WrT", "WkkT", "WvvT")):
                if n:
                    sp.wait_ge(s["w"], 16 * n)
                sp.dma_start(stage[n][:, :, :], a[k].rearrange("(c p) d -> p c d", p=P)).then_inc(s["w"], 16)

            def load(j):
                first, batch, block_ = start(sp, j * (G * DM)), start(sp, (j // GB) * (S * DM)), skew_start(sp, j)
                wait(sp, s["moved"], j)
                sp.dma_start(x2[:, :, :], rows(d["x2"], first)).then_inc(s["x2"], 16)
                wait(sp, s["exp"], NT * j)
                sp.dma_start(path[:, :].bitcast(F32).rearrange("s (c w) -> s c w", w=W), skewed(d["on"], block_)).then_inc(s["path"], 16)
                sp.dma_start(ch[:, :].bitcast(F32), bass.AP(tensor=d["ch"].tensor, offset=batch, ap=[[DM, S], [1, DM]])).then_inc(s["ctx"], 16)
                sp.dma_start(cl[:, :].bitcast(F32), bass.AP(tensor=d["cl"].tensor, offset=batch, ap=[[DM, S], [1, DM]])).then_inc(s["ctx"], 16)

            def group(i, more):
                if more:
                    load(i + 1)
                for t in range(NT):
                    first = start(sp, i * (G * DM) + t * P * DM)
                    sp.wait_ge(s["res"], NT * i + t + 1)
                    sp.dma_start(rows(out, first, 1), res[:, t % 2, :]).then_inc(s_store[t % 2], 16)

            sp.wait_ge(s["wl"], 1)
            load(0)
            group(0, True)
            with sp.Fori(1, NG - 1) as i:
                group(i, True)
            group(NG - 1, False)
            for n in range(2):
                sp.wait_ge(s_store[n], 16 * NG * NT // 2)

        @block.gpsimd
        def _(pool):
            identity(nc, pool, ident, s["ident"])
            nc.gpsimd.memset(half[:, :], -0.5).then_inc(s["ident"], 1)
            nc.gpsimd.memset(inside[:, :], 1.0).then_inc(s["ident"], 1)
            pool.wait_ge(s["ident"], 4)
            nc.gpsimd.memset(inside[:, ::GB], 0.0).then_inc(s["ident"], 1)

            def front(j):
                pool.wait_ge(s["var"], j + 1)
                nc.gpsimd.tensor_tensor(rstd[:, :], ve[:, :], half[:, :], ALU.pow).then_inc(s["rstd"], 1)

            def front_mix(j, c):
                for z in range(2):
                    n = 2 * (C * j + c) + z + 1
                    pool.wait_ge(s["zhi"], n)
                    nc.gpsimd.tensor_tensor(zl[:, z, c, :], mix[:, z, :], zh[:, z, c, :].bitcast(F32), ALU.subtract).then_inc(s["zlo"], 1)

            def group(i, more):
                if more:
                    front(i + 1)
                for m in range(C):
                    pool.wait_ge(s["hhi"], C * i + m + 1)
                    nc.gpsimd.tensor_tensor(hl[:, m, :], r[:, m % 2, :], hh[:, m, :].bitcast(F32), ALU.subtract).then_inc(s["hlo"], 1)
                if more:
                    for c in range(C):
                        front_mix(i + 1, c)

            front(0)
            for c in range(C):
                front_mix(0, c)
            group(0, True)
            with pool.Fori(1, NG - 1) as i:
                group(i, True)
            group(NG - 1, False)

        @block.scalar
        def _(act):
            for n, k in enumerate("rkv"):
                act.wait_ge(s["w"], 16 * n + 16)
                nc.scalar.activation(w[k][0][:, :, :], stage[n][:, :, :], ACT.Copy).then_inc(s["wh"], 1)
            act.wait_ge(s["mu"], 32)

            def front_turn(j, c):
                act.wait_ge(s["turn"], C * j + c + 1)
                if c == 0:
                    act.wait_ge(s["first"], j + 1)
                nc.scalar.activation(xT[:, c, 1:G + 1], pT[c % 2][:, :], ACT.Copy).then_inc(s["xT"], 1)
                act.wait_ge(s["xT"], C * j + c + 1)
                for z in range(2):
                    wait(act, s["mix"], 2 * (C * j + c) + z - 1)
                    nc.scalar.activation(part[:, z, :], xT[:, c, 1:G + 1], ACT.Copy, scale=mu[:, z, c:c + 1]).then_inc(s["part"], 1)

            def move(j):
                act.wait_ge(s["xn"], NT * (j + 1))
                wait(act, s["res"], NT * j)
                nc.scalar.activation(x3[:, :, :], x2[:, :, :], ACT.Copy).then_inc(s["moved"], 1)

            def front_hi(j, c):
                for z in range(2):
                    act.wait_ge(s["mix"], 2 * (C * j + c) + z + 1)
                    nc.scalar.activation(zh[:, z, c, :], mix[:, z, :], ACT.Copy).then_inc(s["zhi"], 1)

            def group(i, more):
                for t in range(NT):
                    act.wait_ge(s["R"], NT * i + t + 1)
                    nc.scalar.activation(gate[:, t, :], pR[t % 2][:, :], ACT.Sigmoid).then_inc(s["gate"], 1)
                for m in range(C):
                    act.wait_ge(s["K"], C * i + m + 1)
                    wait(act, s["hlo"], C * i + m - 1)
                    nc.scalar.activation(r[:, m % 2, :], pK[m % 2][:, :], ACT.Relu).then_inc(s["relued"], 1)
                    act.wait_ge(s["squared"], C * i + m + 1)
                    nc.scalar.activation(hh[:, m, :], r[:, m % 2, :], ACT.Copy).then_inc(s["hhi"], 1)
                if more:
                    for c in range(C):
                        front_turn(i + 1, c)
                        front_hi(i + 1, c)
                    move(i + 1)

            for c in range(C):
                front_turn(0, c)
                front_hi(0, c)
            move(0)
            group(0, True)
            with act.Fori(1, NG - 1) as i:
                group(i, True)
            group(NG - 1, False)

        @block.vector
        def _(dve):
            for n, k in enumerate("rkv"):
                dve.wait_ge(s["wh"], n + 1)
                nc.vector.tensor_tensor(w[k][1][:, :, :], stage[n][:, :, :], w[k][0][:, :, :].bitcast(F32), ALU.subtract).then_inc(s["wl"], 1)
            dve.wait_ge(s["mu"], 32)
            nc.vector.tensor_scalar(nu[:, :, :], mu[:, :, :], -1.0, 1.0, ALU.mult, ALU.add).then_inc(s["nu"], 1)
            dve.wait_ge(s["nu"], 1)

            def front_x3(j, t):
                dve.wait_ge(s["x2"], 16 * (j + 1))
                dve.wait_ge(s["exp"], NT * j + t + 1)
                nc.vector.tensor_tensor(x2[:, t, :], pE[t % 2][:, :], x2[:, t, :], ALU.add).then_inc(s["x3"], 1)
                dve.wait_ge(s["x3"], NT * j + t + 1)
                nc.vector.bn_stats(stats[:, t, :], x2[:, t, :]).then_inc(s["stat"], 1)

            def front_norm(j):
                dve.wait_ge(s["stat"], NT * j + NT)
                nc.vector.memset(pause[:, :], 0.0)
                for t in range(NT):
                    nc.vector.bn_aggr(mv[:, t, :], stats[:, t, :]).then_inc(s["aggr"], 1)
                dve.wait_ge(s["aggr"], NT * j + NT)
                nc.vector.tensor_scalar(ve[:, :], mv[:, :, 1], LN_EPS, None, ALU.add).then_inc(s["var"], 1)
                dve.wait_ge(s["rstd"], j + 1)
                for t in range(NT):
                    nc.vector.tensor_scalar(xn[:, t, :], x2[:, t, :], mv[:, t, 0:1], rstd[:, t:t + 1],
                                            ALU.subtract, ALU.mult).then_inc(s["xn"], 1)
                if isinstance(j, int) and j == 0:
                    nc.vector.memset(xT[:, :, 0:1], 0.0).then_inc(s["first"], 1)
                else:
                    nc.vector.tensor_scalar(xT[:, :, 0:1], xT[:, :, G:G + 1], inside[:, bass.ds(j, 1)], None, ALU.mult).then_inc(s["first"], 1)

            def front_mix(j, c):
                for z in range(2):
                    n = 2 * (C * j + c) + z
                    dve.wait_ge(s["part"], n + 1)
                    if c == 0:
                        dve.wait_ge(s["first"], j + 1)
                    wait(dve, s["zlo"], n - 1)
                    nc.vector.scalar_tensor_tensor(mix[:, z, :], xT[:, c, 0:G], nu[:, z, c:c + 1], part[:, z, :],
                                                   ALU.mult, ALU.add).then_inc(s["mix"], 1)

            def group(i, more):
                if more:
                    for t in range(NT):
                        front_x3(i + 1, t)
                    front_norm(i + 1)
                for m in range(C):
                    dve.wait_ge(s["relued"], C * i + m + 1)
                    nc.vector.scalar_tensor_tensor(r[:, m % 2, :], pK[m % 2][:, :], 0.0, r[:, m % 2, :], ALU.max, ALU.mult).then_inc(s["squared"], 1)
                for t in range(NT):
                    if more:
                        front_mix(i + 1, t)
                    dve.wait_ge(s["V"], NT * i + t + 1)
                    nc.vector.tensor_tensor(gate[:, t, :], pR[t % 2][:, :], gate[:, t, :], ALU.mult).then_inc(s["gated"], 1)
                    dve.wait_ge(s["gated"], NT * i + t + 1)
                    dve.wait_ge(s["moved"], i + 1)
                    wait(dve, s_store[t % 2], 16 * (NT // 2 * i + t // 2))
                    nc.vector.tensor_tensor(res[:, t % 2, :], gate[:, t, :], x3[:, t, :], ALU.add).then_inc(s["res"], 1)

            dve.wait_ge(s["ident"], 5)
            for t in range(NT):
                front_x3(0, t)
            front_norm(0)
            for c in range(C):
                front_mix(0, c)
            group(0, True)
            with dve.Fori(1, NG - 1) as i:
                group(i, True)
            group(NG - 1, False)

        @block.tensor
        def _(pe):
            pe.wait_ge(s["ident"], 2)
            pe.wait_ge(s["wl"], 3)

            def three(out, xh, xl, yh, yl, first, last):
                nc.tensor.matmul(out, xh, yh, start=first, stop=False)
                nc.tensor.matmul(out, xh, yl, start=False, stop=False)
                return nc.tensor.matmul(out, xl, yh, start=False, stop=last)

            def expand(j, t):
                pe.wait_ge(s["path"], 16 * (j + 1))
                pe.wait_ge(s["ctx"], 32 * (j + 1))
                wait(pe, s["x3"], NT * j + t - 1)
                q = slice(t * P, (t + 1) * P)
                nc.tensor.matmul(pE[t % 2][:, :], path[:, q], ch[:, :], start=True, stop=False)
                nc.tensor.matmul(pE[t % 2][:, :], path[:, q], cl[:, :], start=False, stop=True).then_inc(s["exp"], 1)

            def front_turn(j, c):
                pe.wait_ge(s["xn"], NT * (j + 1))
                wait(pe, s["xT"], C * j + c - 1)
                for t in range(NT):
                    last = nc.tensor.transpose(pT[c % 2][:, t * P:(t + 1) * P], xn[:, t, c * P:(c + 1) * P], ident[:, :])
                last.then_inc(s["turn"], 1)

            def gates(i, t):
                if t < 2:
                    wait(pe, s["gated"], NT * i)
                else:
                    pe.wait_ge(s["gate"], NT * i + t - 1)
                q = slice(t * P, (t + 1) * P)
                for c in range(C):
                    last = three(pR[t % 2][:, :], zh[:, 0, c, q], zl[:, 0, c, q], w["r"][0][:, c, :], w["r"][1][:, c, :], c == 0, c == C - 1)
                last.then_inc(s["R"], 1)

            def keys(i, m):
                wait(pe, s["squared"], C * i + m - 1)
                e = slice(m * P, (m + 1) * P)
                for c in range(C):
                    last = three(pK[m % 2][:, :], w["k"][0][:, c, e], w["k"][1][:, c, e], zh[:, 1, c, :], zl[:, 1, c, :], c == 0, c == C - 1)
                last.then_inc(s["K"], 1)

            def values(i, t):
                if t < 2:
                    pe.wait_ge(s["gate"], NT * (i + 1))
                else:
                    pe.wait_ge(s["gated"], NT * i + t - 1)
                pe.wait_ge(s["hlo"], C * (i + 1))
                q = slice(t * P, (t + 1) * P)
                for m in range(C):
                    last = three(pR[t % 2][:, :], hh[:, m, q], hl[:, m, q], w["v"][0][:, m, :], w["v"][1][:, m, :], m == 0, m == C - 1)
                last.then_inc(s["V"], 1)

            def group(i, more):
                pe.wait_ge(s["zlo"], 2 * C * (i + 1))
                for t in range(NT):
                    gates(i, t)
                    if more:
                        expand(i + 1, t)
                for m in range(C):
                    keys(i, m)
                for t in range(NT):
                    if more:
                        front_turn(i + 1, t)
                    values(i, t)

            for t in range(NT):
                expand(0, t)
            for c in range(C):
                front_turn(0, c)
            group(0, True)
            with pe.Fori(1, NG - 1) as i:
                group(i, True)
            group(NG - 1, False)


INPUTS = {
    "x": ("x", lambda v: v.reshape(B * T, DM)),
    "ctx": ("ctx_1024", lambda v: v),
    "mask": ("mask_Bx1xSxS2_bf1", lambda v: v.reshape(B * T, S)[:, ::-1].view("uint8")),
    "WqT": ("L0_xattn_Wq", lambda v: v.T), "bq": ("L0_xattn_bq", lambda v: v.reshape(C, P).T),
    "WkT": ("L0_xattn_Wk", lambda v: v.T), "bk": ("L0_xattn_bk", lambda v: v.reshape(C, P).T),
    "WvT": ("L0_xattn_Wv", lambda v: v.T), "bv": ("L0_xattn_bv", lambda v: v),
    "WoT": ("L0_xattn_Wo", lambda v: v.T), "bo": ("L0_xattn_bo", lambda v: v),
    "rel": ("L0_xattn_rel_emb", lambda v: v.T),
    "WfcT": ("L0_ffn_W_fc", lambda v: v.T), "WprojT": ("L0_ffn_W_proj", lambda v: v.T),
    "WrT": ("L1_ffn_W_r", lambda v: v.T), "WkkT": ("L1_ffn_W_k", lambda v: v.T), "WvvT": ("L1_ffn_W_v", lambda v: v.T),
    "mu_r": ("L1_ffn_mu_r", lambda v: v.reshape(C, P).T), "mu_k": ("L1_ffn_mu_k", lambda v: v.reshape(C, P).T),
}


def kernel(**inputs):
    import numpy as np
    import concourse.bacc as bacc
    from concourse.bass_utils import run_bass_kernel_spmd

    nc = bacc.Bacc("TRN2", target_bir_lowering=False, num_devices=1)
    arrays, a = {}, {}
    for name, (source, lay_out) in INPUTS.items():
        v = np.ascontiguousarray(lay_out(np.asarray(inputs[source])))
        arrays[f"in_{name}"] = v
        a[name] = nc.dram_tensor(f"in_{name}", v.shape, mybir.dt.from_np(v.dtype), kind="ExternalInput").ap()

    def scratch(name, shape, dt=F32):
        return nc.dram_tensor(f"s_{name}", shape, dt, kind="Internal").ap()

    d = {
        "kh": scratch("kh", (B, P, C, S)), "kl": scratch("kl", (B, P, C, S)),
        "c2h": scratch("c2h", (B, P, C, S)), "c2l": scratch("c2l", (B, P, C, S)),
        "vh": scratch("vh", (B, S, DM)), "vl": scratch("vl", (B, S, DM)),
        "ch": scratch("ch", (B, S, DM)), "cl": scratch("cl", (B, S, DM)),
        "aa": scratch("aa", (B, S, 1)), "rel": scratch("rel", (H, RELW)),
        "dist": scratch("dist", (B, NB, SLOTS * W)), "on": scratch("on", (B, NB, SLOTS * W)),
        "x1": scratch("x1", (B * T, DM)), "x2": scratch("x2", (B * T, DM)),
    }
    out = nc.dram_tensor("out", (B * T, DM), F32, kind="ExternalOutput").ap()
    prepare(nc, a, d)
    attention(nc, a, d)
    spiking(nc, a, d)
    align(nc, a, d)
    mixing(nc, a, d, out)
    r = run_bass_kernel_spmd(nc, [arrays], core_ids=[0])
    return r.results[0]["out"].reshape(B, T, DM)
```

```python
import concourse.bass as bass
from concourse import mybir
from contextlib import ExitStack

F32 = mybir.dt.float32
F32R = mybir.dt.float32r
BF16 = mybir.dt.bfloat16
U8 = mybir.dt.uint8
ALU = mybir.AluOpType
ACT = mybir.ActivationFunctionType
AX = mybir.AxisListType.X

P = 128
B, T, DM = 4, 2048, 512
S = 77
H, DH = 16, 32
HP = P // DH
C = DM // P
FF = 2048
NF = FF // P
G = 512
NT = G // P
NG = B * T // G
GB = T // G
MAX_REL = 1023
SCALE = DH ** -0.5
LN_EPS = 1e-5
BETA, THRESHOLD, STEPS = 0.9, 1.0, 5
BIG = 1e30
PAD = T - 1 - MAX_REL
RELW = PAD + 2 * MAX_REL + 1

W = 64
NB = T // W
SLOTS = S + NB - 1
SKEW_ROW, SKEW_BLOCK, SKEW_BATCH = W, (SLOTS + 1) * W, NB * SLOTS * W
GBLK = G // W


def wait(eng, sem, value):
    if not isinstance(value, int) or value > 0:
        eng.wait_ge(sem, value)


def start(eng, offset):
    return offset if isinstance(offset, int) else eng.snap(offset)


def rows(dram, first, tiles=NT, width=DM):
    tile = [[P * width, tiles]] if tiles > 1 else []
    return bass.AP(tensor=dram.tensor, offset=first, ap=[[width, P]] + tile + [[1, width]])


def skew_start(eng, group):
    return start(eng, (group // GB) * SKEW_BATCH + (group % GB) * (GBLK * SKEW_BLOCK))


def skewed(scratch, first):
    return bass.AP(tensor=scratch.tensor, offset=first,
                   ap=[[SKEW_ROW, S], [SKEW_BLOCK, GBLK], [1, W]])


def place(nc, ctx):
    def sb(name, shape, dt=F32):
        return ctx.enter_context(nc.sbuf_tensor(name, shape, dt))

    def ps(name, shape=(P, 512)):
        return ctx.enter_context(nc.psum_tensor(name, list(shape), F32))

    def sem(name):
        return ctx.enter_context(nc.semaphore(name))

    return sb, ps, sem


def identity(nc, eng, ident, s_ident):
    nc.gpsimd.memset(ident[:, :], 0.0).then_inc(s_ident, 1)
    eng.wait_ge(s_ident, 1)
    nc.gpsimd.affine_select(out=ident[:, :], in_=ident[:, :], compare_op=ALU.not_equal, fill=1.0,
                            base=0, pattern=[[-1, P]], channel_multiplier=1).then_inc(s_ident, 1)


def prepare(nc, a, d):
    with ExitStack() as ctx:
        sb, ps, sem = place(nc, ctx)
        ident = sb("p_ident", [P, P])
        wk = sb("p_wk", [P, C, DM])
        wv = sb("p_wv", [P, C, DM])
        bk = sb("p_bk", [P, C])
        bv = sb("p_bv", [S, DM])
        cx = sb("p_cx", [S, B, DM])
        cxT = sb("p_cxT", [P, B, C, S])
        cxR = sb("p_cxR", [P, B, C, S])
        kf = sb("p_kf", [P, B, C, S])
        kh = sb("p_kh", [P, B, C, S], F32R)
        kl = sb("p_kl", [P, B, C, S], F32R)
        vf = sb("p_vf", [S, B, DM])
        vh = sb("p_vh", [S, B, DM], F32R)
        vl = sb("p_vl", [S, B, DM], F32R)
        c2f = sb("p_c2f", [P, B, C, S])
        c2h = sb("p_c2h", [P, B, C, S], F32R)
        c2l = sb("p_c2l", [P, B, C, S], F32R)
        ch = sb("p_ch", [S, B, DM], F32R)
        cl = sb("p_cl", [S, B, DM], F32R)
        sq = sb("p_sq", [S, DM])
        aa = sb("p_aa", [S, B])
        rel = sb("p_rel", [H, 2 * MAX_REL + 1])
        relp = sb("p_relp", [H, PAD])
        zero = sb("p_zero", [P, SLOTS * W])
        pT = [ps(f"p_pT{b}") for b in range(B)]
        pK = [ps(f"p_pK{b}") for b in range(B)]
        s_ident, s_cx, s_w, s_b, s_rel = sem("p_ident_s"), sem("p_cx_s"), sem("p_w_s"), sem("p_b_s"), sem("p_rel_s")
        s_zero, s_relp, s_T, s_cxT, s_K, s_V = (sem("p_zero_s"), sem("p_relp_s"), sem("p_T_s"),
                                               sem("p_cxT_s"), sem("p_K_s"), sem("p_V_s"))
        s_full, s_hi, s_lo, s_aa, s_out = sem("p_full_s"), sem("p_hi_s"), sem("p_lo_s"), sem("p_aa_s"), sem("p_out_s")
        block = ctx.enter_context(nc.Block())

        @block.sync
        def _(sp):
            sp.dma_start(cx[:, :, :], a["ctx"].rearrange("b s d -> s b d")).then_inc(s_cx, 16)
            sp.dma_start(wk[:, :, :], a["WkT"].rearrange("(c p) d -> p c d", p=P)).then_inc(s_w, 16)
            sp.dma_start(wv[:, :, :], a["WvT"].rearrange("(c p) d -> p c d", p=P)).then_inc(s_w, 16)
            sp.dma_start(bk[:, :], a["bk"]).then_inc(s_b, 16)
            sp.dma_start(bv[:, :], a["bv"].partition_broadcast(S)).then_inc(s_b, 16)
            sp.dma_start(rel[:, :], a["rel"]).then_inc(s_rel, 16)
            n = 0
            sp.wait_ge(s_rel, 16)
            sp.dma_start(d["rel"][:, 0:2 * MAX_REL + 1], rel[:, :]).then_inc(s_out, 16)
            sp.wait_ge(s_relp, 1)
            sp.dma_start(d["rel"][:, 2 * MAX_REL + 1:RELW], relp[:, :]).then_inc(s_out, 16)
            n += 2
            sp.wait_ge(s_zero, 1)
            for b in range(B):
                sp.dma_start(bass.AP(tensor=d["dist"].tensor, offset=b * SKEW_BATCH,
                                     ap=[[SLOTS * W, NB], [1, SLOTS * W]]),
                             zero[b * NB:(b + 1) * NB, :]).then_inc(s_out, 16)
                n += 1
            sp.wait_ge(s_hi, 4)
            sp.wait_ge(s_lo, 4)
            sp.wait_ge(s_aa, B)
            for dst, src in (("kh", kh), ("kl", kl), ("c2h", c2h), ("c2l", c2l)):
                sp.dma_start(d[dst].rearrange("b p c s -> p b c s"), src[:, :, :, :].bitcast(F32)).then_inc(s_out, 16)
                n += 1
            for dst, src in (("vh", vh), ("vl", vl), ("ch", ch), ("cl", cl)):
                sp.dma_start(d[dst].rearrange("b s d -> s b d"), src[:, :, :].bitcast(F32)).then_inc(s_out, 16)
                n += 1
            for b in range(B):
                sp.dma_start(d["aa"][b, :, :], aa[:, b:b + 1]).then_inc(s_out, 16)
                n += 1
            sp.wait_ge(s_out, 16 * n)

        @block.gpsimd
        def _(pool):
            identity(nc, pool, ident, s_ident)
            nc.gpsimd.memset(zero[:, :], 0.0).then_inc(s_zero, 1)
            pool.wait_ge(s_rel, 16)
            nc.gpsimd.tensor_copy(relp[:, :], rel[:, 2 * MAX_REL:2 * MAX_REL + 1].broadcast_to([H, PAD])).then_inc(s_relp, 1)

        @block.tensor
        def _(pe):
            pe.wait_ge(s_ident, 2)
            pe.wait_ge(s_cx, 16)
            for b in range(B):
                for c in range(C):
                    last = nc.tensor.transpose(pT[b][:, c * S:(c + 1) * S], cx[:, b, c * P:(c + 1) * P],
                                               ident[0:S, 0:S])
                last.then_inc(s_T, 1)
            pe.wait_ge(s_w, 32)
            for b in range(B):
                pe.wait_ge(s_cxT, 2 * b + 2)
                for m in range(C):
                    for c in range(C):
                        last = nc.tensor.matmul(pK[b][:, m * S:(m + 1) * S], wk[:, c, m * P:(m + 1) * P],
                                                cxR[:, b, c, :], start=c == 0, stop=c == C - 1)
                last.then_inc(s_K, 1)
            for b in range(B):
                for c in range(C):
                    last = nc.tensor.matmul(pT[b][0:S, :], cxR[:, b, c, :], wv[:, c, :],
                                            start=c == 0, stop=c == C - 1)
                last.then_inc(s_V, 1)

        @block.vector
        def _(dve):
            for b in range(B):
                dve.wait_ge(s_T, b + 1)
                nc.vector.tensor_copy(cxT[:, b, :, :], pT[b][:, 0:C * S].rearrange("p (c s) -> p c s", s=S)).then_inc(s_cxT, 1)
                dve.wait_ge(s_cxT, 2 * b + 1)
                nc.vector.tensor_copy(cxR[:, b, :, :], cxT[:, b, :, ::-1]).then_inc(s_cxT, 1)
            dve.wait_ge(s_b, 32)
            for b in range(B):
                dve.wait_ge(s_K, b + 1)
                for m in range(C):
                    nc.vector.tensor_scalar(kf[:, b, m, :], pK[b][:, m * S:(m + 1) * S], bk[:, m:m + 1], SCALE,
                                            ALU.add, ALU.mult).then_inc(s_full, 1)
            for b in range(B):
                dve.wait_ge(s_V, b + 1)
                nc.vector.tensor_tensor(vf[:, b, :], pT[b][0:S, :], bv[:, :], ALU.add).then_inc(s_full, 1)
            dve.wait_ge(s_cxT, 2 * B)
            nc.vector.tensor_scalar(c2f[:, :, :, :], cxT[:, :, :, :], -2.0, None, ALU.mult).then_inc(s_full, 1)
            for n, (full, hi, lo) in enumerate(((kf, kh, kl), (vf, vh, vl), (c2f, c2h, c2l), (cx, ch, cl))):
                dve.wait_ge(s_hi, n + 1)
                flat = "p b d -> p (b d)" if n % 2 else "p b c s -> p (b c s)"
                full, hi, lo = (r[:].rearrange(flat) for r in (full, hi, lo))
                nc.vector.tensor_tensor(lo, full, hi.bitcast(F32), ALU.subtract).then_inc(s_lo, 1)

        @block.scalar
        def _(act):
            act.wait_ge(s_cx, 16)
            for b in range(B):
                if b:
                    act.wait_ge(s_aa, b)
                nc.scalar.activation(sq[:, :], cx[:, b, :], ACT.Square, accum_out=aa[:, b:b + 1]).then_inc(s_aa, 1)
            act.wait_ge(s_full, B * C)
            nc.scalar.activation(kh[:, :, :, :], kf[:, :, :, :], ACT.Copy).then_inc(s_hi, 1)
            act.wait_ge(s_full, B * C + B)
            nc.scalar.activation(vh[:, :, :], vf[:, :, :], ACT.Copy).then_inc(s_hi, 1)
            act.wait_ge(s_full, B * C + B + 1)
            nc.scalar.activation(c2h[:, :, :, :], c2f[:, :, :, :], ACT.Copy).then_inc(s_hi, 1)
            nc.scalar.activation(ch[:, :, :], cx[:, :, :], ACT.Copy).then_inc(s_hi, 1)


def attention(nc, a, d):
    with ExitStack() as ctx:
        sb, ps, sem = place(nc, ctx)
        STEPS_JOBS = ("P0 P1 P2 P3 Q", "P0 P1 P2 P3 Q X0 X1", "P0 P1 X2 P2 X3 P3 Q", "P0 P1 P2 P3 Q")
        LAST_JOBS = ("P0 P1 P2 P3 Q", "P0 P1 P2 P3 Q", "P0 P1 P2 P3", "P0 P1 P2 P3")
        FIRST = C + 2
        number = {more: {(m, kind): n for n, (m, kind) in enumerate(
                      (m, kind) for m, line in enumerate(lines) for kind in line.split())}
                  for more, lines in ((True, STEPS_JOBS), (False, LAST_JOBS))}
        JOBS = len(number[True])
        ident = sb("a_ident", [P, P])
        wqh, wql = (sb(f"a_wq{n}", [P, C, DM], F32R) for n in "hl")
        woh, wol = (sb(f"a_wo{n}", [P, C, DM], F32R) for n in "hl")
        bq = sb("a_bq", [P, C])
        bo = sb("a_bo", [P, DM])
        half = sb("a_half", [P, NT])
        x = sb("a_x", [P, NT, DM])
        res = sb("a_res", [P, 2, DM])
        stats = sb("a_stats", [P, NT, 6])
        pause = sb("a_pause", [P, 1])
        mv = sb("a_mv", [P, NT, 2])
        ve = sb("a_ve", [P, NT])
        rstd = sb("a_rstd", [P, NT])
        xTh, xTl = (sb(f"a_xT{n}", [P, C, G], F32R) for n in "hl")
        qTh, qTl = (sb(f"a_qT{n}", [P, G], F32R) for n in "hl")
        kbh, kbl = (sb(f"a_kb{n}", [P, 2, C, HP * S], F32R) for n in "hl")
        vh, vl = (sb(f"a_v{n}", [S, 2, C, HP, P], F32R) for n in "hl")
        mask = sb("a_mask", [P, NT, S], U8)
        mneg = sb("a_mneg", [P, NT, S])
        huge = sb("a_huge", [P, 2])
        bias = sb("a_bias", [P, 2, HP, G])
        bm = sb("a_bm", [P, NT, HP, S])
        sc = sb("a_sc", [P, 2, NT, HP, S])
        mx = sb("a_mx", [P, 2, NT, HP])
        rs = sb("a_rs", [P, 2, NT, HP])
        ri = sb("a_ri", [P, 2, NT, HP])
        pTh, pTl = (sb(f"a_pT{n}", [S, HP, G], F32R) for n in "hl")
        oTh, oTl = (sb(f"a_oT{n}", [P, 2, C, G], F32R) for n in "hl")
        pW = [ps(f"a_pW{n}") for n in range(2)]
        pS = ctx.enter_context(nc.psum_tensor("a_pS", [P, NT, 512], F32))
        pV = ps("a_pV")
        pO = ps("a_pO")
        names = ("cleared ident w wh wl const x stat aggr var rstd xn xb split hi lo mask mneg bm score added maxed "
                 "exped recip normed pv ohi olo wo x1").split()
        s = {n: sem(f"a_{n}_s") for n in names}
        s_kb, s_v, s_bias, s_res, s_store = ([sem(f"a_{name}{n}_s") for n in range(2)]
                                             for name in ("kb", "v", "bias", "res", "store"))
        block = ctx.enter_context(nc.Block())
        stage = [x[:, :, :], sc[:, :, :, :, :].rearrange("p u t j s -> p (u t j s)")[:, 0:C * DM].rearrange("p (c d) -> p c d", d=DM)]

        def job(i, m, kind, more):
            return JOBS * i + FIRST + number[more][(m, kind)] + 1

        def load_keys(sp, i, side, pair):
            first = start(sp, (i // GB) * (P * C * S))
            at = [start(sp, first + j * DH * C * S) for j in range(HP)]
            for hi_lo, (dst, src) in enumerate(((kbh, d["kh"]), (kbl, d["kl"]))):
                for j in range(HP):
                    r = slice(j * DH, (j + 1) * DH)
                    if j == 0 and hi_lo == 0:
                        wait(sp, s["score"], 2 * C * (i - 1))
                    sp.dma_start(dst[r, side, :, j * S:(j + 1) * S].bitcast(F32),
                                 bass.AP(tensor=src.tensor, offset=at[j], ap=[[C * S, DH], [S, C], [1, S]])).then_inc(s_kb[side], 16)

        def load_values(sp, i, side):
            first = start(sp, (i // GB) * (S * DM))
            at = [start(sp, first + j * DH) for j in range(HP)]
            for hi_lo, (dst, src) in enumerate(((vh, d["vh"]), (vl, d["vl"]))):
                for j in range(HP):
                    e = slice(j * DH, (j + 1) * DH)
                    if j == 0 and hi_lo == 0:
                        wait(sp, s["pv"], C * (i - 1))
                    sp.dma_start(dst[:, side, :, j, e].bitcast(F32),
                                 bass.AP(tensor=src.tensor, offset=at[j], ap=[[DM, S], [P, C], [1, DH]])).then_inc(s_v[side], 16)

        def load_bias(sp, i, m):
            first = start(sp, (i % GB) * G + (MAX_REL - (S - 1) + m * HP * RELW))
            wait(sp, s["bm"], 2 * (C * i + m) - 2)
            sp.dma_start(bias[:, m % 2, :, 0:G - P + S],
                         bass.AP(tensor=d["rel"].tensor, offset=first,
                                 ap=[[1, P], [RELW, HP], [1, G - P + S]])).then_inc(s_bias[m % 2], 16)

        def load_mask(sp, i):
            first = start(sp, i * (G * S))
            sp.dma_start(mask[:, :, :], rows(a["mask"], first, width=S)).then_inc(s["mask"], 16)

        def load_x(sp, i):
            first = start(sp, i * (G * DM))
            if isinstance(i, int) and i == 1:
                sp.wait_ge(s["split"], C)
            elif not isinstance(i, int) or i:
                sp.wait_ge(s["split"], job(i - 2, 2, "X3", True))
            sp.dma_start(x[:, :, :], rows(a["x"], first)).then_inc(s["x"], 16)

        def load_res(sp, i, m):
            first = start(sp, i * (G * DM) + m * P * DM)
            wait(sp, s_store[m % 2], 16 * (2 * i + m // 2))
            sp.dma_start(res[:, m % 2, :], rows(a["x"], first, 1)).then_inc(s_res[m % 2], 16)

        @block.sync
        def _(sp):
            sp.dma_start(bq[:, :], a["bq"]).then_inc(s["const"], 16)
            sp.dma_start(bo[:, :], a["bo"].partition_broadcast(P)).then_inc(s["const"], 16)
            for n, w in enumerate(("WqT", "WoT")):
                sp.dma_start(stage[n], a[w].rearrange("(c p) d -> p c d", p=P)).then_inc(s["w"], 16)
                sp.wait_ge(s["w"], 16 * n + 16)
            load_mask(sp, 0)
            load_bias(sp, 0, 0)
            sp.wait_ge(s["wl"], 1)
            load_x(sp, 0)
            load_bias(sp, 0, 1)
            sp.wait_ge(s["cleared"], 4)
            load_keys(sp, 0, 0, 0)
            load_values(sp, 0, 0)
            load_bias(sp, 0, 2)

            def store(i, m):
                first = start(sp, i * (G * DM) + m * P * DM)
                sp.wait_ge(s["x1"], C * i + m + 1)
                sp.dma_start(rows(d["x1"], first, 1), res[:, m % 2, :]).then_inc(s_store[m % 2], 16)

            def group(i, side, more, first=False):
                if more:
                    load_x(sp, i + 1)
                for m in range(C):
                    if m < 1:
                        load_bias(sp, i, m + 3)
                        if more:
                            load_mask(sp, i + 1)
                    elif more:
                        load_bias(sp, i + 1, m - 1)
                    if m == 0 and more:
                        load_keys(sp, i + 1, 1 - side, 0)
                        load_values(sp, i + 1, 1 - side)
                    if not first:
                        store(i - 1, m)
                    if m < 2:
                        if not first:
                            load_res(sp, i - 1, m + 2)
                    else:
                        load_res(sp, i, m - 2)

            group(0, 0, True, True)
            with sp.Fori(0, NG // 2 - 1) as k:
                group(k * 2 + 1, 1, True)
                group(k * 2 + 2, 0, True)
            group(NG - 1, 1, False)
            for m in range(C):
                store(NG - 1, m)
                if m < 2:
                    load_res(sp, NG - 1, m + 2)
            for n in range(2):
                sp.wait_ge(s_store[n], 16 * NG * NT // 2)

        @block.gpsimd
        def _(pool):
            identity(nc, pool, ident, s["ident"])
            nc.gpsimd.memset(half[:, :], -0.5).then_inc(s["ident"], 1)
            nc.gpsimd.memset(huge[:, 0:1], -1.0).then_inc(s["ident"], 1)
            nc.gpsimd.memset(huge[:, 1:2], 3e38).then_inc(s["ident"], 1)
            for values in (vh, vl):
                nc.gpsimd.memset(values[:].rearrange("s a c j p -> s (a c j p)").bitcast(F32), 0.0).then_inc(s["cleared"], 1)
            pool.wait_ge(s["ident"], 5)
            pool.wait_ge(s["const"], 32)

            def column(n):
                return huge[:, n:n + 1].unsqueeze(2).broadcast_to([P, NT, S])

            def exponent(i):
                pool.wait_ge(s["var"], i + 1)
                nc.gpsimd.tensor_tensor(rstd[:, :], ve[:, :], half[:, :], ALU.pow).then_inc(s["rstd"], 1)

            def add_bo(i, m):
                pool.wait_ge(s_res[m % 2], 16 * (2 * i + m // 2) + 16)
                nc.gpsimd.tensor_tensor(res[:, m % 2, :], res[:, m % 2, :], bo[:, :], ALU.add).then_inc(s["xb"], 1)

            def mask_row(i):
                pool.wait_ge(s["mask"], 16 * i + 16)
                wait(pool, s["bm"], 2 * C * i)
                for n, (in0, in1, op) in enumerate(((mask[:, :, :], column(0), ALU.add), (mneg[:, :, :], column(1), ALU.mult),
                                                    (mneg[:, :, :], mneg[:, :, :], ALU.add))):
                    nc.gpsimd.tensor_tensor(mneg[:, :, :], in0, in1, op).then_inc(s["mneg"], 1)
                    pool.wait_ge(s["mneg"], 3 * i + n + 1)

            def add_mask(i, m, h):
                if h == 0:
                    pool.wait_ge(s_bias[m % 2], 16 * (2 * i + m // 2) + 16)
                wait(pool, s["added"], 2 * (C * i + m - 1) + h + 1)
                t = slice(2 * h, 2 * h + 2)
                nc.gpsimd.tensor_tensor(
                    bm[:, t, :, :], bias[:, m % 2, :, :].rearrange("p j (t q) -> p t j q", q=P)[:, t, :, 0:S],
                    mneg[:, t, :].unsqueeze(2).broadcast_to([P, 2, HP, S]), ALU.add).then_inc(s["bm"], 1)

            def normalise_probs(i, m, h):
                t = slice(2 * h, 2 * h + 2)
                pool.wait_ge(s["recip"], 2 * (C * i + m) + h + 1)
                nc.gpsimd.tensor_tensor(sc[:, m % 2, t, :, :], sc[:, m % 2, t, :, :],
                                        ri[:, m % 2, t, :].unsqueeze(3).broadcast_to([P, 2, HP, S]), ALU.mult).then_inc(s["normed"], 1)

            def group(i, more, first=False):
                for m in range(C):
                    one = (i, m + 1) if m < C - 1 else (i + 1, 0)
                    two = (i, m + 2) if m < 2 else (i + 1, m - 2)
                    if m == 2 and more:
                        mask_row(i + 1)
                    if m < 2 or more:
                        add_mask(*two, 0)
                        add_mask(*two, 1)
                    if m < C - 1 or more:
                        normalise_probs(*one, 0)
                        normalise_probs(*one, 1)
                    if m == 0 and more:
                        exponent(i + 1)
                    if m == C - 1:
                        add_bo(i, 0)
                    elif not first:
                        add_bo(i - 1, m + 1)

            exponent(0)
            mask_row(0)
            add_mask(0, 0, 0)
            add_mask(0, 0, 1)
            add_mask(0, 1, 0)
            add_mask(0, 1, 1)
            normalise_probs(0, 0, 0)
            normalise_probs(0, 0, 1)
            group(0, True, True)
            with pool.Fori(0, NG // 2 - 1) as k:
                group(k * 2 + 1, True)
                group(k * 2 + 2, True)
            group(NG - 1, False)
            for m in range(1, C):
                add_bo(NG - 1, m)

        @block.scalar
        def _(act):
            for n, wh in enumerate((wqh, woh)):
                act.wait_ge(s["w"], 16 * n + 16)
                nc.scalar.activation(wh[:, :, :], stage[n], ACT.Copy).then_inc(s["wh"], 1)
            act.wait_ge(s["const"], 32)

            def hi(done, n, out, in_):
                act.wait_ge(s["split"], done)
                nc.scalar.activation(out, in_, ACT.Copy).then_inc(s["hi"], 1)

            def hi_x(done, n, c):
                hi(done, n, xTh[:, c, :], pW[n % 2][:, :])

            def hi_q(done, n, m):
                act.wait_ge(s["split"], done)
                nc.scalar.activation(qTh[:, :], pW[n % 2][:, :], ACT.Identity, bias=bq[:, m:m + 1]).then_inc(s["hi"], 1)

            def exp(i, m, t):
                if t % 2 == 0:
                    act.wait_ge(s["maxed"], 2 * (C * i + m) + t // 2 + 1)
                for j in range(HP):
                    last = nc.scalar.activation(sc[:, m % 2, t, j, :], sc[:, m % 2, t, j, :], ACT.Exp,
                                                bias=mx[:, m % 2, t, j:j + 1], accum_out=rs[:, m % 2, t, j:j + 1])
                if t % 2:
                    last.then_inc(s["exped"], 1)

            exp_after = {"P1": (0,), "P2": (1,), "P3": (2, 3)}

            def group(i, side, more):
                for m in range(C):
                    one = (i, m + 1) if m < C - 1 else (i + 1, 0)
                    for kind in (STEPS_JOBS if more else LAST_JOBS)[m].split():
                        n, done = number[more][(m, kind)], job(i, m, kind, more)
                        if kind[0] == "P":
                            j = int(kind[1])
                            hi(done, n, pTh[:, j, :], pW[n % 2][0:S, :])
                        elif kind[0] == "X":
                            hi_x(done, n, int(kind[1]))
                        else:
                            hi_q(done, n, (m + 2) % C)
                        if m < C - 1 or more:
                            for t in exp_after.get(kind, ()):
                                exp(*one, t)
                        if kind == ("X0" if m == 1 and more else "Q" if m < 2 or more else "P3"):
                            act.wait_ge(s["pv"], C * i + m + 1)
                            nc.scalar.activation(oTh[:, side, m, :], pV[:, :], ACT.Copy).then_inc(s["ohi"], 1)

            for c in range(C):
                hi_x(c + 1, c, c)
            hi_q(C + 1, C, 0)
            for t in range(NT):
                exp(0, 0, t)
            hi_q(C + 2, C + 1, 1)
            group(0, 0, True)
            with act.Fori(0, NG // 2 - 1) as k:
                group(k * 2 + 1, 1, True)
                group(k * 2 + 2, 0, True)
            group(NG - 1, 1, False)

        @block.vector
        def _(dve):
            for n, (wh, wl) in enumerate(((wqh, wql), (woh, wol))):
                dve.wait_ge(s["wh"], n + 1)
                nc.vector.tensor_tensor(wl[:, :, :], stage[n], wh[:, :, :].bitcast(F32), ALU.subtract).then_inc(s["wl"], 1)
                keys = (kbh, kbl)[n]
                nc.vector.memset(keys[:].rearrange("p a c s -> p (a c s)").bitcast(F32), 0.0).then_inc(s["cleared"], 1)

            def norm_stats(i):
                dve.wait_ge(s["x"], 16 * i + 16)
                for t in range(NT):
                    nc.vector.bn_stats(stats[:, t, :], x[:, t, :]).then_inc(s["stat"], 1)
                dve.wait_ge(s["stat"], NT * i + NT)
                nc.vector.memset(pause[:, :], 0.0)
                for t in range(NT):
                    nc.vector.bn_aggr(mv[:, t, :], stats[:, t, :]).then_inc(s["aggr"], 1)
                dve.wait_ge(s["aggr"], NT * i + NT)
                nc.vector.tensor_scalar(ve[:, :], mv[:, :, 1], LN_EPS, None, ALU.add).then_inc(s["var"], 1)

            def normalise(i):
                dve.wait_ge(s["rstd"], i + 1)
                for t in range(NT):
                    nc.vector.tensor_scalar(x[:, t, :], x[:, t, :], mv[:, t, 0:1], rstd[:, t:t + 1],
                                            ALU.subtract, ALU.mult).then_inc(s["xn"], 1)

            def lo(done, out, in_, high):
                dve.wait_ge(s["hi"], done)
                nc.vector.tensor_tensor(out, in_, high.bitcast(F32), ALU.subtract).then_inc(s["lo"], 1)

            def lo_x(done, n, c):
                lo(done, xTl[:, c, :], pW[n % 2][:, :], xTh[:, c, :])

            def lo_q(done, n, m):
                dve.wait_ge(s["hi"], done)
                nc.vector.scalar_tensor_tensor(qTl[:, :], pW[n % 2][:, :], bq[:, m:m + 1],
                                               qTh[:, :].bitcast(F32), ALU.add, ALU.subtract).then_inc(s["lo"], 1)

            def add(i, m, h):
                t = slice(2 * h, 2 * h + 2)
                dve.wait_ge(s["score"], 2 * (C * i + m) + h + 1)
                dve.wait_ge(s["bm"], 2 * (C * i + m) + h + 1)
                nc.vector.tensor_tensor(sc[:, m % 2, t, :, :].rearrange("p t j s -> p t (j s)"), pS[:, t, 0:HP * S],
                                        bm[:, t, :, :].rearrange("p t j s -> p t (j s)"), ALU.add).then_inc(s["added"], 1)

            def maximum(i, m, h):
                t = slice(2 * h, 2 * h + 2)
                dve.wait_ge(s["added"], 2 * (C * i + m) + h + 1)
                nc.vector.tensor_reduce(mx[:, m % 2, t, :], sc[:, m % 2, t, :, :], AX, ALU.max, negate=True).then_inc(s["maxed"], 1)

            def reciprocal(i, m, h):
                t = slice(2 * h, 2 * h + 2)
                dve.wait_ge(s["exped"], 2 * (C * i + m) + h + 1)
                nc.vector.reciprocal(ri[:, m % 2, t, :], rs[:, m % 2, t, :]).then_inc(s["recip"], 1)

            def add_res(i, m):
                dve.wait_ge(s["wo"], C * i + m + 1)
                dve.wait_ge(s["xb"], C * i + m + 1)
                nc.vector.tensor_tensor(res[:, m % 2, :], pO[:, :], res[:, m % 2, :], ALU.add).then_inc(s["x1"], 1)

            def group(i, side, more, first=False):
                for m in range(C):
                    one = (i, m + 1) if m < C - 1 else (i + 1, 0)
                    ahead = m < C - 1 or more
                    if ahead:
                        add(*one, 0)
                        maximum(*one, 0)
                    for kind in (STEPS_JOBS if more else LAST_JOBS)[m].split():
                        n, done = number[more][(m, kind)], job(i, m, kind, more)
                        if kind == "P2" and ahead:
                            maximum(*one, 1)
                        if kind == "P3" and ahead:
                            reciprocal(*one, 0)
                        if kind == "P3" and not first:
                            add_res(i - 1, m)
                        if kind[0] == "P":
                            j = int(kind[1])
                            lo(done, pTl[:, j, :], pW[n % 2][0:S, :], pTh[:, j, :])
                        elif kind[0] == "X":
                            lo_x(done, n, int(kind[1]))
                        else:
                            lo_q(done, n, (m + 2) % C)
                        if kind == "P1" and ahead:
                            add(*one, 1)
                        if kind == "P3" and more:
                            if m == 0:
                                norm_stats(i + 1)
                            if m == 1:
                                normalise(i + 1)
                        if kind == "P3" and ahead:
                            reciprocal(*one, 1)
                        if kind == ("X0" if m == 1 and more else "Q" if m < 2 or more else "P3"):
                            dve.wait_ge(s["ohi"], C * i + m + 1)
                            nc.vector.tensor_tensor(oTl[:, side, m, :], pV[:, :], oTh[:, side, m, :].bitcast(F32),
                                                    ALU.subtract).then_inc(s["olo"], 1)

            norm_stats(0)
            dve.wait_ge(s["wl"], 2)
            normalise(0)
            for c in range(C):
                lo_x(c + 1, c, c)
            lo_q(C + 1, C, 0)
            for h in range(2):
                add(0, 0, h)
                maximum(0, 0, h)
            lo_q(C + 2, C + 1, 1)
            for h in range(2):
                reciprocal(0, 0, h)
            group(0, 0, True, True)
            with dve.Fori(0, NG // 2 - 1) as k:
                group(k * 2 + 1, 1, True)
                group(k * 2 + 2, 0, True)
            group(NG - 1, 1, False)
            for m in range(C):
                add_res(NG - 1, m)

        @block.tensor
        def _(pe):
            pe.wait_ge(s["ident"], 2)
            pe.wait_ge(s["wl"], 2)

            def three(out, xh, xl, yh, yl, first=True, last=True):
                nc.tensor.matmul(out, xh, yh, start=first, stop=False)
                nc.tensor.matmul(out, xh, yl, start=False, stop=False)
                return nc.tensor.matmul(out, xl, yh, start=False, stop=last)

            def turn_x(done, n, c):
                wait(pe, s["lo"], done - 2)
                for t in range(NT):
                    last = nc.tensor.transpose(pW[n % 2][:, t * P:(t + 1) * P], x[:, t, c * P:(c + 1) * P], ident[:, :])
                last.then_inc(s["split"], 1)

            def queries(done, n, m):
                pe.wait_ge(s["lo"], done - 2)
                w = slice(m * P, (m + 1) * P)
                for c in range(C):
                    last = three(pW[n % 2][:, :], wqh[:, c, w], wql[:, c, w], xTh[:, c, :], xTl[:, c, :], c == 0, c == C - 1)
                last.then_inc(s["split"], 1)

            def scores(i, m, side):
                for h in range(2):
                    wait(pe, s["added"], 2 * (C * i + m - 1) + h + 1)
                    for t in (2 * h, 2 * h + 1):
                        q = slice(t * P, (t + 1) * P)
                        last = three(pS[:, t, 0:HP * S], qTh[:, q], qTl[:, q], kbh[:, side, m, :], kbl[:, side, m, :])
                    last.then_inc(s["score"], 1)

            def turn_probs(i, m, j, more):
                n, done = number[more][(m, f"P{j}")], job(i, m, f"P{j}", more)
                pe.wait_ge(s["lo"], done - 2)
                if j == 0:
                    pe.wait_ge(s["normed"], 2 * (C * i + m) + 2)
                for t in range(NT):
                    last = nc.tensor.transpose(pW[n % 2][0:S, t * P:(t + 1) * P], sc[:, m % 2, t, j, :], ident[:, :])
                last.then_inc(s["split"], 1)

            def weigh(i, m, j, side, more):
                if j == 0:
                    wait(pe, s["olo"], C * i + m)
                pe.wait_ge(s["lo"], job(i, m, f"P{j}", more))
                last = three(pV[:, :], vh[:, side, m, j, :], vl[:, side, m, j, :], pTh[:, j, :], pTl[:, j, :], j == 0, j == HP - 1)
                if j == HP - 1:
                    last.then_inc(s["pv"], 1)

            def project(i, m, side, chunks):
                for c in chunks:
                    if c == 0:
                        if m == 0:
                            pe.wait_ge(s["olo"], C * i + C)
                        else:
                            pe.wait_ge(s["x1"], C * i + m)
                    q = slice(m * P, (m + 1) * P)
                    last = three(pO[:, :], oTh[:, side, c, q], oTl[:, side, c, q], woh[:, c, :], wol[:, c, :], c == 0, c == C - 1)
                    if c == C - 1:
                        last.then_inc(s["wo"], 1)

            def group(i, side, pair, more, first=False):
                pe.wait_ge(s_v[side], 16 * 2 * HP * (pair + 1))
                for m in range(C):
                    two = (i, m + 2, side) if m < 2 else (i + 1, m - 2, 1 - side)
                    ahead = m < 2 or more

                    def turn(c):
                        if c == 0:
                            pe.wait_ge(s["xn"], NT * (i + 2))
                        turn_x(job(i, m, f"X{c}", True), number[True][(m, f"X{c}")], c)

                    turn_probs(i, m, 0, more)
                    turn_probs(i, m, 1, more)
                    if not first:
                        project(i - 1, m, 1 - side, (0, 1))
                    if m == 2 and more:
                        turn(2)
                    turn_probs(i, m, 2, more)
                    if not first:
                        project(i - 1, m, 1 - side, (2, 3))
                    if m == 2 and more:
                        turn(3)
                    turn_probs(i, m, 3, more)
                    weigh(i, m, 0, side, more)
                    if m == 2:
                        weigh(i, m, 1, side, more)
                    if ahead:
                        if m == 2:
                            pe.wait_ge(s["lo"], job(i, m, "X3", True))
                        queries(job(i, m, "Q", more), number[more][(m, "Q")], (m + 2) % C)
                    if m == 1 and more:
                        turn(0)
                    if m != 2:
                        weigh(i, m, 1, side, more)
                    weigh(i, m, 2, side, more)
                    weigh(i, m, 3, side, more)
                    if m == 1 and more:
                        turn(1)
                    if ahead:
                        if m == 2:
                            pe.wait_ge(s_kb[1 - side], 16 * 2 * HP * (pair + side + 1))
                        pe.wait_ge(s["lo"], job(i, m, "Q", more))
                        scores(*two)

            pe.wait_ge(s["xn"], NT)
            for c in range(C):
                turn_x(c + 1, c, c)
            pe.wait_ge(s["lo"], C)
            queries(C + 1, C, 0)
            pe.wait_ge(s["lo"], C + 1)
            pe.wait_ge(s_kb[0], 16 * 2 * HP)
            scores(0, 0, 0)
            queries(C + 2, C + 1, 1)
            pe.wait_ge(s["lo"], C + 2)
            scores(0, 1, 0)
            group(0, 0, 0, True, True)
            with pe.Fori(0, NG // 2 - 1) as k:
                group(k * 2 + 1, 1, k, True)
                group(k * 2 + 2, 0, k + 1, True)
            group(NG - 1, 1, NG // 2 - 1, False)
            for m in range(C):
                project(NG - 1, m, 1, range(C))


def spiking(nc, a, d):
    with ExitStack() as ctx:
        sb, ps, sem = place(nc, ctx)
        TURNS = C + NF
        BACKS = C + 1
        ident = sb("f_ident", [P, P])
        ones = sb("f_ones", [1, S])
        half = sb("f_half", [P, NT])
        wfh, wfl = (sb(f"f_wf{n}", [P, C, FF], F32R) for n in "hl")
        wph, wpl = (sb(f"f_wp{n}", [P, NF, DM], F32R) for n in "hl")
        x = sb("f_x", [P, NT, DM])
        y = sb("f_y", [P, NT, DM])
        xp = sb("f_xp", [P, NT, DM])
        xTh, xTl = (sb(f"f_xT{n}", [P, C, G], F32R) for n in "hl")
        r = sb("f_r", [P, 2, G])
        hh, hl = (sb(f"f_h{n}", [P, 2, G], F32R) for n in "hl")
        bTh, bTl = (sb(f"f_bT{n}", [P, 2, G], F32R) for n in "hl")
        mem = sb("f_mem", [P, DM])
        lead = sb("f_lead", [P, DM])
        count = sb("f_count", [P, DM])
        dist = sb("f_dist", [S, G])
        stats = sb("f_stats", [P, NT, 6])
        pause = sb("f_pause", [P, 1])
        mv = sb("f_mv", [P, NT, 2])
        ve = sb("f_ve", [P, NT])
        rstd = sb("f_rstd", [P, NT])
        stats2 = sb("f_stats2", [P, NT, 6])
        mv2 = sb("f_mv2", [P, NT, 2])
        ve2 = sb("f_ve2", [P, NT])
        rstd2 = sb("f_rstd2", [P, NT])
        sq = sb("f_sq", [P, NT])
        bb = sb("f_bb", [1, G])
        ch, cl = (sb(f"f_c{n}", [P, C, S], F32R) for n in "hl")
        aa = sb("f_aa", [S, 1])
        pH = [ps(f"f_pH{n}") for n in range(2)]
        pY = ctx.enter_context(nc.psum_tensor("f_pY", [P, NT, 512], F32))
        pB = ps("f_pB")
        pD = ps("f_pD")
        names = ("ident w wh wl x stat aggr var rstd xn turn hi lo relued squared hhi hlo y ycopied xp lif "
                 "x2 stored2 stat2 aggr2 var2 rstd2 xn2 sq back bhi blo bb ctx dist dclip dsqrt dstore").split()
        s = {n: sem(f"f_{n}_s") for n in names}
        block = ctx.enter_context(nc.Block())
        stage = [x, y]
        WCH = 2 * C
        LIF = 4 + 3 * (STEPS - 2)
        F_STATS, F_NEXT, F_BACK = 8, 10, 10

        @block.sync
        def _(sp):
            for n in range(WCH):
                if n >= 2:
                    sp.wait_ge(s["wl"], n - 1)
                if n < C:
                    src = a["WfcT"][n * P:(n + 1) * P, :].rearrange("p (q d) -> p q d", d=DM)
                else:
                    src = a["WprojT"][(n - C) * 4 * P:(n - C + 1) * 4 * P, :].rearrange("(q p) d -> p q d", p=P)
                if n:
                    sp.wait_ge(s["w"], 16 * n)
                sp.dma_start(stage[n % 2][:, :, :], src).then_inc(s["w"], 16)

            def load_x(i):
                first = start(sp, i * (G * DM))
                wait(sp, s["lo"], C * i)
                sp.dma_start(x[:, :, :], rows(d["x1"], first)).then_inc(s["x"], 16)

            def load_back(k):
                batch, at_aa, first = (start(sp, (k // GB) * (P * C * S)), start(sp, (k // GB) * S), start(sp, k * (G * DM)))
                wait(sp, s["dsqrt"], k)
                sp.dma_start(ch[:, :, :].bitcast(F32), bass.AP(tensor=d["c2h"].tensor, offset=batch, ap=[[C * S, P], [S, C], [1, S]])).then_inc(s["ctx"], 16)
                sp.dma_start(cl[:, :, :].bitcast(F32), bass.AP(tensor=d["c2l"].tensor, offset=batch, ap=[[C * S, P], [S, C], [1, S]])).then_inc(s["ctx"], 16)
                sp.dma_start(aa[:, :], bass.AP(tensor=d["aa"].tensor, offset=at_aa, ap=[[1, S], [1, 1]])).then_inc(s["ctx"], 16)
                wait(sp, s["stored2"], 16 * k)
                sp.dma_start(xp[:, :, :], rows(d["x1"], first)).then_inc(s["xp"], 16)

            def store_back(k):
                first, block_ = start(sp, k * (G * DM)), skew_start(sp, k)
                sp.wait_ge(s["x2"], NT * (k + 1))
                sp.dma_start(rows(d["x2"], first), xp[:, :, :]).then_inc(s["stored2"], 16)
                sp.wait_ge(s["dsqrt"], k + 1)
                sp.dma_start(skewed(d["dist"], block_), dist[:, :].rearrange("s (c w) -> s c w", w=W)).then_inc(s["dstore"], 16)

            def group(i, back, more):
                if back:
                    load_back(i - 1)
                if more:
                    load_x(i + 1)
                if back:
                    store_back(i - 1)

            sp.wait_ge(s["wl"], WCH - 1)
            load_x(0)
            group(0, False, True)
            group(1, True, True)
            with sp.Fori(2, NG - 1) as i:
                group(i, True, True)
            group(NG - 1, True, False)
            load_back(NG - 1)
            store_back(NG - 1)
            sp.wait_ge(s["stored2"], 16 * NG)
            sp.wait_ge(s["dstore"], 16 * NG)

        @block.gpsimd
        def _(pool):
            identity(nc, pool, ident, s["ident"])
            nc.gpsimd.memset(half[:, :], -0.5).then_inc(s["ident"], 1)
            nc.gpsimd.memset(ones[:, :], 1.0).then_inc(s["ident"], 1)
            pool.wait_ge(s["ident"], 4)

            def exponent(i):
                pool.wait_ge(s["var"], i + 1)
                nc.gpsimd.tensor_tensor(rstd[:, :], ve[:, :], half[:, :], ALU.pow).then_inc(s["rstd"], 1)

            def exponent2(k):
                pool.wait_ge(s["var2"], k + 1)
                nc.gpsimd.tensor_tensor(rstd2[:, :], ve2[:, :], half[:, :], ALU.pow).then_inc(s["rstd2"], 1)

            def group(i, back, more):
                for f in range(NF):
                    pool.wait_ge(s["hhi"], NF * i + f + 1)
                    nc.gpsimd.tensor_tensor(hl[:, f % 2, :], r[:, f % 2, :], hh[:, f % 2, :].bitcast(F32), ALU.subtract).then_inc(s["hlo"], 1)
                    if back and f == F_STATS:
                        exponent2(i - 1)
                    if more and f == F_NEXT:
                        exponent(i + 1)

            exponent(0)
            group(0, False, True)
            group(1, True, True)
            with pool.Fori(2, NG - 1) as i:
                group(i, True, True)
            group(NG - 1, True, False)
            exponent2(NG - 1)

        @block.scalar
        def _(act):
            for n in range(WCH):
                act.wait_ge(s["w"], 16 * n + 16)
                out = wfh[:, n, :] if n < C else wph[:, 4 * (n - C):4 * (n - C) + 4, :].rearrange("p q d -> p (q d)")
                nc.scalar.activation(out, stage[n % 2][:, :, :].rearrange("p q d -> p (q d)"), ACT.Copy).then_inc(s["wh"], 1)

            def back_squares(k):
                for t in range(NT):
                    act.wait_ge(s["xn2"], NT * k + t + 1)
                    wait(act, s["sq"], NT * k + t)
                    nc.scalar.activation(lead[:, :], y[:, t, :], ACT.Square, accum_out=sq[:, t:t + 1]).then_inc(s["sq"], 1)

            def back_hi(k, c):
                act.wait_ge(s["back"], BACKS * k + c + 1)
                nc.scalar.activation(bTh[:, c % 2, :], pB[:, :], ACT.Copy).then_inc(s["bhi"], 1)

            def back_root(k):
                act.wait_ge(s["dclip"], k + 1)
                nc.scalar.activation(dist[:, :], dist[:, :], ACT.Sqrt).then_inc(s["dsqrt"], 1)

            def turns(i):
                for c in range(C):
                    act.wait_ge(s["turn"], TURNS * i + c + 1)
                    nc.scalar.activation(xTh[:, c, :], pH[c % 2][:, :], ACT.Copy).then_inc(s["hi"], 1)

            def group(i, back, more):
                for f in range(NF):
                    act.wait_ge(s["turn"], TURNS * i + C + f + 1)
                    wait(act, s["hlo"], NF * i + f - 1)
                    nc.scalar.activation(r[:, f % 2, :], pH[f % 2][:, :], ACT.Relu).then_inc(s["relued"], 1)
                    act.wait_ge(s["squared"], NF * i + f + 1)
                    nc.scalar.activation(hh[:, f % 2, :], r[:, f % 2, :], ACT.Copy).then_inc(s["hhi"], 1)
                    if back and f == F_BACK:
                        back_squares(i - 1)
                    if back and F_BACK < f <= F_BACK + C:
                        back_hi(i - 1, f - F_BACK - 1)
                if more:
                    turns(i + 1)
                act.wait_ge(s["y"], i + 1)
                for t in range(NT):
                    nc.scalar.activation(y[:, t, :], pY[:, t, :], ACT.Copy).then_inc(s["ycopied"], 1)
                if back:
                    back_root(i - 1)

            turns(0)
            group(0, False, True)
            group(1, True, True)
            with act.Fori(2, NG - 1) as i:
                group(i, True, True)
            group(NG - 1, True, False)
            back_squares(NG - 1)
            for c in range(C):
                back_hi(NG - 1, c)
            back_root(NG - 1)

        @block.vector
        def _(dve):
            for n in range(WCH):
                dve.wait_ge(s["wh"], n + 1)
                h, l = ((w[:, n, :] if n < C else w[:, 4 * (n - C):4 * (n - C) + 4, :].rearrange("p q d -> p (q d)"))
                        for w in ((wfh, wfl) if n < C else (wph, wpl)))
                nc.vector.tensor_tensor(l, stage[n % 2][:, :, :].rearrange("p q d -> p (q d)"), h.bitcast(F32), ALU.subtract).then_inc(s["wl"], 1)

            def norm_stats(i):
                dve.wait_ge(s["x"], 16 * i + 16)
                for t in range(NT):
                    nc.vector.bn_stats(stats[:, t, :], x[:, t, :]).then_inc(s["stat"], 1)
                dve.wait_ge(s["stat"], NT * i + NT)
                nc.vector.memset(pause[:, :], 0.0)
                for t in range(NT):
                    nc.vector.bn_aggr(mv[:, t, :], stats[:, t, :]).then_inc(s["aggr"], 1)
                dve.wait_ge(s["aggr"], NT * i + NT)
                nc.vector.tensor_scalar(ve[:, :], mv[:, :, 1], LN_EPS, None, ALU.add).then_inc(s["var"], 1)

            def normalise(i):
                dve.wait_ge(s["rstd"], i + 1)
                for t in range(NT):
                    nc.vector.tensor_scalar(x[:, t, :], x[:, t, :], mv[:, t, 0:1], rstd[:, t:t + 1],
                                            ALU.subtract, ALU.mult).then_inc(s["xn"], 1)

            def spikes(k, t, part):
                n = (NT * k + t) * LIF
                if part == 0:
                    dve.wait_ge(s["ycopied"], NT * (k + 1))
                    wait(dve, s["x2"], NT * k + t)
                    nc.vector.tensor_scalar(count[:, :], y[:, t, :], THRESHOLD, None, ALU.is_gt).then_inc(s["lif"], 1)
                for q in {0: (0,), 1: (1, 2), 2: (3,)}[part]:
                    m = n + 1 + 3 * q
                    old = y[:, t, :] if q == 0 else mem[:, :]
                    if q:
                        dve.wait_ge(s["lif"], m - 1)
                    nc.vector.scalar_tensor_tensor(lead[:, :], old, BETA, y[:, t, :], ALU.mult, ALU.add).then_inc(s["lif"], 1)
                    dve.wait_ge(s["lif"], m + 1)
                    nc.vector.scalar_tensor_tensor(mem[:, :], old, THRESHOLD, lead[:, :], ALU.is_gt, ALU.subtract,
                                                   reverse1=True).then_inc(s["lif"], 1)
                    dve.wait_ge(s["lif"], m + 2)
                    nc.vector.scalar_tensor_tensor(count[:, :], mem[:, :], THRESHOLD, count[:, :], ALU.is_gt, ALU.add).then_inc(s["lif"], 1)
                if part == 2:
                    if t == 0:
                        dve.wait_ge(s["xp"], 16 * (k + 1))
                    dve.wait_ge(s["lif"], n + LIF)
                    nc.vector.scalar_tensor_tensor(xp[:, t, :], count[:, :], 1.0 / STEPS, xp[:, t, :], ALU.mult, ALU.add).then_inc(s["x2"], 1)

            def back_stats(k):
                for t in range(NT):
                    dve.wait_ge(s["x2"], NT * k + t + 1)
                    nc.vector.bn_stats(stats2[:, t, :], xp[:, t, :]).then_inc(s["stat2"], 1)
                dve.wait_ge(s["stat2"], NT * k + NT)
                nc.vector.memset(pause[:, :], 0.0)
                for t in range(NT):
                    nc.vector.bn_aggr(mv2[:, t, :], stats2[:, t, :]).then_inc(s["aggr2"], 1)
                dve.wait_ge(s["aggr2"], NT * k + NT)
                nc.vector.tensor_scalar(ve2[:, :], mv2[:, :, 1], LN_EPS, None, ALU.add).then_inc(s["var2"], 1)

            def back_normalise(k):
                dve.wait_ge(s["rstd2"], k + 1)
                for t in range(NT):
                    nc.vector.tensor_scalar(y[:, t, :], xp[:, t, :], mv2[:, t, 0:1], rstd2[:, t:t + 1],
                                            ALU.subtract, ALU.mult).then_inc(s["xn2"], 1)

            def back_lo(k, c):
                dve.wait_ge(s["bhi"], C * k + c + 1)
                nc.vector.tensor_tensor(bTl[:, c % 2, :], pB[:, :], bTh[:, c % 2, :].bitcast(F32), ALU.subtract).then_inc(s["blo"], 1)

            def back_row(k):
                dve.wait_ge(s["back"], BACKS * k + BACKS)
                nc.vector.tensor_copy(bb[:, :], pB[0:1, :]).then_inc(s["bb"], 1)

            def back_distance(k):
                dve.wait_ge(s["dist"], k + 1)
                wait(dve, s["dstore"], 16 * k)
                nc.vector.tensor_scalar(dist[:, :], pD[0:S, :], aa[:, :], 0.0, ALU.add, ALU.max).then_inc(s["dclip"], 1)

            def turn(i, c):
                dve.wait_ge(s["hi"], C * i + c + 1)
                nc.vector.tensor_tensor(xTl[:, c, :], pH[c % 2][:, :], xTh[:, c, :].bitcast(F32), ALU.subtract).then_inc(s["lo"], 1)

            def group(i, back, more):
                for f in range(NF):
                    dve.wait_ge(s["relued"], NF * i + f + 1)
                    nc.vector.scalar_tensor_tensor(r[:, f % 2, :], pH[f % 2][:, :], 0.0, r[:, f % 2, :], ALU.max, ALU.mult).then_inc(s["squared"], 1)
                    if back and f < F_STATS:
                        for n in range(3 * NT * f // F_STATS, 3 * NT * (f + 1) // F_STATS):
                            spikes(i - 1, n // 3, n % 3)
                    if back and f == F_STATS:
                        back_stats(i - 1)
                    if back and f == F_STATS + 1:
                        back_normalise(i - 1)
                    if more and f == F_NEXT:
                        norm_stats(i + 1)
                    if more and f == F_NEXT + 1:
                        normalise(i + 1)
                    if back and F_BACK < f <= F_BACK + C:
                        back_lo(i - 1, f - F_BACK - 1)
                for c in range(C):
                    if back and c == C - 1:
                        back_row(i - 1)
                    if more:
                        turn(i + 1, c)
                if back:
                    back_distance(i - 1)

            norm_stats(0)
            normalise(0)
            for c in range(C):
                turn(0, c)
            group(0, False, True)
            group(1, True, True)
            with dve.Fori(2, NG - 1) as i:
                group(i, True, True)
            group(NG - 1, True, False)
            for t in range(NT):
                for part in range(3):
                    spikes(NG - 1, t, part)
            back_stats(NG - 1)
            back_normalise(NG - 1)
            for c in range(C):
                back_lo(NG - 1, c)
            back_row(NG - 1)
            back_distance(NG - 1)

        @block.tensor
        def _(pe):
            pe.wait_ge(s["ident"], 4)
            pe.wait_ge(s["wl"], WCH)

            def three(out, xh, xl, yh, yl, first, last):
                nc.tensor.matmul(out, xh, yh, start=first, stop=False)
                nc.tensor.matmul(out, xh, yl, start=False, stop=False)
                return nc.tensor.matmul(out, xl, yh, start=False, stop=last)

            def hidden(i, f):
                if f > 1:
                    pe.wait_ge(s["squared"], NF * i + f - 1)
                w = slice(f * P, (f + 1) * P)
                for c in range(C):
                    last = three(pH[f % 2][:, :], wfh[:, c, w], wfl[:, c, w], xTh[:, c, :], xTl[:, c, :], c == 0, c == C - 1)
                last.then_inc(s["turn"], 1)

            def project(i, f, tiles=range(NT)):
                pe.wait_ge(s["hlo"], NF * i + f + 1)
                if f == 0:
                    wait(pe, s["ycopied"], NT * i)
                for t in tiles:
                    q = slice(t * P, (t + 1) * P)
                    last = three(pY[:, t, :], hh[:, f % 2, q], hl[:, f % 2, q], wph[:, f, :], wpl[:, f, :], f == 0, f == NF - 1)
                if f == NF - 1 and t == NT - 1:
                    last.then_inc(s["y"], 1)

            def back_turn(k, c):
                pe.wait_ge(s["xn2"], NT * (k + 1))
                if c:
                    pe.wait_ge(s["blo"], C * k + c)
                else:
                    wait(pe, s["bb"], k)
                for t in range(NT):
                    last = nc.tensor.transpose(pB[:, t * P:(t + 1) * P], y[:, t, c * P:(c + 1) * P], ident[:, :])
                last.then_inc(s["back"], 1)

            def back_dist(k, c):
                pe.wait_ge(s["blo"], C * k + c + 1)
                if c == 0:
                    pe.wait_ge(s["ctx"], 48 * (k + 1))
                    wait(pe, s["dclip"], k)
                three(pD[0:S, :], ch[:, c, :], cl[:, c, :], bTh[:, c % 2, :], bTl[:, c % 2, :], c == 0, False)

            def back_row(k):
                pe.wait_ge(s["sq"], NT * (k + 1))
                pe.wait_ge(s["blo"], C * (k + 1))
                for t in range(NT):
                    last = nc.tensor.matmul(pB[0:1, t * P:(t + 1) * P], sq[:, t:t + 1], ident[:, :], start=True, stop=True)
                last.then_inc(s["back"], 1)

            def back_finish(k):
                pe.wait_ge(s["bb"], k + 1)
                nc.tensor.matmul(pD[0:S, :], ones[:, :], bb[:, :], start=False, stop=True).then_inc(s["dist"], 1)

            def turn(i, c):
                if c == 0:
                    pe.wait_ge(s["xn"], NT * (i + 1))
                if c < 2:
                    wait(pe, s["squared"], NF * i - 1 + c)
                else:
                    pe.wait_ge(s["lo"], C * i + c - 1)
                for t in range(NT):
                    last = nc.tensor.transpose(pH[c % 2][:, t * P:(t + 1) * P], x[:, t, c * P:(c + 1) * P], ident[:, :])
                last.then_inc(s["turn"], 1)

            def group(i, back, more):
                pe.wait_ge(s["lo"], C * i + C)
                hidden(i, 0)
                hidden(i, 1)
                for f in range(NF):
                    if f < NF - 1:
                        project(i, f)
                    if f + 2 < NF:
                        hidden(i, f + 2)
                    if back and F_BACK < f <= F_BACK + C:
                        back_dist(i - 1, f - F_BACK - 1)
                    if back and F_BACK <= f < F_BACK + C:
                        back_turn(i - 1, f - F_BACK)
                    if more and f == NF - 3:
                        turn(i + 1, 0)
                    if more and f == NF - 2:
                        turn(i + 1, 1)
                        turn(i + 1, 2)
                    if back and f == NF - 2:
                        back_row(i - 1)
                project(i, NF - 1, range(0, NT // 2))
                if more:
                    turn(i + 1, C - 1)
                if back:
                    back_finish(i - 1)
                project(i, NF - 1, range(NT // 2, NT))

            for c in range(C):
                turn(0, c)
            group(0, False, True)
            group(1, True, True)
            with pe.Fori(2, NG - 1) as i:
                group(i, True, True)
            group(NG - 1, True, False)
            for c in range(C):
                back_turn(NG - 1, c)
                back_dist(NG - 1, c)
            back_row(NG - 1)
            back_finish(NG - 1)


def align(nc, a, d):
    with ExitStack() as ctx:
        sb, ps, sem = place(nc, ctx)
        D = sb("d_D", [P, SLOTS, W + 1])
        R = sb("d_R", [P, SLOTS + 1, W + 1])
        M = sb("d_M", [P, SLOTS, W + 1])
        le = sb("d_le", [P, SLOTS, W], BF16)
        left = sb("d_left", [P, SLOTS, W + 1], BF16)
        diag = sb("d_diag", [P, SLOTS, W + 1], BF16)
        up = sb("d_up", [P, SLOTS, W], BF16)
        edge = sb("d_edge", [P, 2, SLOTS], BF16)
        on = sb("d_on", [P, SLOTS + 1, W + 1])
        inner = sb("d_inner", [P, 1])
        viaD = sb("d_viaD", [P, W])
        viaU = sb("d_viaU", [P, W])
        enter = sb("d_enter", [P, W])
        names = "D init R best edge flags inner on0 sh pr en on out".split()
        s = {n: sem(f"d_{n}_s") for n in names}
        block = ctx.enter_context(nc.Block())
        from_left = [(p - 1) % 32 for p in range(32)]
        from_right = [(p + 1) % 32 for p in range(32)]

        @block.sync
        def _(sp):
            for b in range(B):
                sp.dma_start(D[b * NB:(b + 1) * NB, :, 1:W + 1],
                             bass.AP(tensor=d["dist"].tensor, offset=b * SKEW_BATCH,
                                     ap=[[SLOTS * W, NB], [W, SLOTS], [1, W]])).then_inc(s["D"], 16)
            sp.wait_ge(s["on"], SLOTS)
            for b in range(B):
                sp.dma_start(bass.AP(tensor=d["on"].tensor, offset=b * SKEW_BATCH,
                                     ap=[[SLOTS * W, NB], [W, SLOTS], [1, W]]),
                             on[b * NB:(b + 1) * NB, 0:SLOTS, 0:W]).then_inc(s["out"], 16)
            sp.wait_ge(s["out"], 16 * B)

        @block.gpsimd
        def _(pool):
            nc.gpsimd.memset(inner[:, :], 1.0).then_inc(s["inner"], 1)
            nc.gpsimd.memset(enter[:, :], 0.0).then_inc(s["inner"], 1)
            for b in range(B):
                pool.wait_ge(s["inner"], 2 * b + 2)
                last = (b + 1) * NB - 1
                nc.gpsimd.affine_select(out=inner[:, :], in_=inner[:, :], compare_op=ALU.not_equal, fill=0.0,
                                        base=-last, pattern=[[0, 1]], channel_multiplier=1).then_inc(s["inner"], 1)
                nc.gpsimd.affine_select(out=enter[:, :], in_=enter[:, :], compare_op=ALU.not_equal, fill=1.0,
                                        base=-(last * W + W - 1), pattern=[[1, W]], channel_multiplier=W).then_inc(s["inner"], 1)

        @block.vector
        def _(dve):
            nc.vector.memset(R[:, 0, :], BIG).then_inc(s["init"], 1)
            nc.vector.memset(D[:, :, 0:1], 0.0).then_inc(s["init"], 1)
            dve.wait_ge(s["init"], 2)
            for b in range(B):
                nc.vector.memset(R[b * NB:b * NB + 1, 0, 0:1], 0.0).then_inc(s["init"], 1)
                nc.vector.memset(D[b * NB:b * NB + 1, :, 0:1], BIG).then_inc(s["init"], 1)
            dve.wait_ge(s["init"], 2 + 2 * B)
            dve.wait_ge(s["D"], 16 * B)
            for t in range(SLOTS):
                if t:
                    dve.wait_ge(s["R"], t)
                nc.vector.stream_shuffle(M[:, t, 0:1], R[:, t, W:W + 1], from_left).then_inc(s["best"], 1)
                nc.vector.tensor_tensor(M[:, t, 1:W + 1], R[:, t, 1:W + 1], R[:, t, 0:W], ALU.min).then_inc(s["best"], 1)
                dve.wait_ge(s["best"], 2 * t + 2)
                nc.vector.tensor_tensor_scan(R[:, t + 1, :], M[:, t, :], D[:, t, :], BIG, ALU.min, ALU.add).then_inc(s["R"], 1)
            dve.wait_ge(s["R"], SLOTS)

            nc.vector.tensor_tensor(le[:, :, :], R[:, 0:SLOTS, 0:W], R[:, 0:SLOTS, 1:W + 1], ALU.is_le).then_inc(s["flags"], 1)
            nc.vector.tensor_tensor(left[:, :, 0:W], R[:, 1:SLOTS + 1, 0:W], M[:, :, 1:W + 1], ALU.is_lt).then_inc(s["flags"], 1)
            dve.wait_ge(s["flags"], 2)
            nc.vector.scalar_tensor_tensor(diag[:, :, 0:W], left[:, :, 0:W], 0.5, le[:, :, :], ALU.is_lt, ALU.mult).then_inc(s["flags"], 1)
            dve.wait_ge(s["flags"], 3)
            nc.vector.tensor_tensor(up[:, :, :], diag[:, :, 0:W], left[:, :, 0:W], ALU.add).then_inc(s["flags"], 1)
            dve.wait_ge(s["flags"], 4)
            nc.vector.tensor_scalar(up[:, :, :], up[:, :, :], 0.5, None, ALU.is_lt).then_inc(s["flags"], 1)
            for n, flag in enumerate((left, diag)):
                nc.vector.stream_shuffle(edge[:, n, :], flag[:, :, 0], from_right).then_inc(s["edge"], 1)
            dve.wait_ge(s["edge"], 2)
            dve.wait_ge(s["inner"], 2 + 2 * B)
            for n, flag in enumerate((left, diag)):
                nc.vector.memset(flag[:, SLOTS - 1, W:W + 1], 0.0).then_inc(s["flags"], 1)
                nc.vector.tensor_scalar(flag[:, 0:SLOTS - 1, W], edge[:, n, 1:SLOTS], inner[:, 0:1], None, ALU.mult).then_inc(s["flags"], 1)
            nc.vector.memset(on[:, SLOTS, :], 0.0).then_inc(s["on0"], 1)
            dve.wait_ge(s["flags"], 9)
            dve.wait_ge(s["on0"], 1)

            for n in range(SLOTS):
                t = SLOTS - 1 - n
                if n:
                    dve.wait_ge(s["on"], n)
                    nc.vector.stream_shuffle(on[:, t, W:W + 1], on[:, t + 1, 0:1], from_right).then_inc(s["sh"], 1)
                    nc.vector.tensor_tensor(viaD[:, :], on[:, t + 1, 1:W + 1], diag[:, t + 1, 1:W + 1], ALU.mult).then_inc(s["pr"], 1)
                    nc.vector.tensor_tensor(viaU[:, :], on[:, t + 1, 0:W], up[:, t + 1, :], ALU.mult).then_inc(s["pr"], 1)
                    dve.wait_ge(s["pr"], 2 * n)
                    nc.vector.tensor_tensor(enter[:, :], viaD[:, :], viaU[:, :], ALU.add).then_inc(s["en"], 1)
                    dve.wait_ge(s["en"], n)
                else:
                    nc.vector.memset(on[:, t, W:W + 1], 0.0).then_inc(s["sh"], 1)
                dve.wait_ge(s["sh"], n + 1)
                nc.vector.tensor_tensor_scan(on[:, t, W - 1::-1], left[:, t, W:0:-1], enter[:, ::-1], on[:, t, W:W + 1],
                                             ALU.mult, ALU.add).then_inc(s["on"], 1)


def mixing(nc, a, d, out):
    with ExitStack() as ctx:
        sb, ps, sem = place(nc, ctx)
        ident = sb("m_ident", [P, P])
        half = sb("m_half", [P, NT])
        w = {k: [sb(f"m_{k}{n}", [P, C, DM], F32R) for n in "hl"] for k in ("r", "k", "v")}
        mu = sb("m_mu", [P, 2, C])
        nu = sb("m_nu", [P, 2, C])
        inside = sb("m_inside", [P, NG])
        x3 = sb("m_x3", [P, 2, NT, DM])
        path = sb("m_path", [S, G], F32R)
        ch, cl = (sb(f"m_c{n}", [S, DM], F32R) for n in "hl")
        xn = sb("m_xn", [P, NT, DM])
        stats = sb("m_stats", [P, NT, 6])
        pause = sb("m_pause", [P, 1])
        mv = sb("m_mv", [P, NT, 2])
        ve = sb("m_ve", [P, NT])
        rstd = sb("m_rstd", [P, NT])
        xT = sb("m_xT", [P, C, G + 1])
        part = sb("m_part", [P, 2, G])
        mix = sb("m_mix", [P, 2, G])
        zh, zl = (sb(f"m_z{n}", [P, 2, 2, C, G], F32R) for n in "hl")
        r = sb("m_relu", [P, 2, G])
        hh, hl = (sb(f"m_h{n}", [P, C, G], F32R) for n in "hl")
        gate = sb("m_gate", [P, NT, DM])
        res = sb("m_res", [P, 2, DM])
        pE = [ps(f"m_pE{n}") for n in range(2)]
        pT = [ps(f"m_pT{n}") for n in range(2)]
        pK = [ps(f"m_pK{n}") for n in range(2)]
        pR = [ps(f"m_pR{n}") for n in range(2)]
        names = ("ident w wh wl mu nu path ctx exp x3 stat aggr var rstd xn turn first xT part mix zhi zlo "
                 "R gate K relued squared hhi hlo V gated res").split()
        s = {n: sem(f"m_{n}_s") for n in names}
        s_store, s_x2 = ([sem(f"m_{name}{n}_s") for n in range(2)] for name in ("store", "x2"))
        block = ctx.enter_context(nc.Block())
        stage = [x3[:, 0, :, :], x3[:, 1, :, :], xn[:, :, :]]

        @block.sync
        def _(sp):
            sp.dma_start(mu[:, 0, :], a["mu_r"]).then_inc(s["mu"], 16)
            sp.dma_start(mu[:, 1, :], a["mu_k"]).then_inc(s["mu"], 16)
            for n, k in enumerate(("WrT", "WkkT", "WvvT")):
                if n:
                    sp.wait_ge(s["w"], 16 * n)
                sp.dma_start(stage[n], a[k].rearrange("(c p) d -> p c d", p=P)).then_inc(s["w"], 16)

            def load_x2(j, side, t):
                first = start(sp, j * (G * DM) + t * P * DM)
                sp.dma_start(x3[:, side, t, :], rows(d["x2"], first, 1)).then_inc(s_x2[side], 16)

            def load_path(j):
                batch, block_ = start(sp, (j // GB) * (S * DM)), skew_start(sp, j)
                wait(sp, s["exp"], NT * j)
                sp.dma_start(path[:, :].bitcast(F32).rearrange("s (c w) -> s c w", w=W), skewed(d["on"], block_)).then_inc(s["path"], 16)
                sp.dma_start(ch[:, :].bitcast(F32), bass.AP(tensor=d["ch"].tensor, offset=batch, ap=[[DM, S], [1, DM]])).then_inc(s["ctx"], 16)
                sp.dma_start(cl[:, :].bitcast(F32), bass.AP(tensor=d["cl"].tensor, offset=batch, ap=[[DM, S], [1, DM]])).then_inc(s["ctx"], 16)

            def group(i, side, ahead=True):
                for t in range(NT):
                    first = start(sp, i * (G * DM) + t * P * DM)
                    sp.wait_ge(s["res"], NT * i + t + 1)
                    sp.dma_start(rows(out, first, 1), res[:, t % 2, :]).then_inc(s_store[t % 2], 16)
                    if ahead:
                        load_x2(i + 2, side, t)
                        if t == 1:
                            load_path(i + 2)

            sp.wait_ge(s["wl"], 1)
            for t in range(NT):
                load_x2(0, 0, t)
            load_path(0)
            sp.wait_ge(s["wl"], 2)
            for t in range(NT):
                load_x2(1, 1, t)
            load_path(1)
            group(0, 0)
            with sp.Fori(0, NG // 2 - 2) as k:
                group(k * 2 + 1, 1)
                group(k * 2 + 2, 0)
            group(NG - 3, 1)
            group(NG - 2, 0, False)
            group(NG - 1, 1, False)
            for n in range(2):
                sp.wait_ge(s_store[n], 16 * NG * NT // 2)

        @block.gpsimd
        def _(pool):
            identity(nc, pool, ident, s["ident"])
            nc.gpsimd.memset(half[:, :], -0.5).then_inc(s["ident"], 1)
            nc.gpsimd.memset(inside[:, :], 1.0).then_inc(s["ident"], 1)
            pool.wait_ge(s["ident"], 4)
            nc.gpsimd.memset(inside[:, ::GB], 0.0).then_inc(s["ident"], 1)

            def front(j):
                pool.wait_ge(s["var"], j + 1)
                nc.gpsimd.tensor_tensor(rstd[:, :], ve[:, :], half[:, :], ALU.pow).then_inc(s["rstd"], 1)

            def front_mix(j, side, c):
                for z in range(2):
                    n = 2 * (C * j + c) + z + 1
                    pool.wait_ge(s["zhi"], n)
                    nc.gpsimd.tensor_tensor(zl[:, side, z, c, :], mix[:, z, :], zh[:, side, z, c, :].bitcast(F32), ALU.subtract).then_inc(s["zlo"], 1)

            def group(i, side, more):
                for m in range(C):
                    if more and m == 2:
                        front(i + 1)
                    pool.wait_ge(s["hhi"], C * i + m + 1)
                    nc.gpsimd.tensor_tensor(hl[:, m, :], r[:, m % 2, :], hh[:, m, :].bitcast(F32), ALU.subtract).then_inc(s["hlo"], 1)
                if more:
                    for c in range(C):
                        front_mix(i + 1, 1 - side, c)

            front(0)
            for c in range(C):
                front_mix(0, 0, c)
            group(0, 0, True)
            with pool.Fori(0, NG // 2 - 1) as k:
                group(k * 2 + 1, 1, True)
                group(k * 2 + 2, 0, True)
            group(NG - 1, 1, False)

        @block.scalar
        def _(act):
            for n, k in enumerate("rkv"):
                act.wait_ge(s["w"], 16 * n + 16)
                nc.scalar.activation(w[k][0][:, :, :], stage[n], ACT.Copy).then_inc(s["wh"], 1)
            act.wait_ge(s["mu"], 32)

            def front_turn(j, c):
                act.wait_ge(s["turn"], C * j + c + 1)
                if c == 0:
                    act.wait_ge(s["first"], j + 1)
                nc.scalar.activation(xT[:, c, 1:G + 1], pT[c % 2][:, :], ACT.Copy).then_inc(s["xT"], 1)
                act.wait_ge(s["xT"], C * j + c + 1)
                for z in range(2):
                    wait(act, s["mix"], 2 * (C * j + c) + z - 1)
                    nc.scalar.activation(part[:, z, :], xT[:, c, 1:G + 1], ACT.Copy, scale=mu[:, z, c:c + 1]).then_inc(s["part"], 1)

            def front_hi(j, side, c):
                for z in range(2):
                    act.wait_ge(s["mix"], 2 * (C * j + c) + z + 1)
                    nc.scalar.activation(zh[:, side, z, c, :], mix[:, z, :], ACT.Copy).then_inc(s["zhi"], 1)

            def group(i, side, more):
                for m in range(C):
                    act.wait_ge(s["K"], C * i + m + 1)
                    wait(act, s["hlo"], C * i + m - 1)
                    nc.scalar.activation(r[:, m % 2, :], pK[m % 2][:, :], ACT.Relu).then_inc(s["relued"], 1)
                    act.wait_ge(s["squared"], C * i + m + 1)
                    nc.scalar.activation(hh[:, m, :], r[:, m % 2, :], ACT.Copy).then_inc(s["hhi"], 1)
                for t in range(NT):
                    act.wait_ge(s["R"], NT * i + t + 1)
                    nc.scalar.activation(gate[:, t, :], pR[t % 2][:, :], ACT.Sigmoid).then_inc(s["gate"], 1)
                    if more:
                        if t:
                            front_hi(i + 1, 1 - side, t - 1)
                        front_turn(i + 1, t)
                if more:
                    front_hi(i + 1, 1 - side, C - 1)

            for c in range(C):
                front_turn(0, c)
                front_hi(0, 0, c)
            group(0, 0, True)
            with act.Fori(0, NG // 2 - 1) as k:
                group(k * 2 + 1, 1, True)
                group(k * 2 + 2, 0, True)
            group(NG - 1, 1, False)

        @block.vector
        def _(dve):
            for n, k in enumerate("rkv"):
                dve.wait_ge(s["wh"], n + 1)
                nc.vector.tensor_tensor(w[k][1][:, :, :], stage[n], w[k][0][:, :, :].bitcast(F32), ALU.subtract).then_inc(s["wl"], 1)
            dve.wait_ge(s["mu"], 32)
            nc.vector.tensor_scalar(nu[:, :, :], mu[:, :, :], -1.0, 1.0, ALU.mult, ALU.add).then_inc(s["nu"], 1)
            dve.wait_ge(s["nu"], 1)

            def front_x3(j, side, pair, t):
                if t == 0:
                    dve.wait_ge(s_x2[side], 16 * NT * (pair + 1))
                dve.wait_ge(s["exp"], NT * j + t + 1)
                nc.vector.tensor_tensor(x3[:, side, t, :], pE[t % 2][:, :], x3[:, side, t, :], ALU.add).then_inc(s["x3"], 1)
                dve.wait_ge(s["x3"], NT * j + t + 1)
                nc.vector.bn_stats(stats[:, t, :], x3[:, side, t, :]).then_inc(s["stat"], 1)

            def front_norm(j, side):
                dve.wait_ge(s["stat"], NT * j + NT)
                nc.vector.memset(pause[:, :], 0.0)
                for t in range(NT):
                    nc.vector.bn_aggr(mv[:, t, :], stats[:, t, :]).then_inc(s["aggr"], 1)
                dve.wait_ge(s["aggr"], NT * j + NT)
                nc.vector.tensor_scalar(ve[:, :], mv[:, :, 1], LN_EPS, None, ALU.add).then_inc(s["var"], 1)
                dve.wait_ge(s["rstd"], j + 1)
                for t in range(NT):
                    nc.vector.tensor_scalar(xn[:, t, :], x3[:, side, t, :], mv[:, t, 0:1], rstd[:, t:t + 1],
                                            ALU.subtract, ALU.mult).then_inc(s["xn"], 1)
                if isinstance(j, int) and j == 0:
                    nc.vector.memset(xT[:, :, 0:1], 0.0).then_inc(s["first"], 1)
                else:
                    nc.vector.tensor_scalar(xT[:, :, 0:1], xT[:, :, G:G + 1], inside[:, bass.ds(j, 1)], None, ALU.mult).then_inc(s["first"], 1)

            def front_mix(j, c):
                for z in range(2):
                    n = 2 * (C * j + c) + z
                    dve.wait_ge(s["part"], n + 1)
                    if c == 0:
                        dve.wait_ge(s["first"], j + 1)
                    wait(dve, s["zlo"], n - 1)
                    nc.vector.scalar_tensor_tensor(mix[:, z, :], xT[:, c, 0:G], nu[:, z, c:c + 1], part[:, z, :],
                                                   ALU.mult, ALU.add).then_inc(s["mix"], 1)

            def group(i, side, pair, more):
                for m in range(C):
                    dve.wait_ge(s["relued"], C * i + m + 1)
                    nc.vector.scalar_tensor_tensor(r[:, m % 2, :], pK[m % 2][:, :], 0.0, r[:, m % 2, :], ALU.max, ALU.mult).then_inc(s["squared"], 1)
                    if more and m < 2:
                        front_x3(i + 1, 1 - side, pair + side, 2 * m)
                        front_x3(i + 1, 1 - side, pair + side, 2 * m + 1)
                    if more and m == 2:
                        front_norm(i + 1, 1 - side)
                if more:
                    for c in range(C):
                        front_mix(i + 1, c)
                for t in range(NT):
                    dve.wait_ge(s["V"], NT * i + t + 1)
                    nc.vector.tensor_tensor(gate[:, t, :], pR[t % 2][:, :], gate[:, t, :], ALU.mult).then_inc(s["gated"], 1)
                    dve.wait_ge(s["gated"], NT * i + t + 1)
                    wait(dve, s_store[t % 2], 16 * (NT // 2 * i + t // 2))
                    nc.vector.tensor_tensor(res[:, t % 2, :], gate[:, t, :], x3[:, side, t, :], ALU.add).then_inc(s["res"], 1)

            dve.wait_ge(s["ident"], 5)
            for t in range(NT):
                front_x3(0, 0, 0, t)
            front_norm(0, 0)
            for c in range(C):
                front_mix(0, c)
            group(0, 0, 0, True)
            with dve.Fori(0, NG // 2 - 1) as k:
                group(k * 2 + 1, 1, k, True)
                group(k * 2 + 2, 0, k + 1, True)
            group(NG - 1, 1, NG // 2 - 1, False)

        @block.tensor
        def _(pe):
            pe.wait_ge(s["ident"], 2)
            pe.wait_ge(s["wl"], 3)

            def three(out, xh, xl, yh, yl, first, last):
                nc.tensor.matmul(out, xh, yh, start=first, stop=False)
                nc.tensor.matmul(out, xh, yl, start=False, stop=False)
                return nc.tensor.matmul(out, xl, yh, start=False, stop=last)

            def expand(j, t):
                pe.wait_ge(s["path"], 16 * (j + 1))
                pe.wait_ge(s["ctx"], 32 * (j + 1))
                wait(pe, s["x3"], NT * j + t - 1)
                q = slice(t * P, (t + 1) * P)
                nc.tensor.matmul(pE[t % 2][:, :], path[:, q], ch[:, :], start=True, stop=False)
                nc.tensor.matmul(pE[t % 2][:, :], path[:, q], cl[:, :], start=False, stop=True).then_inc(s["exp"], 1)

            def front_turn(j, c):
                pe.wait_ge(s["xn"], NT * (j + 1))
                wait(pe, s["xT"], C * j + c - 1)
                for t in range(NT):
                    last = nc.tensor.transpose(pT[c % 2][:, t * P:(t + 1) * P], xn[:, t, c * P:(c + 1) * P], ident[:, :])
                last.then_inc(s["turn"], 1)

            def gates(i, side, t):
                if t < 2:
                    wait(pe, s["gated"], NT * i)
                else:
                    pe.wait_ge(s["gate"], NT * i + t - 1)
                q = slice(t * P, (t + 1) * P)
                for c in range(C):
                    last = three(pR[t % 2][:, :], zh[:, side, 0, c, q], zl[:, side, 0, c, q], w["r"][0][:, c, :], w["r"][1][:, c, :], c == 0, c == C - 1)
                last.then_inc(s["R"], 1)

            def keys(i, side, m):
                wait(pe, s["squared"], C * i + m - 1)
                e = slice(m * P, (m + 1) * P)
                for c in range(C):
                    last = three(pK[m % 2][:, :], w["k"][0][:, c, e], w["k"][1][:, c, e], zh[:, side, 1, c, :], zl[:, side, 1, c, :], c == 0, c == C - 1)
                last.then_inc(s["K"], 1)

            def values(i, t):
                if t < 2:
                    pe.wait_ge(s["gate"], NT * i + t + 3)
                else:
                    pe.wait_ge(s["gated"], NT * i + t - 1)
                pe.wait_ge(s["hlo"], C * (i + 1))
                q = slice(t * P, (t + 1) * P)
                for m in range(C):
                    last = three(pR[t % 2][:, :], hh[:, m, q], hl[:, m, q], w["v"][0][:, m, :], w["v"][1][:, m, :], m == 0, m == C - 1)
                last.then_inc(s["V"], 1)

            def group(i, side, more):
                pe.wait_ge(s["zlo"], 2 * C * (i + 1))
                for m in range(C):
                    keys(i, side, m)
                    if more and m < 2:
                        expand(i + 1, 2 * m)
                        expand(i + 1, 2 * m + 1)
                for t in range(NT):
                    gates(i, side, t)
                    if more and t < NT - 1:
                        front_turn(i + 1, t)
                for t in range(NT):
                    values(i, t)
                    if more and t == 0:
                        front_turn(i + 1, NT - 1)

            for t in range(NT):
                expand(0, t)
            for c in range(C):
                front_turn(0, c)
            group(0, 0, True)
            with pe.Fori(0, NG // 2 - 1) as k:
                group(k * 2 + 1, 1, True)
                group(k * 2 + 2, 0, True)
            group(NG - 1, 1, False)


INPUTS = {
    "x": ("x", lambda v: v.reshape(B * T, DM)),
    "ctx": ("ctx_1024", lambda v: v),
    "mask": ("mask_Bx1xSxS2_bf1", lambda v: v.reshape(B * T, S)[:, ::-1].view("uint8")),
    "WqT": ("L0_xattn_Wq", lambda v: v.T), "bq": ("L0_xattn_bq", lambda v: v.reshape(C, P).T),
    "WkT": ("L0_xattn_Wk", lambda v: v.T), "bk": ("L0_xattn_bk", lambda v: v.reshape(C, P).T),
    "WvT": ("L0_xattn_Wv", lambda v: v.T), "bv": ("L0_xattn_bv", lambda v: v),
    "WoT": ("L0_xattn_Wo", lambda v: v.T), "bo": ("L0_xattn_bo", lambda v: v),
    "rel": ("L0_xattn_rel_emb", lambda v: v.T),
    "WfcT": ("L0_ffn_W_fc", lambda v: v.T), "WprojT": ("L0_ffn_W_proj", lambda v: v.T),
    "WrT": ("L1_ffn_W_r", lambda v: v.T), "WkkT": ("L1_ffn_W_k", lambda v: v.T), "WvvT": ("L1_ffn_W_v", lambda v: v.T),
    "mu_r": ("L1_ffn_mu_r", lambda v: v.reshape(C, P).T), "mu_k": ("L1_ffn_mu_k", lambda v: v.reshape(C, P).T),
}


def kernel(**inputs):
    import numpy as np
    import concourse.bacc as bacc
    from concourse.bass_utils import run_bass_kernel_spmd

    nc = bacc.Bacc("TRN2", target_bir_lowering=False, num_devices=1)
    arrays, a = {}, {}
    for name, (source, lay_out) in INPUTS.items():
        v = np.ascontiguousarray(lay_out(np.asarray(inputs[source])))
        arrays[f"in_{name}"] = v
        a[name] = nc.dram_tensor(f"in_{name}", v.shape, mybir.dt.from_np(v.dtype), kind="ExternalInput").ap()

    def scratch(name, shape, dt=F32):
        return nc.dram_tensor(f"s_{name}", shape, dt, kind="Internal").ap()

    d = {
        "kh": scratch("kh", (B, P, C, S)), "kl": scratch("kl", (B, P, C, S)),
        "c2h": scratch("c2h", (B, P, C, S)), "c2l": scratch("c2l", (B, P, C, S)),
        "vh": scratch("vh", (B, S, DM)), "vl": scratch("vl", (B, S, DM)),
        "ch": scratch("ch", (B, S, DM)), "cl": scratch("cl", (B, S, DM)),
        "aa": scratch("aa", (B, S, 1)), "rel": scratch("rel", (H, RELW)),
        "dist": scratch("dist", (B, NB, SLOTS * W)), "on": scratch("on", (B, NB, SLOTS * W)),
        "x1": scratch("x1", (B * T, DM)), "x2": scratch("x2", (B * T, DM)),
    }
    out = nc.dram_tensor("out", (B * T, DM), F32, kind="ExternalOutput").ap()
    prepare(nc, a, d)
    attention(nc, a, d)
    spiking(nc, a, d)
    align(nc, a, d)
    mixing(nc, a, d, out)
    r = run_bass_kernel_spmd(nc, [arrays], core_ids=[0])
    return r.results[0]["out"].reshape(B, T, DM)
```

```python
import concourse.bass as bass
from concourse import mybir
from contextlib import ExitStack

F32 = mybir.dt.float32
F32R = mybir.dt.float32r
BF16 = mybir.dt.bfloat16
U8 = mybir.dt.uint8
ALU = mybir.AluOpType
ACT = mybir.ActivationFunctionType
AX = mybir.AxisListType.X

P = 128
B, T, DM = 4, 2048, 512
S = 77
H, DH = 16, 32
HP = P // DH
C = DM // P
FF = 2048
NF = FF // P
G = 512
NT = G // P
NG = B * T // G
GB = T // G
MAX_REL = 1023
SCALE = DH ** -0.5
LN_EPS = 1e-5
BETA, THRESHOLD, STEPS = 0.9, 1.0, 5
BIG = 1e30
PAD = T - 1 - MAX_REL
RELW = PAD + 2 * MAX_REL + 1

W = 64
NB = T // W
SLOTS = S + NB - 1
SKEW_ROW, SKEW_BLOCK, SKEW_BATCH = W, (SLOTS + 1) * W, NB * SLOTS * W
GBLK = G // W


def wait(eng, sem, value):
    if not isinstance(value, int) or value > 0:
        eng.wait_ge(sem, value)


def start(eng, offset):
    return offset if isinstance(offset, int) else eng.snap(offset)


def rows(dram, first, tiles=NT, width=DM):
    tile = [[P * width, tiles]] if tiles > 1 else []
    return bass.AP(tensor=dram.tensor, offset=first, ap=[[width, P]] + tile + [[1, width]])


def skew_start(eng, group):
    return start(eng, (group // GB) * SKEW_BATCH + (group % GB) * (GBLK * SKEW_BLOCK))


def skewed(scratch, first):
    return bass.AP(tensor=scratch.tensor, offset=first,
                   ap=[[SKEW_ROW, S], [SKEW_BLOCK, GBLK], [1, W]])


def place(nc, ctx):
    def sb(name, shape, dt=F32):
        return ctx.enter_context(nc.sbuf_tensor(name, shape, dt))

    def ps(name, shape=(P, 512)):
        return ctx.enter_context(nc.psum_tensor(name, list(shape), F32))

    def sem(name):
        return ctx.enter_context(nc.semaphore(name))

    return sb, ps, sem


def identity(nc, eng, ident, s_ident):
    nc.gpsimd.memset(ident[:, :], 0.0).then_inc(s_ident, 1)
    eng.wait_ge(s_ident, 1)
    nc.gpsimd.affine_select(out=ident[:, :], in_=ident[:, :], compare_op=ALU.not_equal, fill=1.0,
                            base=0, pattern=[[-1, P]], channel_multiplier=1).then_inc(s_ident, 1)


def prepare(nc, a, d, w):
    with ExitStack() as ctx:
        sb, ps, sem = place(nc, ctx)
        ident = sb("p_ident", [P, P])
        wk = sb("p_wk", [P, C, DM])
        wv = sb("p_wv", [P, C, DM])
        bk = sb("p_bk", [P, C])
        bv = sb("p_bv", [S, DM])
        cx = sb("p_cx", [S, B, DM])
        cxT = sb("p_cxT", [P, B, C, S])
        cxR = sb("p_cxR", [P, C, B, S])
        kf = sb("p_kf", [P, B, C, S])
        kh = sb("p_kh", [P, B, C, S], F32R)
        kl = sb("p_kl", [P, B, C, S], F32R)
        vf = sb("p_vf", [S, B, DM])
        vh = sb("p_vh", [S, B, DM], F32R)
        vl = sb("p_vl", [S, B, DM], F32R)
        c2f = sb("p_c2f", [P, B, C, S])
        c2h = sb("p_c2h", [P, B, C, S], F32R)
        c2l = sb("p_c2l", [P, B, C, S], F32R)
        ch = sb("p_ch", [S, B, DM], F32R)
        cl = sb("p_cl", [S, B, DM], F32R)
        sq = sb("p_sq", [S, DM])
        aa = sb("p_aa", [S, B])
        rel = sb("p_rel", [H, 2 * MAX_REL + 1])
        relp = sb("p_relp", [H, PAD])
        zero = sb("p_zero", [P, SLOTS * W])
        stage = sb("p_stage", [P, 2, C, DM])
        s_stage, s_wh, s_wl = [sem(f"p_stage{n}_s") for n in range(2)], sem("p_wh_s"), sem("p_wl_s")
        pT = [ps(f"p_pT{b}") for b in range(B)]
        pK = [ps(f"p_pK{m}") for m in range(C)]
        s_ident, s_cx, s_w, s_b, s_rel = sem("p_ident_s"), sem("p_cx_s"), sem("p_w_s"), sem("p_b_s"), sem("p_rel_s")
        s_zero, s_relp, s_T, s_cxT, s_K, s_V = (sem("p_zero_s"), sem("p_relp_s"), sem("p_T_s"),
                                               sem("p_cxT_s"), sem("p_K_s"), sem("p_V_s"))
        s_full, s_hi, s_lo, s_aa, s_out = sem("p_full_s"), sem("p_hi_s"), sem("p_lo_s"), sem("p_aa_s"), sem("p_out_s")
        block = ctx.enter_context(nc.Block())

        @block.sync
        def _(sp):
            sp.dma_start(cx[:, :, :], a["ctx"].rearrange("b s d -> s b d")).then_inc(s_cx, 16)
            sp.dma_start(wk[:, :, :], a["WkT"].rearrange("(c p) d -> p c d", p=P)).then_inc(s_w, 16)
            sp.dma_start(wv[:, :, :], a["WvT"].rearrange("(c p) d -> p c d", p=P)).then_inc(s_w, 16)
            sp.dma_start(bk[:, :], a["bk"]).then_inc(s_b, 16)
            sp.dma_start(bv[:, :], a["bv"].partition_broadcast(S)).then_inc(s_b, 16)
            sp.dma_start(rel[:, :], a["rel"]).then_inc(s_rel, 16)
            for n, name in enumerate(("WqT", "WoT")):
                sp.dma_start(stage[:, n, :, :], a[name].rearrange("(c p) d -> p c d", p=P)).then_inc(s_stage[n], 16)
            sp.wait_ge(s_rel, 16)
            sp.dma_start(d["rel"][:, 0:2 * MAX_REL + 1], rel[:, :]).then_inc(s_out, 16)
            sp.wait_ge(s_relp, 1)
            sp.dma_start(d["rel"][:, 2 * MAX_REL + 1:RELW], relp[:, :]).then_inc(s_out, 16)
            sp.wait_ge(s_zero, 1)
            for b in range(B):
                sp.dma_start(bass.AP(tensor=d["dist"].tensor, offset=b * SKEW_BATCH,
                                     ap=[[SLOTS * W, NB], [1, SLOTS * W]]),
                             zero[b * NB:(b + 1) * NB, :]).then_inc(s_out, 16)
            sp.wait_ge(s_aa, B)
            for b in range(B):
                sp.dma_start(d["aa"][b, :, :], aa[:, b:b + 1]).then_inc(s_out, 16)
            for n, (dst, high, low) in enumerate((("c2", c2h, c2l), ("c", ch, cl), ("k", kh, kl), ("v", vh, vl))):
                layout = "b s d -> s b d" if n % 2 else "b p c s -> p b c s"
                sp.wait_ge(s_hi, n + 1)
                sp.dma_start(d[dst + "h"].rearrange(layout), high[:].bitcast(F32)).then_inc(s_out, 16)
                sp.wait_ge(s_lo, n + 1)
                sp.dma_start(d[dst + "l"].rearrange(layout), low[:].bitcast(F32)).then_inc(s_out, 16)
            sp.wait_ge(s_out, 16 * (2 + B + B + 8))

        @block.gpsimd
        def _(pool):
            identity(nc, pool, ident, s_ident)
            nc.gpsimd.memset(zero[:, :], 0.0).then_inc(s_zero, 1)
            pool.wait_ge(s_rel, 16)
            nc.gpsimd.tensor_copy(relp[:, :], rel[:, 2 * MAX_REL:2 * MAX_REL + 1].broadcast_to([H, PAD])).then_inc(s_relp, 1)

        @block.tensor
        def _(pe):
            pe.wait_ge(s_ident, 2)
            pe.wait_ge(s_cx, 16)
            for b in range(B):
                for c in range(C):
                    last = nc.tensor.transpose(pT[b][:, c * S:(c + 1) * S], cx[:, b, c * P:(c + 1) * P],
                                               ident[0:S, 0:S])
                last.then_inc(s_T, 1)
            pe.wait_ge(s_w, 32)
            pe.wait_ge(s_cxT, 2 * B)
            for m in range(C):
                for c in range(C):
                    last = nc.tensor.matmul(pK[m][:, 0:B * S], wk[:, c, m * P:(m + 1) * P],
                                            cxR[:, c, :, :].rearrange("p b s -> p (b s)"), start=c == 0, stop=c == C - 1)
                last.then_inc(s_K, 1)
            for b in range(B):
                for c in range(C):
                    last = nc.tensor.matmul(pT[b][0:S, :], cxR[:, c, b, :], wv[:, c, :],
                                            start=c == 0, stop=c == C - 1)
                last.then_inc(s_V, 1)

        @block.vector
        def _(dve):
            for b in range(B):
                dve.wait_ge(s_T, b + 1)
                nc.vector.tensor_copy(cxT[:, b, :, :], pT[b][:, 0:C * S].rearrange("p (c s) -> p c s", s=S)).then_inc(s_cxT, 1)
                dve.wait_ge(s_cxT, 2 * b + 1)
                nc.vector.tensor_copy(cxR[:, :, b, :], cxT[:, b, :, ::-1]).then_inc(s_cxT, 1)
            def lo(n, full, high, low):
                dve.wait_ge(s_hi, n + 1)
                flat = "p b d -> p (b d)" if n % 2 else "p b c s -> p (b c s)"
                full, high, low = (r[:].rearrange(flat) for r in (full, high, low))
                nc.vector.tensor_tensor(low, full, high.bitcast(F32), ALU.subtract).then_inc(s_lo, 1)

            dve.wait_ge(s_cxT, 2 * B)
            nc.vector.tensor_scalar(c2f[:, :, :, :], cxT[:, :, :, :], -2.0, None, ALU.mult).then_inc(s_full, 1)
            lo(0, c2f, c2h, c2l)
            lo(1, cx, ch, cl)
            dve.wait_ge(s_b, 32)
            for m in range(C):
                dve.wait_ge(s_K, m + 1)
                nc.vector.tensor_scalar(kf[:, :, m, :], pK[m][:, 0:B * S].rearrange("p (b s) -> p b s", s=S), bk[:, m:m + 1], SCALE,
                                        ALU.add, ALU.mult).then_inc(s_full, 1)
            lo(2, kf, kh, kl)
            for n, k in enumerate("qo"):
                dve.wait_ge(s_wh, n + 1)
                nc.vector.tensor_tensor(w[k][1][:, :, :], stage[:, n, :, :], w[k][0][:, :, :].bitcast(F32), ALU.subtract).then_inc(s_wl, 1)
            for b in range(B):
                dve.wait_ge(s_V, b + 1)
                nc.vector.tensor_tensor(vf[:, b, :], pT[b][0:S, :], bv[:, :], ALU.add).then_inc(s_full, 1)
            lo(3, vf, vh, vl)

        @block.scalar
        def _(act):
            act.wait_ge(s_cx, 16)
            for b in range(B):
                if b:
                    act.wait_ge(s_aa, b)
                nc.scalar.activation(sq[:, :], cx[:, b, :], ACT.Square, accum_out=aa[:, b:b + 1]).then_inc(s_aa, 1)
            act.wait_ge(s_full, 1)
            nc.scalar.activation(c2h[:, :, :, :], c2f[:, :, :, :], ACT.Copy).then_inc(s_hi, 1)
            nc.scalar.activation(ch[:, :, :], cx[:, :, :], ACT.Copy).then_inc(s_hi, 1)
            for n, k in enumerate("qo"):
                act.wait_ge(s_stage[n], 16)
                nc.scalar.activation(w[k][0][:, :, :], stage[:, n, :, :], ACT.Copy).then_inc(s_wh, 1)
            act.wait_ge(s_full, 1 + C)
            nc.scalar.activation(kh[:, :, :, :], kf[:, :, :, :], ACT.Copy).then_inc(s_hi, 1)
            act.wait_ge(s_full, 1 + C + B)
            nc.scalar.activation(vh[:, :, :], vf[:, :, :], ACT.Copy).then_inc(s_hi, 1)


def attention(nc, a, d, w):
    with ExitStack() as ctx:
        sb, ps, sem = place(nc, ctx)
        STEPS_JOBS = ("P0 P1 P2 P3 Q", "P0 P1 P2 P3 Q X0 X1", "P0 P1 X2 P2 X3 P3 Q", "P0 P1 P2 P3 Q")
        LAST_JOBS = ("P0 P1 P2 P3 Q", "P0 P1 P2 P3 Q", "P0 P1 P2 P3", "P0 P1 P2 P3")
        FIRST = C + 2
        number = {more: {(m, kind): n for n, (m, kind) in enumerate(
                      (m, kind) for m, line in enumerate(lines) for kind in line.split())}
                  for more, lines in ((True, STEPS_JOBS), (False, LAST_JOBS))}
        JOBS = len(number[True])
        ident = sb("a_ident", [P, P])
        (wqh, wql), (woh, wol) = w["q"], w["o"]
        bq = sb("a_bq", [P, C])
        bo = sb("a_bo", [P, DM])
        half = sb("a_half", [P, NT])
        x = sb("a_x", [P, NT, DM])
        res = sb("a_res", [P, 2, DM])
        stats = sb("a_stats", [P, NT, 6])
        pause = sb("a_pause", [P, 1])
        mv = sb("a_mv", [P, NT, 2])
        ve = sb("a_ve", [P, NT])
        rstd = sb("a_rstd", [P, NT])
        xTh, xTl = (sb(f"a_xT{n}", [P, C, G], F32R) for n in "hl")
        qTh, qTl = (sb(f"a_qT{n}", [P, G], F32R) for n in "hl")
        kbh, kbl = (sb(f"a_kb{n}", [P, 2, C, HP * S], F32R) for n in "hl")
        vh, vl = (sb(f"a_v{n}", [S, 2, C, HP, P], F32R) for n in "hl")
        mask = sb("a_mask", [P, NT, S], U8)
        mneg = sb("a_mneg", [P, NT, S])
        huge = sb("a_huge", [P, 2])
        bias = sb("a_bias", [P, 2, HP, G])
        bm = sb("a_bm", [P, NT, HP, S])
        sc = sb("a_sc", [P, 2, NT, HP, S])
        mx = sb("a_mx", [P, 2, NT, HP])
        rs = sb("a_rs", [P, 2, NT, HP])
        ri = sb("a_ri", [P, 2, NT, HP])
        pTh, pTl = (sb(f"a_pT{n}", [S, HP, G], F32R) for n in "hl")
        oTh, oTl = (sb(f"a_oT{n}", [P, 2, C, G], F32R) for n in "hl")
        pW = [ps(f"a_pW{n}") for n in range(2)]
        pS = ctx.enter_context(nc.psum_tensor("a_pS", [P, NT, 512], F32))
        pV = ps("a_pV")
        pO = ps("a_pO")
        names = ("cleared ident const x stat aggr var rstd xn xb split hi lo mask mneg bm score added maxed "
                 "exped recip normed pv ohi olo wo x1").split()
        s = {n: sem(f"a_{n}_s") for n in names}
        s_kb, s_v, s_bias, s_res, s_store = ([sem(f"a_{name}{n}_s") for n in range(2)]
                                             for name in ("kb", "v", "bias", "res", "store"))
        block = ctx.enter_context(nc.Block())
        def job(i, m, kind, more):
            return JOBS * i + FIRST + number[more][(m, kind)] + 1

        def load_keys(sp, i, side):
            first = start(sp, (i // GB) * (P * C * S))
            at = [start(sp, first + j * DH * C * S) for j in range(HP)]
            for hi_lo, (dst, src) in enumerate(((kbh, d["kh"]), (kbl, d["kl"]))):
                for j in range(HP):
                    r = slice(j * DH, (j + 1) * DH)
                    if j == 0 and hi_lo == 0:
                        wait(sp, s["score"], 2 * C * (i - 1))
                    sp.dma_start(dst[r, side, :, j * S:(j + 1) * S].bitcast(F32),
                                 bass.AP(tensor=src.tensor, offset=at[j], ap=[[C * S, DH], [S, C], [1, S]])).then_inc(s_kb[side], 16)

        def load_values(sp, i, side):
            first = start(sp, (i // GB) * (S * DM))
            at = [start(sp, first + j * DH) for j in range(HP)]
            for hi_lo, (dst, src) in enumerate(((vh, d["vh"]), (vl, d["vl"]))):
                for j in range(HP):
                    e = slice(j * DH, (j + 1) * DH)
                    if j == 0 and hi_lo == 0:
                        wait(sp, s["pv"], C * (i - 1))
                    sp.dma_start(dst[:, side, :, j, e].bitcast(F32),
                                 bass.AP(tensor=src.tensor, offset=at[j], ap=[[DM, S], [P, C], [1, DH]])).then_inc(s_v[side], 16)

        def load_bias(sp, i, m):
            first = start(sp, (i % GB) * G + (MAX_REL - (S - 1) + m * HP * RELW))
            wait(sp, s["bm"], 2 * (C * i + m) - 2)
            sp.dma_start(bias[:, m % 2, :, 0:G - P + S],
                         bass.AP(tensor=d["rel"].tensor, offset=first,
                                 ap=[[1, P], [RELW, HP], [1, G - P + S]])).then_inc(s_bias[m % 2], 16)

        def load_mask(sp, i):
            first = start(sp, i * (G * S))
            sp.dma_start(mask[:, :, :], rows(a["mask"], first, width=S)).then_inc(s["mask"], 16)

        def load_x(sp, i):
            first = start(sp, i * (G * DM))
            if isinstance(i, int) and i == 1:
                sp.wait_ge(s["split"], C)
            elif not isinstance(i, int) or i:
                sp.wait_ge(s["split"], job(i - 2, 2, "X3", True))
            sp.dma_start(x[:, :, :], rows(a["x"], first)).then_inc(s["x"], 16)

        def load_res(sp, i, m):
            first = start(sp, i * (G * DM) + m * P * DM)
            wait(sp, s_store[m % 2], 16 * (2 * i + m // 2))
            sp.dma_start(res[:, m % 2, :], rows(a["x"], first, 1)).then_inc(s_res[m % 2], 16)

        @block.sync
        def _(sp):
            load_x(sp, 0)
            sp.dma_start(bq[:, :], a["bq"]).then_inc(s["const"], 16)
            sp.dma_start(bo[:, :], a["bo"].partition_broadcast(P)).then_inc(s["const"], 16)
            load_mask(sp, 0)
            load_bias(sp, 0, 0)
            sp.wait_ge(s["cleared"], 4)
            load_keys(sp, 0, 0)
            load_bias(sp, 0, 1)
            load_values(sp, 0, 0)
            load_bias(sp, 0, 2)

            def store(i, m):
                first = start(sp, i * (G * DM) + m * P * DM)
                sp.wait_ge(s["x1"], C * i + m + 1)
                sp.dma_start(rows(d["x1"], first, 1), res[:, m % 2, :]).then_inc(s_store[m % 2], 16)

            def group(i, side, more, first=False):
                if more:
                    load_x(sp, i + 1)
                for m in range(C):
                    if m < 1:
                        load_bias(sp, i, m + 3)
                        if more:
                            load_mask(sp, i + 1)
                    elif more:
                        load_bias(sp, i + 1, m - 1)
                    if m == 0 and more:
                        load_keys(sp, i + 1, 1 - side)
                        load_values(sp, i + 1, 1 - side)
                    if not first:
                        store(i - 1, m)
                    if m < 2:
                        if not first:
                            load_res(sp, i - 1, m + 2)
                    else:
                        load_res(sp, i, m - 2)

            group(0, 0, True, True)
            with sp.Fori(0, NG // 2 - 1) as k:
                group(k * 2 + 1, 1, True)
                group(k * 2 + 2, 0, True)
            group(NG - 1, 1, False)
            for m in range(C):
                store(NG - 1, m)
                if m < 2:
                    load_res(sp, NG - 1, m + 2)
            for n in range(2):
                sp.wait_ge(s_store[n], 16 * NG * NT // 2)

        @block.gpsimd
        def _(pool):
            identity(nc, pool, ident, s["ident"])
            nc.gpsimd.memset(half[:, :], -0.5).then_inc(s["ident"], 1)
            nc.gpsimd.memset(huge[:, 0:1], -1.0).then_inc(s["ident"], 1)
            nc.gpsimd.memset(huge[:, 1:2], 3e38).then_inc(s["ident"], 1)
            for values in (vh, vl):
                nc.gpsimd.memset(values[:].rearrange("s a c j p -> s (a c j p)").bitcast(F32), 0.0).then_inc(s["cleared"], 1)
            pool.wait_ge(s["ident"], 5)
            pool.wait_ge(s["const"], 32)

            def column(n):
                return huge[:, n:n + 1].unsqueeze(2).broadcast_to([P, NT, S])

            def exponent(i):
                pool.wait_ge(s["var"], i + 1)
                nc.gpsimd.tensor_tensor(rstd[:, :], ve[:, :], half[:, :], ALU.pow).then_inc(s["rstd"], 1)

            def add_bo(i, m):
                pool.wait_ge(s_res[m % 2], 16 * (2 * i + m // 2) + 16)
                nc.gpsimd.tensor_tensor(res[:, m % 2, :], res[:, m % 2, :], bo[:, :], ALU.add).then_inc(s["xb"], 1)

            def mask_row(i):
                pool.wait_ge(s["mask"], 16 * i + 16)
                wait(pool, s["bm"], 2 * C * i)
                for n, (in0, in1, op) in enumerate(((mask[:, :, :], column(0), ALU.add), (mneg[:, :, :], column(1), ALU.mult),
                                                    (mneg[:, :, :], mneg[:, :, :], ALU.add))):
                    nc.gpsimd.tensor_tensor(mneg[:, :, :], in0, in1, op).then_inc(s["mneg"], 1)
                    pool.wait_ge(s["mneg"], 3 * i + n + 1)

            def add_mask(i, m, h):
                if h == 0:
                    pool.wait_ge(s_bias[m % 2], 16 * (2 * i + m // 2) + 16)
                wait(pool, s["added"], 2 * (C * i + m - 1) + h + 1)
                t = slice(2 * h, 2 * h + 2)
                nc.gpsimd.tensor_tensor(
                    bm[:, t, :, :], bias[:, m % 2, :, :].rearrange("p j (t q) -> p t j q", q=P)[:, t, :, 0:S],
                    mneg[:, t, :].unsqueeze(2).broadcast_to([P, 2, HP, S]), ALU.add).then_inc(s["bm"], 1)

            def normalise_probs(i, m, h):
                t = slice(2 * h, 2 * h + 2)
                pool.wait_ge(s["recip"], 2 * (C * i + m) + h + 1)
                nc.gpsimd.tensor_tensor(sc[:, m % 2, t, :, :], sc[:, m % 2, t, :, :],
                                        ri[:, m % 2, t, :].unsqueeze(3).broadcast_to([P, 2, HP, S]), ALU.mult).then_inc(s["normed"], 1)

            def group(i, more, first=False):
                for m in range(C):
                    one = (i, m + 1) if m < C - 1 else (i + 1, 0)
                    two = (i, m + 2) if m < 2 else (i + 1, m - 2)
                    if m == 2 and more:
                        mask_row(i + 1)
                    if m < 2 or more:
                        add_mask(*two, 0)
                        add_mask(*two, 1)
                    if m == 1 and more:
                        exponent(i + 1)
                    if m < C - 1 or more:
                        normalise_probs(*one, 0)
                        normalise_probs(*one, 1)
                    if m == C - 1:
                        add_bo(i, 0)
                    elif not first:
                        add_bo(i - 1, m + 1)

            exponent(0)
            mask_row(0)
            add_mask(0, 0, 0)
            add_mask(0, 0, 1)
            add_mask(0, 1, 0)
            add_mask(0, 1, 1)
            normalise_probs(0, 0, 0)
            normalise_probs(0, 0, 1)
            group(0, True, True)
            with pool.Fori(0, NG // 2 - 1) as k:
                group(k * 2 + 1, True)
                group(k * 2 + 2, True)
            group(NG - 1, False)
            for m in range(1, C):
                add_bo(NG - 1, m)

        @block.scalar
        def _(act):
            act.wait_ge(s["const"], 32)

            def hi(done, n, out, in_):
                act.wait_ge(s["split"], done)
                nc.scalar.activation(out, in_, ACT.Copy).then_inc(s["hi"], 1)

            def hi_x(done, n, c):
                hi(done, n, xTh[:, c, :], pW[n % 2][:, :])

            def hi_q(done, n, m):
                act.wait_ge(s["split"], done)
                nc.scalar.activation(qTh[:, :], pW[n % 2][:, :], ACT.Identity, bias=bq[:, m:m + 1]).then_inc(s["hi"], 1)

            def exp(i, m, t):
                if t % 2 == 0:
                    act.wait_ge(s["maxed"], 2 * (C * i + m) + t // 2 + 1)
                for j in range(HP):
                    last = nc.scalar.activation(sc[:, m % 2, t, j, :], sc[:, m % 2, t, j, :], ACT.Exp,
                                                bias=mx[:, m % 2, t, j:j + 1], accum_out=rs[:, m % 2, t, j:j + 1])
                if t % 2:
                    last.then_inc(s["exped"], 1)

            exp_after = {"P1": (0,), "P2": (1,), "P3": (2, 3)}

            def group(i, side, more):
                for m in range(C):
                    one = (i, m + 1) if m < C - 1 else (i + 1, 0)
                    for kind in (STEPS_JOBS if more else LAST_JOBS)[m].split():
                        n, done = number[more][(m, kind)], job(i, m, kind, more)
                        if kind[0] == "P":
                            j = int(kind[1])
                            hi(done, n, pTh[:, j, :], pW[n % 2][0:S, :])
                        elif kind[0] == "X":
                            hi_x(done, n, int(kind[1]))
                        else:
                            hi_q(done, n, (m + 2) % C)
                        if m < C - 1 or more:
                            for t in exp_after.get(kind, ()):
                                exp(*one, t)
                        if kind == ("X0" if m == 1 and more else "Q" if m < 2 or more else "P3"):
                            act.wait_ge(s["pv"], C * i + m + 1)
                            nc.scalar.activation(oTh[:, side, m, :], pV[:, :], ACT.Copy).then_inc(s["ohi"], 1)

            for c in range(C):
                hi_x(c + 1, c, c)
            hi_q(C + 1, C, 0)
            exp(0, 0, 0)
            exp(0, 0, 1)
            hi_q(C + 2, C + 1, 1)
            exp(0, 0, 2)
            exp(0, 0, 3)
            group(0, 0, True)
            with act.Fori(0, NG // 2 - 1) as k:
                group(k * 2 + 1, 1, True)
                group(k * 2 + 2, 0, True)
            group(NG - 1, 1, False)

        @block.vector
        def _(dve):
            for keys in (kbh, kbl):
                nc.vector.memset(keys[:].rearrange("p a c s -> p (a c s)").bitcast(F32), 0.0).then_inc(s["cleared"], 1)

            def norm_stats(i, tiles):
                dve.wait_ge(s["x"], 16 * i + 16)
                for t in tiles:
                    nc.vector.bn_stats(stats[:, t, :], x[:, t, :]).then_inc(s["stat"], 1)

            def norm_variance(i):
                dve.wait_ge(s["stat"], NT * i + NT)
                nc.vector.memset(pause[:, :], 0.0)
                for t in range(NT):
                    nc.vector.bn_aggr(mv[:, t, :], stats[:, t, :]).then_inc(s["aggr"], 1)
                dve.wait_ge(s["aggr"], NT * i + NT)
                nc.vector.tensor_scalar(ve[:, :], mv[:, :, 1], LN_EPS, None, ALU.add).then_inc(s["var"], 1)

            def normalise(i):
                dve.wait_ge(s["rstd"], i + 1)
                for t in range(NT):
                    nc.vector.tensor_scalar(x[:, t, :], x[:, t, :], mv[:, t, 0:1], rstd[:, t:t + 1],
                                            ALU.subtract, ALU.mult).then_inc(s["xn"], 1)

            def lo(done, out, in_, high):
                dve.wait_ge(s["hi"], done)
                nc.vector.tensor_tensor(out, in_, high.bitcast(F32), ALU.subtract).then_inc(s["lo"], 1)

            def lo_x(done, n, c):
                lo(done, xTl[:, c, :], pW[n % 2][:, :], xTh[:, c, :])

            def lo_q(done, n, m):
                dve.wait_ge(s["hi"], done)
                nc.vector.scalar_tensor_tensor(qTl[:, :], pW[n % 2][:, :], bq[:, m:m + 1],
                                               qTh[:, :].bitcast(F32), ALU.add, ALU.subtract).then_inc(s["lo"], 1)

            def add(i, m, h):
                t = slice(2 * h, 2 * h + 2)
                dve.wait_ge(s["score"], 2 * (C * i + m) + h + 1)
                dve.wait_ge(s["bm"], 2 * (C * i + m) + h + 1)
                nc.vector.tensor_tensor(sc[:, m % 2, t, :, :].rearrange("p t j s -> p t (j s)"), pS[:, t, 0:HP * S],
                                        bm[:, t, :, :].rearrange("p t j s -> p t (j s)"), ALU.add).then_inc(s["added"], 1)

            def maximum(i, m, h):
                t = slice(2 * h, 2 * h + 2)
                dve.wait_ge(s["added"], 2 * (C * i + m) + h + 1)
                nc.vector.tensor_reduce(mx[:, m % 2, t, :], sc[:, m % 2, t, :, :], AX, ALU.max, negate=True).then_inc(s["maxed"], 1)

            def reciprocal(i, m, h):
                t = slice(2 * h, 2 * h + 2)
                dve.wait_ge(s["exped"], 2 * (C * i + m) + h + 1)
                nc.vector.reciprocal(ri[:, m % 2, t, :], rs[:, m % 2, t, :]).then_inc(s["recip"], 1)

            def add_res(i, m):
                dve.wait_ge(s["wo"], C * i + m + 1)
                dve.wait_ge(s["xb"], C * i + m + 1)
                nc.vector.tensor_tensor(res[:, m % 2, :], pO[:, :], res[:, m % 2, :], ALU.add).then_inc(s["x1"], 1)

            def group(i, side, more, first=False):
                for m in range(C):
                    one = (i, m + 1) if m < C - 1 else (i + 1, 0)
                    ahead = m < C - 1 or more
                    if ahead:
                        add(*one, 0)
                        maximum(*one, 0)
                    for kind in (STEPS_JOBS if more else LAST_JOBS)[m].split():
                        n, done = number[more][(m, kind)], job(i, m, kind, more)
                        if kind == "P2" and ahead:
                            maximum(*one, 1)
                        if kind == "P3" and ahead:
                            reciprocal(*one, 0)
                        if kind == "P3" and not first:
                            add_res(i - 1, m)
                        if kind[0] == "P":
                            j = int(kind[1])
                            lo(done, pTl[:, j, :], pW[n % 2][0:S, :], pTh[:, j, :])
                        elif kind[0] == "X":
                            lo_x(done, n, int(kind[1]))
                        else:
                            lo_q(done, n, (m + 2) % C)
                            if m == 0 and more:
                                norm_stats(i + 1, (3,))
                        if kind == "P1" and ahead:
                            add(*one, 1)
                            if m == 1 and more:
                                norm_variance(i + 1)
                        if kind == "P3" and more:
                            if m == 0:
                                norm_stats(i + 1, (0, 1, 2))
                            if m == 1:
                                normalise(i + 1)
                        if kind == "P3" and ahead:
                            reciprocal(*one, 1)
                        if kind == ("X0" if m == 1 and more else "Q" if m < 2 or more else "P3"):
                            dve.wait_ge(s["ohi"], C * i + m + 1)
                            nc.vector.tensor_tensor(oTl[:, side, m, :], pV[:, :], oTh[:, side, m, :].bitcast(F32),
                                                    ALU.subtract).then_inc(s["olo"], 1)

            norm_stats(0, range(NT))
            norm_variance(0)
            normalise(0)
            for c in range(C):
                lo_x(c + 1, c, c)
            lo_q(C + 1, C, 0)
            for h in range(2):
                add(0, 0, h)
                maximum(0, 0, h)
            lo_q(C + 2, C + 1, 1)
            for h in range(2):
                reciprocal(0, 0, h)
            group(0, 0, True, True)
            with dve.Fori(0, NG // 2 - 1) as k:
                group(k * 2 + 1, 1, True)
                group(k * 2 + 2, 0, True)
            group(NG - 1, 1, False)
            for m in range(C):
                add_res(NG - 1, m)

        @block.tensor
        def _(pe):
            pe.wait_ge(s["ident"], 2)

            def three(out, xh, xl, yh, yl, first=True, last=True):
                nc.tensor.matmul(out, xh, yh, start=first, stop=False)
                nc.tensor.matmul(out, xh, yl, start=False, stop=False)
                return nc.tensor.matmul(out, xl, yh, start=False, stop=last)

            def turn_x(done, n, c):
                wait(pe, s["lo"], done - 2)
                for t in range(NT):
                    last = nc.tensor.transpose(pW[n % 2][:, t * P:(t + 1) * P], x[:, t, c * P:(c + 1) * P], ident[:, :])
                last.then_inc(s["split"], 1)

            def queries(done, n, m):
                pe.wait_ge(s["lo"], done - 2)
                w = slice(m * P, (m + 1) * P)
                for c in range(C):
                    last = three(pW[n % 2][:, :], wqh[:, c, w], wql[:, c, w], xTh[:, c, :], xTl[:, c, :], c == 0, c == C - 1)
                last.then_inc(s["split"], 1)

            def scores(i, m, side):
                for h in range(2):
                    wait(pe, s["added"], 2 * (C * i + m - 1) + h + 1)
                    for t in (2 * h, 2 * h + 1):
                        q = slice(t * P, (t + 1) * P)
                        last = three(pS[:, t, 0:HP * S], qTh[:, q], qTl[:, q], kbh[:, side, m, :], kbl[:, side, m, :])
                    last.then_inc(s["score"], 1)

            def turn_probs(i, m, j, more):
                n, done = number[more][(m, f"P{j}")], job(i, m, f"P{j}", more)
                pe.wait_ge(s["lo"], done - 2)
                if j == 0:
                    pe.wait_ge(s["normed"], 2 * (C * i + m) + 2)
                for t in range(NT):
                    last = nc.tensor.transpose(pW[n % 2][0:S, t * P:(t + 1) * P], sc[:, m % 2, t, j, :], ident[:, :])
                last.then_inc(s["split"], 1)

            def weigh(i, m, j, side, more):
                if j == 0:
                    wait(pe, s["olo"], C * i + m)
                pe.wait_ge(s["lo"], job(i, m, f"P{j}", more))
                last = three(pV[:, :], vh[:, side, m, j, :], vl[:, side, m, j, :], pTh[:, j, :], pTl[:, j, :], j == 0, j == HP - 1)
                if j == HP - 1:
                    last.then_inc(s["pv"], 1)

            def project(i, m, side, chunks):
                for c in chunks:
                    if c == 0:
                        if m == 0:
                            pe.wait_ge(s["olo"], C * i + C)
                        else:
                            pe.wait_ge(s["x1"], C * i + m)
                    q = slice(m * P, (m + 1) * P)
                    last = three(pO[:, :], oTh[:, side, c, q], oTl[:, side, c, q], woh[:, c, :], wol[:, c, :], c == 0, c == C - 1)
                    if c == C - 1:
                        last.then_inc(s["wo"], 1)

            def group(i, side, pair, more, first=False):
                pe.wait_ge(s_v[side], 16 * 2 * HP * (pair + 1))
                for m in range(C):
                    two = (i, m + 2, side) if m < 2 else (i + 1, m - 2, 1 - side)
                    ahead = m < 2 or more

                    def turn(c):
                        if c == 0:
                            pe.wait_ge(s["xn"], NT * (i + 2))
                        turn_x(job(i, m, f"X{c}", True), number[True][(m, f"X{c}")], c)

                    turn_probs(i, m, 0, more)
                    turn_probs(i, m, 1, more)
                    if not first:
                        project(i - 1, m, 1 - side, (0, 1))
                    if m == 2 and more:
                        turn(2)
                    turn_probs(i, m, 2, more)
                    if not first:
                        project(i - 1, m, 1 - side, (2, 3))
                    if m == 2 and more:
                        turn(3)
                    if m == 2:
                        weigh(i, m, 0, side, more)
                    turn_probs(i, m, 3, more)
                    if m != 2:
                        weigh(i, m, 0, side, more)
                    if ahead:
                        if m == 2:
                            pe.wait_ge(s["lo"], job(i, m, "X3", True))
                        queries(job(i, m, "Q", more), number[more][(m, "Q")], (m + 2) % C)
                    weigh(i, m, 1, side, more)
                    if m == 1 and more:
                        turn(0)
                    weigh(i, m, 2, side, more)
                    weigh(i, m, 3, side, more)
                    if m == 1 and more:
                        turn(1)
                    if ahead:
                        if m == 2:
                            pe.wait_ge(s_kb[1 - side], 16 * 2 * HP * (pair + side + 1))
                        pe.wait_ge(s["lo"], job(i, m, "Q", more))
                        scores(*two)

            pe.wait_ge(s["xn"], NT)
            for c in range(C):
                turn_x(c + 1, c, c)
            pe.wait_ge(s["lo"], C)
            queries(C + 1, C, 0)
            pe.wait_ge(s["lo"], C + 1)
            pe.wait_ge(s_kb[0], 16 * 2 * HP)
            scores(0, 0, 0)
            queries(C + 2, C + 1, 1)
            pe.wait_ge(s["lo"], C + 2)
            scores(0, 1, 0)
            group(0, 0, 0, True, True)
            with pe.Fori(0, NG // 2 - 1) as k:
                group(k * 2 + 1, 1, k, True)
                group(k * 2 + 2, 0, k + 1, True)
            group(NG - 1, 1, NG // 2 - 1, False)
            for m in range(C):
                project(NG - 1, m, 1, range(C))


def spiking(nc, a, d):
    with ExitStack() as ctx:
        sb, ps, sem = place(nc, ctx)
        TURNS = C + NF
        BACKS = C + 1
        ident = sb("f_ident", [P, P])
        ones = sb("f_ones", [1, S])
        half = sb("f_half", [P, NT])
        wfh, wfl = (sb(f"f_wf{n}", [P, C, FF], F32R) for n in "hl")
        wph, wpl = (sb(f"f_wp{n}", [P, NF, DM], F32R) for n in "hl")
        x = sb("f_x", [P, NT, DM])
        y = sb("f_y", [P, NT, DM])
        xp = sb("f_xp", [P, NT, DM])
        xTh, xTl = (sb(f"f_xT{n}", [P, C, G], F32R) for n in "hl")
        r = sb("f_r", [P, 2, G])
        hh, hl = (sb(f"f_h{n}", [P, 2, G], F32R) for n in "hl")
        bTh, bTl = (sb(f"f_bT{n}", [P, 2, G], F32R) for n in "hl")
        mem = sb("f_mem", [P, DM])
        lead = sb("f_lead", [P, DM])
        count = sb("f_count", [P, DM])
        dist = sb("f_dist", [S, G])
        stats = sb("f_stats", [P, NT, 6])
        pause = sb("f_pause", [P, 1])
        mv = sb("f_mv", [P, NT, 2])
        ve = sb("f_ve", [P, NT])
        rstd = sb("f_rstd", [P, NT])
        stats2 = sb("f_stats2", [P, NT, 6])
        mv2 = sb("f_mv2", [P, NT, 2])
        ve2 = sb("f_ve2", [P, NT])
        rstd2 = sb("f_rstd2", [P, NT])
        sq = sb("f_sq", [P, NT])
        bb = sb("f_bb", [1, G])
        ch, cl = (sb(f"f_c{n}", [P, C, S], F32R) for n in "hl")
        aa = sb("f_aa", [S, 1])
        pH = [ps(f"f_pH{n}") for n in range(2)]
        pY = ctx.enter_context(nc.psum_tensor("f_pY", [P, NT, 512], F32))
        pB = ps("f_pB")
        pD = ps("f_pD")
        names = ("ident wh wl x stat aggr var rstd xn turn hi lo relued squared hhi hlo y ycopied xp lif "
                 "x2 stored2 stat2 aggr2 var2 rstd2 xn2 sq back bhi blo bb ctx dist dclip dsqrt dstore").split()
        s = {n: sem(f"f_{n}_s") for n in names}
        block = ctx.enter_context(nc.Block())
        stage = [y, xp]
        s_w = [sem(f"f_w{n}_s") for n in range(len(stage))]
        WCH = 2 * C
        PARTS = STEPS - 1
        LIF = 1 + 3 * PARTS
        F_STATS, F_NEXT, F_BACK = 8, 10, 10

        @block.sync
        def _(sp):
            def load_x(i):
                first = start(sp, i * (G * DM))
                wait(sp, s["lo"], C * i)
                sp.dma_start(x[:, :, :], rows(d["x1"], first)).then_inc(s["x"], 16)

            load_x(0)
            for n in range(WCH):
                if n >= len(stage):
                    sp.wait_ge(s["wl"], n - len(stage) + 1)
                if n < C:
                    src = a["WfcT"][n * P:(n + 1) * P, :].rearrange("p (q d) -> p q d", d=DM)
                else:
                    src = a["WprojT"][(n - C) * 4 * P:(n - C + 1) * 4 * P, :].rearrange("(q p) d -> p q d", p=P)
                sp.dma_start(stage[n % len(stage)][:, :, :], src).then_inc(s_w[n % len(stage)], 16)

            def load_back(k):
                batch, at_aa, first = (start(sp, (k // GB) * (P * C * S)), start(sp, (k // GB) * S), start(sp, k * (G * DM)))
                wait(sp, s["dsqrt"], k)
                sp.dma_start(ch[:, :, :].bitcast(F32), bass.AP(tensor=d["c2h"].tensor, offset=batch, ap=[[C * S, P], [S, C], [1, S]])).then_inc(s["ctx"], 16)
                sp.dma_start(cl[:, :, :].bitcast(F32), bass.AP(tensor=d["c2l"].tensor, offset=batch, ap=[[C * S, P], [S, C], [1, S]])).then_inc(s["ctx"], 16)
                sp.dma_start(aa[:, :], bass.AP(tensor=d["aa"].tensor, offset=at_aa, ap=[[1, S], [1, 1]])).then_inc(s["ctx"], 16)
                wait(sp, s["stored2"], 16 * k)
                sp.dma_start(xp[:, :, :], rows(d["x1"], first)).then_inc(s["xp"], 16)

            def store_back(k):
                first, block_ = start(sp, k * (G * DM)), skew_start(sp, k)
                sp.wait_ge(s["x2"], NT * (k + 1))
                sp.dma_start(rows(d["x2"], first), xp[:, :, :]).then_inc(s["stored2"], 16)
                sp.wait_ge(s["dsqrt"], k + 1)
                sp.dma_start(skewed(d["dist"], block_), dist[:, :].rearrange("s (c w) -> s c w", w=W)).then_inc(s["dstore"], 16)

            def group(i, back, more):
                if back:
                    load_back(i - 1)
                if more:
                    load_x(i + 1)
                if back:
                    store_back(i - 1)

            group(0, False, True)
            sp.wait_ge(s["wl"], WCH)
            group(1, True, True)
            with sp.Fori(2, NG - 1) as i:
                group(i, True, True)
            group(NG - 1, True, False)
            load_back(NG - 1)
            store_back(NG - 1)
            sp.wait_ge(s["stored2"], 16 * NG)
            sp.wait_ge(s["dstore"], 16 * NG)

        @block.gpsimd
        def _(pool):
            identity(nc, pool, ident, s["ident"])
            nc.gpsimd.memset(half[:, :], -0.5).then_inc(s["ident"], 1)
            nc.gpsimd.memset(ones[:, :], 1.0).then_inc(s["ident"], 1)
            pool.wait_ge(s["ident"], 4)

            def exponent(i):
                pool.wait_ge(s["var"], i + 1)
                nc.gpsimd.tensor_tensor(rstd[:, :], ve[:, :], half[:, :], ALU.pow).then_inc(s["rstd"], 1)

            def exponent2(k):
                pool.wait_ge(s["var2"], k + 1)
                nc.gpsimd.tensor_tensor(rstd2[:, :], ve2[:, :], half[:, :], ALU.pow).then_inc(s["rstd2"], 1)

            def group(i, back, more):
                for f in range(NF):
                    pool.wait_ge(s["hhi"], NF * i + f + 1)
                    nc.gpsimd.tensor_tensor(hl[:, f % 2, :], r[:, f % 2, :], hh[:, f % 2, :].bitcast(F32), ALU.subtract).then_inc(s["hlo"], 1)
                    if back and f == F_STATS:
                        exponent2(i - 1)
                    if more and f == F_NEXT:
                        exponent(i + 1)

            exponent(0)
            group(0, False, True)
            group(1, True, True)
            with pool.Fori(2, NG - 1) as i:
                group(i, True, True)
            group(NG - 1, True, False)
            exponent2(NG - 1)

        @block.scalar
        def _(act):
            def weight_hi(n):
                act.wait_ge(s_w[n % len(stage)], 16 * (n // len(stage) + 1))
                out = wfh[:, n, :] if n < C else wph[:, 4 * (n - C):4 * (n - C) + 4, :].rearrange("p q d -> p (q d)")
                nc.scalar.activation(out, stage[n % len(stage)][:, :, :].rearrange("p q d -> p (q d)"), ACT.Copy).then_inc(s["wh"], 1)

            def back_squares(k):
                for t in range(NT):
                    act.wait_ge(s["xn2"], NT * k + t + 1)
                    wait(act, s["sq"], NT * k + t)
                    nc.scalar.activation(lead[:, :], y[:, t, :], ACT.Square, accum_out=sq[:, t:t + 1]).then_inc(s["sq"], 1)

            def back_hi(k, c):
                act.wait_ge(s["back"], BACKS * k + c + 1)
                nc.scalar.activation(bTh[:, c % 2, :], pB[:, :], ACT.Copy).then_inc(s["bhi"], 1)

            def back_root(k):
                act.wait_ge(s["dclip"], k + 1)
                nc.scalar.activation(dist[:, :], dist[:, :], ACT.Sqrt).then_inc(s["dsqrt"], 1)

            def turns(i):
                for c in range(C):
                    act.wait_ge(s["turn"], TURNS * i + c + 1)
                    nc.scalar.activation(xTh[:, c, :], pH[c % 2][:, :], ACT.Copy).then_inc(s["hi"], 1)

            def group(i, back, more):
                for f in range(NF):
                    act.wait_ge(s["turn"], TURNS * i + C + f + 1)
                    wait(act, s["hlo"], NF * i + f - 1)
                    nc.scalar.activation(r[:, f % 2, :], pH[f % 2][:, :], ACT.Relu).then_inc(s["relued"], 1)
                    act.wait_ge(s["squared"], NF * i + f + 1)
                    nc.scalar.activation(hh[:, f % 2, :], r[:, f % 2, :], ACT.Copy).then_inc(s["hhi"], 1)
                    if not back and f < C:
                        weight_hi(C + f)
                    if back and f == F_BACK:
                        back_squares(i - 1)
                    if back and F_BACK < f <= F_BACK + C:
                        back_hi(i - 1, f - F_BACK - 1)
                if more:
                    turns(i + 1)
                act.wait_ge(s["y"], i + 1)
                for t in range(NT):
                    nc.scalar.activation(y[:, t, :], pY[:, t, :], ACT.Copy).then_inc(s["ycopied"], 1)
                if back:
                    back_root(i - 1)

            weight_hi(0)
            weight_hi(1)
            turns(0)
            weight_hi(2)
            weight_hi(3)
            group(0, False, True)
            group(1, True, True)
            with act.Fori(2, NG - 1) as i:
                group(i, True, True)
            group(NG - 1, True, False)
            for c in range(C):
                back_hi(NG - 1, c)
            back_squares(NG - 1)
            back_root(NG - 1)

        @block.vector
        def _(dve):
            def weight_lo(n):
                dve.wait_ge(s["wh"], n + 1)
                h, l = ((w[:, n, :] if n < C else w[:, 4 * (n - C):4 * (n - C) + 4, :].rearrange("p q d -> p (q d)"))
                        for w in ((wfh, wfl) if n < C else (wph, wpl)))
                nc.vector.tensor_tensor(l, stage[n % len(stage)][:, :, :].rearrange("p q d -> p (q d)"), h.bitcast(F32), ALU.subtract).then_inc(s["wl"], 1)

            def norm_stats(i):
                dve.wait_ge(s["x"], 16 * i + 16)
                for t in range(NT):
                    nc.vector.bn_stats(stats[:, t, :], x[:, t, :]).then_inc(s["stat"], 1)
                dve.wait_ge(s["stat"], NT * i + NT)
                nc.vector.memset(pause[:, :], 0.0)
                for t in range(NT):
                    nc.vector.bn_aggr(mv[:, t, :], stats[:, t, :]).then_inc(s["aggr"], 1)
                dve.wait_ge(s["aggr"], NT * i + NT)
                nc.vector.tensor_scalar(ve[:, :], mv[:, :, 1], LN_EPS, None, ALU.add).then_inc(s["var"], 1)

            def normalise(i):
                dve.wait_ge(s["rstd"], i + 1)
                for t in range(NT):
                    nc.vector.tensor_scalar(x[:, t, :], x[:, t, :], mv[:, t, 0:1], rstd[:, t:t + 1],
                                            ALU.subtract, ALU.mult).then_inc(s["xn"], 1)

            def spikes(k, t, part):
                n = (NT * k + t) * LIF
                if part == 0:
                    dve.wait_ge(s["ycopied"], NT * (k + 1))
                    wait(dve, s["x2"], NT * k + t)
                    nc.vector.tensor_scalar(count[:, :], y[:, t, :], THRESHOLD, None, ALU.is_gt).then_inc(s["lif"], 1)
                m = n + 1 + 3 * part
                old = y[:, t, :] if part == 0 else mem[:, :]
                if part:
                    dve.wait_ge(s["lif"], m - 1)
                nc.vector.scalar_tensor_tensor(lead[:, :], old, BETA, y[:, t, :], ALU.mult, ALU.add).then_inc(s["lif"], 1)
                dve.wait_ge(s["lif"], m + 1)
                nc.vector.scalar_tensor_tensor(mem[:, :], old, THRESHOLD, lead[:, :], ALU.is_gt, ALU.subtract,
                                               reverse1=True).then_inc(s["lif"], 1)
                dve.wait_ge(s["lif"], m + 2)
                nc.vector.scalar_tensor_tensor(count[:, :], mem[:, :], THRESHOLD, count[:, :], ALU.is_gt, ALU.add).then_inc(s["lif"], 1)
                if part == PARTS - 1:
                    if t == 0:
                        dve.wait_ge(s["xp"], 16 * (k + 1))
                    dve.wait_ge(s["lif"], n + LIF)
                    nc.vector.scalar_tensor_tensor(xp[:, t, :], count[:, :], 1.0 / STEPS, xp[:, t, :], ALU.mult, ALU.add).then_inc(s["x2"], 1)

            def back_stats(k):
                for t in range(NT):
                    dve.wait_ge(s["x2"], NT * k + t + 1)
                    nc.vector.bn_stats(stats2[:, t, :], xp[:, t, :]).then_inc(s["stat2"], 1)
                dve.wait_ge(s["stat2"], NT * k + NT)
                nc.vector.memset(pause[:, :], 0.0)
                for t in range(NT):
                    nc.vector.bn_aggr(mv2[:, t, :], stats2[:, t, :]).then_inc(s["aggr2"], 1)
                dve.wait_ge(s["aggr2"], NT * k + NT)
                nc.vector.tensor_scalar(ve2[:, :], mv2[:, :, 1], LN_EPS, None, ALU.add).then_inc(s["var2"], 1)

            def back_normalise(k):
                dve.wait_ge(s["rstd2"], k + 1)
                for t in range(NT):
                    nc.vector.tensor_scalar(y[:, t, :], xp[:, t, :], mv2[:, t, 0:1], rstd2[:, t:t + 1],
                                            ALU.subtract, ALU.mult).then_inc(s["xn2"], 1)

            def back_lo(k, c):
                dve.wait_ge(s["bhi"], C * k + c + 1)
                nc.vector.tensor_tensor(bTl[:, c % 2, :], pB[:, :], bTh[:, c % 2, :].bitcast(F32), ALU.subtract).then_inc(s["blo"], 1)

            def back_row(k):
                dve.wait_ge(s["back"], BACKS * k + BACKS)
                nc.vector.tensor_copy(bb[:, :], pB[0:1, :]).then_inc(s["bb"], 1)

            def back_distance(k):
                dve.wait_ge(s["dist"], k + 1)
                wait(dve, s["dstore"], 16 * k)
                nc.vector.tensor_scalar(dist[:, :], pD[0:S, :], aa[:, :], 0.0, ALU.add, ALU.max).then_inc(s["dclip"], 1)

            def turn(i, c):
                dve.wait_ge(s["hi"], C * i + c + 1)
                nc.vector.tensor_tensor(xTl[:, c, :], pH[c % 2][:, :], xTh[:, c, :].bitcast(F32), ALU.subtract).then_inc(s["lo"], 1)

            def group(i, back, more):
                for f in range(NF):
                    dve.wait_ge(s["relued"], NF * i + f + 1)
                    nc.vector.scalar_tensor_tensor(r[:, f % 2, :], pH[f % 2][:, :], 0.0, r[:, f % 2, :], ALU.max, ALU.mult).then_inc(s["squared"], 1)
                    if not back and f < C:
                        weight_lo(C + f)
                    if back and f < F_STATS:
                        for n in range(PARTS * NT * f // F_STATS, PARTS * NT * (f + 1) // F_STATS):
                            spikes(i - 1, n // PARTS, n % PARTS)
                    if back and f == F_STATS:
                        back_stats(i - 1)
                    if back and f == F_STATS + 1:
                        back_normalise(i - 1)
                    if more and f == F_NEXT:
                        norm_stats(i + 1)
                    if more and f == F_NEXT + 1:
                        normalise(i + 1)
                    if back and F_BACK < f <= F_BACK + C:
                        back_lo(i - 1, f - F_BACK - 1)
                for c in range(C):
                    if back and c == C - 1:
                        back_row(i - 1)
                    if more:
                        turn(i + 1, c)
                if back:
                    back_distance(i - 1)

            norm_stats(0)
            normalise(0)
            weight_lo(0)
            weight_lo(1)
            for c in range(C):
                turn(0, c)
            weight_lo(2)
            weight_lo(3)
            group(0, False, True)
            group(1, True, True)
            with dve.Fori(2, NG - 1) as i:
                group(i, True, True)
            group(NG - 1, True, False)
            for t in range(NT):
                for part in range(PARTS):
                    spikes(NG - 1, t, part)
            back_stats(NG - 1)
            back_normalise(NG - 1)
            for c in range(C):
                back_lo(NG - 1, c)
            back_row(NG - 1)
            back_distance(NG - 1)

        @block.tensor
        def _(pe):
            pe.wait_ge(s["ident"], 4)

            def three(out, xh, xl, yh, yl, first, last):
                nc.tensor.matmul(out, xh, yh, start=first, stop=False)
                nc.tensor.matmul(out, xh, yl, start=False, stop=False)
                return nc.tensor.matmul(out, xl, yh, start=False, stop=last)

            def hidden(i, f):
                if f > 1:
                    pe.wait_ge(s["squared"], NF * i + f - 1)
                w = slice(f * P, (f + 1) * P)
                for c in range(C):
                    last = three(pH[f % 2][:, :], wfh[:, c, w], wfl[:, c, w], xTh[:, c, :], xTl[:, c, :], c == 0, c == C - 1)
                last.then_inc(s["turn"], 1)

            def project(i, f, tiles=range(NT)):
                pe.wait_ge(s["hlo"], NF * i + f + 1)
                if f == 0:
                    wait(pe, s["ycopied"], NT * i)
                for t in tiles:
                    q = slice(t * P, (t + 1) * P)
                    last = three(pY[:, t, :], hh[:, f % 2, q], hl[:, f % 2, q], wph[:, f, :], wpl[:, f, :], f == 0, f == NF - 1)
                if f == NF - 1 and t == NT - 1:
                    last.then_inc(s["y"], 1)

            def back_turn(k, c):
                pe.wait_ge(s["xn2"], NT * (k + 1))
                if c:
                    pe.wait_ge(s["blo"], C * k + c)
                else:
                    wait(pe, s["bb"], k)
                for t in range(NT):
                    last = nc.tensor.transpose(pB[:, t * P:(t + 1) * P], y[:, t, c * P:(c + 1) * P], ident[:, :])
                last.then_inc(s["back"], 1)

            def back_dist(k, c):
                pe.wait_ge(s["blo"], C * k + c + 1)
                if c == 0:
                    pe.wait_ge(s["ctx"], 48 * (k + 1))
                    wait(pe, s["dclip"], k)
                three(pD[0:S, :], ch[:, c, :], cl[:, c, :], bTh[:, c % 2, :], bTl[:, c % 2, :], c == 0, False)

            def back_row(k):
                pe.wait_ge(s["sq"], NT * (k + 1))
                pe.wait_ge(s["blo"], C * (k + 1))
                for t in range(NT):
                    last = nc.tensor.matmul(pB[0:1, t * P:(t + 1) * P], sq[:, t:t + 1], ident[:, :], start=True, stop=True)
                last.then_inc(s["back"], 1)

            def back_finish(k):
                pe.wait_ge(s["bb"], k + 1)
                nc.tensor.matmul(pD[0:S, :], ones[:, :], bb[:, :], start=False, stop=True).then_inc(s["dist"], 1)

            def turn(i, c):
                if c == 0:
                    pe.wait_ge(s["xn"], NT * (i + 1))
                if c < 2:
                    wait(pe, s["squared"], NF * i - 1 + c)
                else:
                    pe.wait_ge(s["lo"], C * i + c - 1)
                for t in range(NT):
                    last = nc.tensor.transpose(pH[c % 2][:, t * P:(t + 1) * P], x[:, t, c * P:(c + 1) * P], ident[:, :])
                last.then_inc(s["turn"], 1)

            def group(i, back, more):
                pe.wait_ge(s["lo"], C * i + C)
                if not back:
                    pe.wait_ge(s["wl"], C)
                hidden(i, 0)
                hidden(i, 1)
                for f in range(NF):
                    if not back and f % 4 == 0:
                        pe.wait_ge(s["wl"], C + f // 4 + 1)
                    if f < NF - 1:
                        project(i, f)
                    if f + 2 < NF:
                        hidden(i, f + 2)
                    if back and F_BACK < f <= F_BACK + C:
                        back_dist(i - 1, f - F_BACK - 1)
                    if back and F_BACK <= f < F_BACK + C:
                        back_turn(i - 1, f - F_BACK)
                    if more and f == NF - 3:
                        turn(i + 1, 0)
                    if more and f == NF - 2:
                        turn(i + 1, 1)
                        turn(i + 1, 2)
                    if back and f == NF - 2:
                        back_row(i - 1)
                project(i, NF - 1, range(0, NT // 2))
                if more:
                    turn(i + 1, C - 1)
                if back:
                    back_finish(i - 1)
                project(i, NF - 1, range(NT // 2, NT))

            for c in range(C):
                turn(0, c)
            group(0, False, True)
            group(1, True, True)
            with pe.Fori(2, NG - 1) as i:
                group(i, True, True)
            group(NG - 1, True, False)
            for c in range(C):
                back_turn(NG - 1, c)
                back_dist(NG - 1, c)
            back_row(NG - 1)
            back_finish(NG - 1)


def align(nc, a, d, w):
    with ExitStack() as ctx:
        sb, ps, sem = place(nc, ctx)
        CHUNKS = 4
        D = sb("d_D", [P, SLOTS + 1, W + 1])
        on = D
        R = sb("d_R", [P, SLOTS + 1, W + 1])
        M = sb("d_M", [P, SLOTS, W + 1])
        left = sb("d_left", [P, SLOTS, W + 1], BF16)
        into = sb("d_into", [P, SLOTS, W + 1], BF16)
        edge = sb("d_edge", [P, 2, SLOTS], BF16)
        inner = sb("d_inner", [P, 1])
        via = sb("d_via", [P, W + 1])
        enter = sb("d_enter", [P, W])
        stage = sb("d_stage", [P, 2, C, DM])
        names = "init R best edge flags inner on0 sh pr en on out wh wl".split()
        s = {n: sem(f"d_{n}_s") for n in names}
        s_D = [sem(f"d_D{k}_s") for k in range(CHUNKS)]
        s_w = [sem(f"d_w{n}_s") for n in range(2)]
        block = ctx.enter_context(nc.Block())
        from_left = [(p - 1) % 32 for p in range(32)]
        from_right = [(p + 1) % 32 for p in range(32)]
        bounds = [SLOTS * k // CHUNKS for k in range(CHUNKS + 1)]

        def part(k):
            return slice(bounds[k], bounds[k + 1])

        def blocks(scratch, b, k):
            return bass.AP(tensor=scratch.tensor, offset=b * SKEW_BATCH + bounds[k] * W,
                           ap=[[SLOTS * W, NB], [W, bounds[k + 1] - bounds[k]], [1, W]])

        @block.sync
        def _(sp):
            for k in range(CHUNKS):
                for b in range(B):
                    sp.dma_start(D[b * NB:(b + 1) * NB, part(k), 1:W + 1], blocks(d["dist"], b, k)).then_inc(s_D[k], 16)
            for n, name in enumerate(("WrT", "WkkT", "WvvT")):
                if n >= 2:
                    sp.wait_ge(s["wl"], n - 1)
                sp.dma_start(stage[:, n % 2, :, :], a[name].rearrange("(c p) d -> p c d", p=P)).then_inc(s_w[n % 2], 16)
            for k in reversed(range(CHUNKS)):
                sp.wait_ge(s["on"], SLOTS - bounds[k])
                for b in range(B):
                    sp.dma_start(blocks(d["on"], b, k), on[b * NB:(b + 1) * NB, part(k), 0:W]).then_inc(s["out"], 16)
            sp.wait_ge(s["out"], 16 * B * CHUNKS)

        @block.scalar
        def _(act):
            for n, k in enumerate("rkv"):
                act.wait_ge(s_w[n % 2], 16 * (n // 2 + 1))
                nc.scalar.activation(w[k][0][:, :, :], stage[:, n % 2, :, :], ACT.Copy).then_inc(s["wh"], 1)

        @block.gpsimd
        def _(pool):
            nc.gpsimd.memset(inner[:, :], 1.0).then_inc(s["inner"], 1)
            nc.gpsimd.memset(enter[:, :], 0.0).then_inc(s["inner"], 1)
            for b in range(B):
                pool.wait_ge(s["inner"], 2 * b + 2)
                last = (b + 1) * NB - 1
                nc.gpsimd.affine_select(out=inner[:, :], in_=inner[:, :], compare_op=ALU.not_equal, fill=0.0,
                                        base=-last, pattern=[[0, 1]], channel_multiplier=1).then_inc(s["inner"], 1)
                nc.gpsimd.affine_select(out=enter[:, :], in_=enter[:, :], compare_op=ALU.not_equal, fill=1.0,
                                        base=-(last * W + W - 1), pattern=[[1, W]], channel_multiplier=W).then_inc(s["inner"], 1)
            for n, k in enumerate("rkv"):
                pool.wait_ge(s["wh"], n + 1)
                nc.gpsimd.tensor_tensor(w[k][1][:, :, :], stage[:, n % 2, :, :], w[k][0][:, :, :].bitcast(F32), ALU.subtract).then_inc(s["wl"], 1)

        @block.vector
        def _(dve):
            nc.vector.memset(R[:, 0, :], BIG).then_inc(s["init"], 1)
            nc.vector.memset(D[:, 0:SLOTS, 0:1], 0.0).then_inc(s["init"], 1)
            dve.wait_ge(s["init"], 2)
            for b in range(B):
                nc.vector.memset(R[b * NB:b * NB + 1, 0, 0:1], 0.0).then_inc(s["init"], 1)
                nc.vector.memset(D[b * NB:b * NB + 1, 0:SLOTS, 0:1], BIG).then_inc(s["init"], 1)
            dve.wait_ge(s["init"], 2 + 2 * B)

            def is_left(t):
                nc.vector.tensor_tensor(left[:, t, 0:W], R[:, t + 1, 0:W], M[:, t, 1:W + 1], ALU.is_lt).then_inc(s["flags"], 1)

            for t in range(SLOTS):
                if t in bounds:
                    dve.wait_ge(s_D[bounds.index(t)], 16 * B)
                if t >= 2:
                    is_left(t - 2)
                if t:
                    dve.wait_ge(s["R"], t)
                nc.vector.stream_shuffle(M[:, t, 0:1], R[:, t, W:W + 1], from_left).then_inc(s["best"], 1)
                nc.vector.tensor_tensor(M[:, t, 1:W + 1], R[:, t, 1:W + 1], R[:, t, 0:W], ALU.min).then_inc(s["best"], 1)
                nc.vector.tensor_tensor(into[:, t, 0:W], R[:, t, 0:W], R[:, t, 1:W + 1], ALU.is_le).then_inc(s["flags"], 1)
                dve.wait_ge(s["best"], 2 * t + 2)
                nc.vector.tensor_tensor_scan(R[:, t + 1, :], M[:, t, :], D[:, t, :], BIG, ALU.min, ALU.add).then_inc(s["R"], 1)
            dve.wait_ge(s["R"], SLOTS)

            is_left(SLOTS - 2)
            is_left(SLOTS - 1)
            done = 2 * SLOTS + 1
            dve.wait_ge(s["flags"], done - 1)
            nc.vector.scalar_tensor_tensor(into[:, :, 0:W], left[:, :, 0:W], -3.0, into[:, :, 0:W], ALU.mult, ALU.add).then_inc(s["flags"], 1)
            dve.wait_ge(s["flags"], done)
            sides = (left, into)
            for n, flag in enumerate(sides):
                nc.vector.stream_shuffle(edge[:, n, :], flag[:, :, 0], from_right).then_inc(s["edge"], 1)
            dve.wait_ge(s["edge"], 2)
            dve.wait_ge(s["inner"], 2 + 2 * B)
            for n, flag in enumerate(sides):
                nc.vector.memset(flag[:, SLOTS - 1, W:W + 1], 0.0).then_inc(s["flags"], 1)
                nc.vector.tensor_scalar(flag[:, 0:SLOTS - 1, W], edge[:, n, 1:SLOTS], inner[:, 0:1], None, ALU.mult).then_inc(s["flags"], 1)
            nc.vector.memset(on[:, SLOTS, :], 0.0).then_inc(s["on0"], 1)
            dve.wait_ge(s["flags"], done + 4)
            dve.wait_ge(s["on0"], 1)

            for n in range(SLOTS):
                t = SLOTS - 1 - n
                if n:
                    dve.wait_ge(s["on"], n)
                    nc.vector.stream_shuffle(on[:, t, W:W + 1], on[:, t + 1, 0:1], from_right).then_inc(s["sh"], 1)
                    nc.vector.scalar_tensor_tensor(via[:, :], into[:, t + 1, :], 1.0, on[:, t + 1, :], ALU.add, ALU.mult).then_inc(s["pr"], 1)
                    dve.wait_ge(s["pr"], n)
                    nc.vector.scalar_tensor_tensor(enter[:, :], via[:, 1:W + 1], 1.5, via[:, 0:W], ALU.is_lt, ALU.is_equal).then_inc(s["en"], 1)
                    dve.wait_ge(s["en"], n)
                else:
                    nc.vector.memset(on[:, t, W:W + 1], 0.0).then_inc(s["sh"], 1)
                dve.wait_ge(s["sh"], n + 1)
                nc.vector.tensor_tensor_scan(on[:, t, W - 1::-1], left[:, t, W:0:-1], enter[:, ::-1], on[:, t, W:W + 1],
                                             ALU.mult, ALU.add).then_inc(s["on"], 1)


def mixing(nc, a, d, w, out):
    with ExitStack() as ctx:
        sb, ps, sem = place(nc, ctx)
        ident = sb("m_ident", [P, P])
        half = sb("m_half", [P, NT])
        mu = sb("m_mu", [P, 2, C])
        nu = sb("m_nu", [P, 2, C])
        inside = sb("m_inside", [P, NG])
        x3 = sb("m_x3", [P, 2, NT, DM])
        path = sb("m_path", [S, G], F32R)
        ch, cl = (sb(f"m_c{n}", [S, DM], F32R) for n in "hl")
        xn = sb("m_xn", [P, NT, DM])
        stats = sb("m_stats", [P, NT, 6])
        pause = sb("m_pause", [P, 1])
        mv = sb("m_mv", [P, NT, 2])
        ve = sb("m_ve", [P, NT])
        rstd = sb("m_rstd", [P, NT])
        xT = sb("m_xT", [P, C, G + 1])
        part = sb("m_part", [P, 2, G])
        mix = sb("m_mix", [P, 2, G])
        zh, zl = (sb(f"m_z{n}", [P, 2, 2, C, G], F32R) for n in "hl")
        r = sb("m_relu", [P, 2, G])
        hh, hl = (sb(f"m_h{n}", [P, C, G], F32R) for n in "hl")
        gate = sb("m_gate", [P, NT, DM])
        res = sb("m_res", [P, 2, DM])
        pE = [ps(f"m_pE{n}") for n in range(2)]
        pT = [ps(f"m_pT{n}") for n in range(2)]
        pK = [ps(f"m_pK{n}") for n in range(2)]
        pR = [ps(f"m_pR{n}") for n in range(2)]
        pV = pK + pR
        names = ("ident mu nu path ctx exp x3 stat aggr var rstd xn turn first xT part mix zhi zlo "
                 "R gate K relued squared hhi hlo V gated res").split()
        s = {n: sem(f"m_{n}_s") for n in names}
        s_store = [sem(f"m_store{n}_s") for n in range(2)]
        s_x2 = [[sem(f"m_x2_{n}{t}_s") for t in range(NT)] for n in range(2)]
        block = ctx.enter_context(nc.Block())
        @block.sync
        def _(sp):
            sp.dma_start(mu[:, 0, :], a["mu_r"]).then_inc(s["mu"], 16)
            sp.dma_start(mu[:, 1, :], a["mu_k"]).then_inc(s["mu"], 16)

            def load_x2(j, side, t):
                first = start(sp, j * (G * DM) + t * P * DM)
                sp.dma_start(x3[:, side, t, :], rows(d["x2"], first, 1)).then_inc(s_x2[side][t], 16)

            def load_path(j):
                batch, block_ = start(sp, (j // GB) * (S * DM)), skew_start(sp, j)
                wait(sp, s["exp"], NT * j)
                sp.dma_start(path[:, :].bitcast(F32).rearrange("s (c w) -> s c w", w=W), skewed(d["on"], block_)).then_inc(s["path"], 16)
                sp.dma_start(ch[:, :].bitcast(F32), bass.AP(tensor=d["ch"].tensor, offset=batch, ap=[[DM, S], [1, DM]])).then_inc(s["ctx"], 16)
                sp.dma_start(cl[:, :].bitcast(F32), bass.AP(tensor=d["cl"].tensor, offset=batch, ap=[[DM, S], [1, DM]])).then_inc(s["ctx"], 16)

            def group(i, side, ahead=True):
                if ahead:
                    load_path(i + 2)
                for t in range(NT):
                    first = start(sp, i * (G * DM) + t * P * DM)
                    sp.wait_ge(s["res"], NT * i + t + 1)
                    sp.dma_start(rows(out, first, 1), res[:, t % 2, :]).then_inc(s_store[t % 2], 16)
                    if ahead:
                        load_x2(i + 2, side, t)

            for t in range(NT):
                load_x2(0, 0, t)
            load_path(0)
            for t in range(NT):
                load_x2(1, 1, t)
            load_path(1)
            group(0, 0)
            with sp.Fori(0, NG // 2 - 2) as k:
                group(k * 2 + 1, 1)
                group(k * 2 + 2, 0)
            group(NG - 3, 1)
            group(NG - 2, 0, False)
            group(NG - 1, 1, False)
            for n in range(2):
                sp.wait_ge(s_store[n], 16 * NG * NT // 2)

        @block.gpsimd
        def _(pool):
            identity(nc, pool, ident, s["ident"])
            nc.gpsimd.memset(half[:, :], -0.5).then_inc(s["ident"], 1)
            nc.gpsimd.memset(inside[:, :], 1.0).then_inc(s["ident"], 1)
            pool.wait_ge(s["ident"], 4)
            nc.gpsimd.memset(inside[:, ::GB], 0.0).then_inc(s["ident"], 1)

            def front(j):
                pool.wait_ge(s["var"], j + 1)
                nc.gpsimd.tensor_tensor(rstd[:, :], ve[:, :], half[:, :], ALU.pow).then_inc(s["rstd"], 1)

            def front_mix(j, side, c):
                for z in range(2):
                    n = 2 * (C * j + c) + z + 1
                    pool.wait_ge(s["zhi"], n)
                    nc.gpsimd.tensor_tensor(zl[:, side, z, c, :], mix[:, z, :], zh[:, side, z, c, :].bitcast(F32), ALU.subtract).then_inc(s["zlo"], 1)

            def group(i, side, more):
                for m in range(C):
                    if more and m == 2:
                        front(i + 1)
                    pool.wait_ge(s["hhi"], C * i + m + 1)
                    nc.gpsimd.tensor_tensor(hl[:, m, :], r[:, m % 2, :], hh[:, m, :].bitcast(F32), ALU.subtract).then_inc(s["hlo"], 1)
                if more:
                    for c in range(C):
                        front_mix(i + 1, 1 - side, c)

            front(0)
            for c in range(C):
                front_mix(0, 0, c)
            group(0, 0, True)
            with pool.Fori(0, NG // 2 - 1) as k:
                group(k * 2 + 1, 1, True)
                group(k * 2 + 2, 0, True)
            group(NG - 1, 1, False)

        @block.scalar
        def _(act):
            act.wait_ge(s["mu"], 32)

            def front_turn(j, c):
                act.wait_ge(s["turn"], C * j + c + 1)
                if c == 0:
                    act.wait_ge(s["first"], j + 1)
                nc.scalar.activation(xT[:, c, 1:G + 1], pT[c % 2][:, :], ACT.Copy).then_inc(s["xT"], 1)
                act.wait_ge(s["xT"], C * j + c + 1)
                for z in range(2):
                    wait(act, s["mix"], 2 * (C * j + c) + z - 1)
                    nc.scalar.activation(part[:, z, :], xT[:, c, 1:G + 1], ACT.Copy, scale=mu[:, z, c:c + 1]).then_inc(s["part"], 1)

            def front_hi(j, side, c):
                for z in range(2):
                    act.wait_ge(s["mix"], 2 * (C * j + c) + z + 1)
                    nc.scalar.activation(zh[:, side, z, c, :], mix[:, z, :], ACT.Copy).then_inc(s["zhi"], 1)

            def group(i, side, more):
                for m in range(C):
                    act.wait_ge(s["K"], C * i + m + 1)
                    wait(act, s["hlo"], C * i + m - 1)
                    nc.scalar.activation(r[:, m % 2, :], pK[m % 2][:, :], ACT.Relu).then_inc(s["relued"], 1)
                    act.wait_ge(s["squared"], C * i + m + 1)
                    nc.scalar.activation(hh[:, m, :], r[:, m % 2, :], ACT.Copy).then_inc(s["hhi"], 1)
                for t in range(NT):
                    act.wait_ge(s["R"], NT * i + t + 1)
                    nc.scalar.activation(gate[:, t, :], pR[t % 2][:, :], ACT.Sigmoid).then_inc(s["gate"], 1)
                    if more:
                        if t:
                            front_hi(i + 1, 1 - side, t - 1)
                        front_turn(i + 1, t)
                if more:
                    front_hi(i + 1, 1 - side, C - 1)

            for c in range(C):
                front_turn(0, c)
                front_hi(0, 0, c)
            group(0, 0, True)
            with act.Fori(0, NG // 2 - 1) as k:
                group(k * 2 + 1, 1, True)
                group(k * 2 + 2, 0, True)
            group(NG - 1, 1, False)

        @block.vector
        def _(dve):
            dve.wait_ge(s["mu"], 32)
            nc.vector.tensor_scalar(nu[:, :, :], mu[:, :, :], -1.0, 1.0, ALU.mult, ALU.add).then_inc(s["nu"], 1)
            dve.wait_ge(s["nu"], 1)

            def front_x3(j, side, pair, t):
                dve.wait_ge(s_x2[side][t], 16 * (pair + 1))
                dve.wait_ge(s["exp"], NT * j + t + 1)
                nc.vector.tensor_tensor(x3[:, side, t, :], pE[t % 2][:, :], x3[:, side, t, :], ALU.add).then_inc(s["x3"], 1)

            def front_stats(j, side, t):
                dve.wait_ge(s["x3"], NT * j + t + 1)
                nc.vector.bn_stats(stats[:, t, :], x3[:, side, t, :]).then_inc(s["stat"], 1)

            def front_norm(j, side):
                dve.wait_ge(s["stat"], NT * j + NT)
                nc.vector.memset(pause[:, :], 0.0)
                for t in range(NT):
                    nc.vector.bn_aggr(mv[:, t, :], stats[:, t, :]).then_inc(s["aggr"], 1)
                dve.wait_ge(s["aggr"], NT * j + NT)
                nc.vector.tensor_scalar(ve[:, :], mv[:, :, 1], LN_EPS, None, ALU.add).then_inc(s["var"], 1)
                dve.wait_ge(s["rstd"], j + 1)
                for t in range(NT):
                    nc.vector.tensor_scalar(xn[:, t, :], x3[:, side, t, :], mv[:, t, 0:1], rstd[:, t:t + 1],
                                            ALU.subtract, ALU.mult).then_inc(s["xn"], 1)
                if isinstance(j, int) and j == 0:
                    nc.vector.memset(xT[:, :, 0:1], 0.0).then_inc(s["first"], 1)
                else:
                    nc.vector.tensor_scalar(xT[:, :, 0:1], xT[:, :, G:G + 1], inside[:, bass.ds(j, 1)], None, ALU.mult).then_inc(s["first"], 1)

            def front_mix(j, c):
                for z in range(2):
                    n = 2 * (C * j + c) + z
                    dve.wait_ge(s["part"], n + 1)
                    if c == 0:
                        dve.wait_ge(s["first"], j + 1)
                    wait(dve, s["zlo"], n - 1)
                    nc.vector.scalar_tensor_tensor(mix[:, z, :], xT[:, c, 0:G], nu[:, z, c:c + 1], part[:, z, :],
                                                   ALU.mult, ALU.add).then_inc(s["mix"], 1)

            def group(i, side, pair, more):
                for m in range(C):
                    if more and m < 2:
                        front_x3(i + 1, 1 - side, pair + side, 2 * m)
                    dve.wait_ge(s["relued"], C * i + m + 1)
                    nc.vector.scalar_tensor_tensor(r[:, m % 2, :], pK[m % 2][:, :], 0.0, r[:, m % 2, :], ALU.max, ALU.mult).then_inc(s["squared"], 1)
                    if more and m < 2:
                        front_x3(i + 1, 1 - side, pair + side, 2 * m + 1)
                        front_stats(i + 1, 1 - side, 2 * m)
                        front_stats(i + 1, 1 - side, 2 * m + 1)
                    if more and m == 2:
                        front_norm(i + 1, 1 - side)
                if more:
                    for c in range(C):
                        front_mix(i + 1, c)
                for t in range(NT):
                    dve.wait_ge(s["V"], NT * i + t + 1)
                    nc.vector.tensor_tensor(gate[:, t, :], pV[t][:, :], gate[:, t, :], ALU.mult).then_inc(s["gated"], 1)
                    dve.wait_ge(s["gated"], NT * i + t + 1)
                    wait(dve, s_store[t % 2], 16 * (NT // 2 * i + t // 2))
                    nc.vector.tensor_tensor(res[:, t % 2, :], gate[:, t, :], x3[:, side, t, :], ALU.add).then_inc(s["res"], 1)

            dve.wait_ge(s["ident"], 5)
            for t in range(NT):
                front_x3(0, 0, 0, t)
                front_stats(0, 0, t)
            front_norm(0, 0)
            for c in range(C):
                front_mix(0, c)
            group(0, 0, 0, True)
            with dve.Fori(0, NG // 2 - 1) as k:
                group(k * 2 + 1, 1, k, True)
                group(k * 2 + 2, 0, k + 1, True)
            group(NG - 1, 1, NG // 2 - 1, False)

        @block.tensor
        def _(pe):
            pe.wait_ge(s["ident"], 2)

            def three(out, xh, xl, yh, yl, first, last):
                nc.tensor.matmul(out, xh, yh, start=first, stop=False)
                nc.tensor.matmul(out, xh, yl, start=False, stop=False)
                return nc.tensor.matmul(out, xl, yh, start=False, stop=last)

            def expand(j, t):
                pe.wait_ge(s["path"], 16 * (j + 1))
                pe.wait_ge(s["ctx"], 32 * (j + 1))
                wait(pe, s["x3"], NT * j + t - 1)
                q = slice(t * P, (t + 1) * P)
                nc.tensor.matmul(pE[t % 2][:, :], path[:, q], ch[:, :], start=True, stop=False)
                nc.tensor.matmul(pE[t % 2][:, :], path[:, q], cl[:, :], start=False, stop=True).then_inc(s["exp"], 1)

            def front_turn(j, c):
                pe.wait_ge(s["xn"], NT * (j + 1))
                wait(pe, s["xT"], C * j + c - 1)
                for t in range(NT):
                    last = nc.tensor.transpose(pT[c % 2][:, t * P:(t + 1) * P], xn[:, t, c * P:(c + 1) * P], ident[:, :])
                last.then_inc(s["turn"], 1)

            def gates(i, side, t):
                if t < 2:
                    wait(pe, s["gated"], NT * i)
                else:
                    pe.wait_ge(s["gate"], NT * i + t - 1)
                q = slice(t * P, (t + 1) * P)
                for c in range(C):
                    last = three(pR[t % 2][:, :], zh[:, side, 0, c, q], zl[:, side, 0, c, q], w["r"][0][:, c, :], w["r"][1][:, c, :], c == 0, c == C - 1)
                last.then_inc(s["R"], 1)

            def keys(i, side, m):
                if m < 2:
                    wait(pe, s["gated"], NT * (i - 1) + m + 1)
                else:
                    pe.wait_ge(s["squared"], C * i + m - 1)
                e = slice(m * P, (m + 1) * P)
                for c in range(C):
                    last = three(pK[m % 2][:, :], w["k"][0][:, c, e], w["k"][1][:, c, e], zh[:, side, 1, c, :], zl[:, side, 1, c, :], c == 0, c == C - 1)
                last.then_inc(s["K"], 1)

            def values(i, t):
                if t >= 2:
                    pe.wait_ge(s["gate"], NT * i + t + 1)
                pe.wait_ge(s["hlo"], C * (i + 1))
                q = slice(t * P, (t + 1) * P)
                for m in range(C):
                    last = three(pV[t][:, :], hh[:, m, q], hl[:, m, q], w["v"][0][:, m, :], w["v"][1][:, m, :], m == 0, m == C - 1)
                last.then_inc(s["V"], 1)

            def group(i, side, more):
                pe.wait_ge(s["zlo"], 2 * C * (i + 1))
                for m in range(C):
                    keys(i, side, m)
                    if more and m < 2:
                        expand(i + 1, 2 * m)
                        expand(i + 1, 2 * m + 1)
                for t in range(NT):
                    gates(i, side, t)
                    if more and t < NT - 1:
                        front_turn(i + 1, t)
                for t in range(NT):
                    values(i, t)
                    if more and t == 0:
                        front_turn(i + 1, NT - 1)

            for t in range(NT):
                expand(0, t)
            for c in range(C):
                front_turn(0, c)
            group(0, 0, True)
            with pe.Fori(0, NG // 2 - 1) as k:
                group(k * 2 + 1, 1, True)
                group(k * 2 + 2, 0, True)
            group(NG - 1, 1, False)


INPUTS = {
    "x": ("x", lambda v: v.reshape(B * T, DM)),
    "ctx": ("ctx_1024", lambda v: v),
    "mask": ("mask_Bx1xSxS2_bf1", lambda v: v.reshape(B * T, S)[:, ::-1].view("uint8")),
    "WqT": ("L0_xattn_Wq", lambda v: v.T), "bq": ("L0_xattn_bq", lambda v: v.reshape(C, P).T),
    "WkT": ("L0_xattn_Wk", lambda v: v.T), "bk": ("L0_xattn_bk", lambda v: v.reshape(C, P).T),
    "WvT": ("L0_xattn_Wv", lambda v: v.T), "bv": ("L0_xattn_bv", lambda v: v),
    "WoT": ("L0_xattn_Wo", lambda v: v.T), "bo": ("L0_xattn_bo", lambda v: v),
    "rel": ("L0_xattn_rel_emb", lambda v: v.T),
    "WfcT": ("L0_ffn_W_fc", lambda v: v.T), "WprojT": ("L0_ffn_W_proj", lambda v: v.T),
    "WrT": ("L1_ffn_W_r", lambda v: v.T), "WkkT": ("L1_ffn_W_k", lambda v: v.T), "WvvT": ("L1_ffn_W_v", lambda v: v.T),
    "mu_r": ("L1_ffn_mu_r", lambda v: v.reshape(C, P).T), "mu_k": ("L1_ffn_mu_k", lambda v: v.reshape(C, P).T),
}


def kernel(**inputs):
    import numpy as np
    import concourse.bacc as bacc
    from concourse.bass_utils import run_bass_kernel_spmd

    nc = bacc.Bacc("TRN2", target_bir_lowering=False, num_devices=1)
    arrays, a = {}, {}
    for name, (source, lay_out) in INPUTS.items():
        v = np.ascontiguousarray(lay_out(np.asarray(inputs[source])))
        arrays[f"in_{name}"] = v
        a[name] = nc.dram_tensor(f"in_{name}", v.shape, mybir.dt.from_np(v.dtype), kind="ExternalInput").ap()

    def scratch(name, shape, dt=F32):
        return nc.dram_tensor(f"s_{name}", shape, dt, kind="Internal").ap()

    d = {
        "kh": scratch("kh", (B, P, C, S)), "kl": scratch("kl", (B, P, C, S)),
        "c2h": scratch("c2h", (B, P, C, S)), "c2l": scratch("c2l", (B, P, C, S)),
        "vh": scratch("vh", (B, S, DM)), "vl": scratch("vl", (B, S, DM)),
        "ch": scratch("ch", (B, S, DM)), "cl": scratch("cl", (B, S, DM)),
        "aa": scratch("aa", (B, S, 1)), "rel": scratch("rel", (H, RELW)),
        "dist": scratch("dist", (B, NB, SLOTS * W)), "on": scratch("on", (B, NB, SLOTS * W)),
        "x1": scratch("x1", (B * T, DM)), "x2": scratch("x2", (B * T, DM)),
    }
    out = nc.dram_tensor("out", (B * T, DM), F32, kind="ExternalOutput").ap()
    with ExitStack() as ctx:
        w = {k: [ctx.enter_context(nc.sbuf_tensor(f"w_{k}{n}", [P, C, DM], F32R)) for n in "hl"] for k in "qo"}
        prepare(nc, a, d, w)
        attention(nc, a, d, w)
    spiking(nc, a, d)
    with ExitStack() as ctx:
        w = {k: [ctx.enter_context(nc.sbuf_tensor(f"w_{k}{n}", [P, C, DM], F32R)) for n in "hl"] for k in "rkv"}
        align(nc, a, d, w)
        mixing(nc, a, d, w, out)
    r = run_bass_kernel_spmd(nc, [arrays], core_ids=[0])
    return r.results[0]["out"].reshape(B, T, DM)
```
